# Optimizing a Trainium2 kernel written in Bass

```python
import numpy as np
import jax
import jax.numpy as jnp

def _softmax(x, axis=-1):
    return jax.nn.softmax(x, axis=axis)

def _gelu(x):
    return jax.nn.gelu(x, approximate=True)

def _silu(x):
    return jax.nn.silu(x)

def _sigmoid(x):
    return jax.nn.sigmoid(x)

def _layernorm(x, axis=-1, eps=1e-05):
    m = jnp.mean(x, axis=axis, keepdims=True)
    v = jnp.var(x, axis=axis, keepdims=True)
    return (x - m) / jnp.sqrt(v + eps)

def _scatter_add(tgt, idx, src, axis=0):
    return tgt.at[idx].add(src)

def _segment_sum(src, seg, n):
    return jax.ops.segment_sum(src, seg, n)
kernel_name = 'mk_gps_d1_gnn_r8_832625'

def setup_inputs(seed: int=0):
    np.random.seed(seed)
    _w = jnp.asarray

    def _rec_inputs():
        import jax
        import jax.numpy as jnp
        _gk = jax.random.key(seed)
        x = -0.0003713 + 1 * jax.random.normal(jax.random.fold_in(_gk, 1), (6250, 256), jnp.float32)
        src = jax.random.randint(jax.random.fold_in(_gk, 2), (100000,), 0, 6250, jnp.int32)
        dst = jnp.minimum((6250 * jax.random.uniform(jax.random.fold_in(_gk, 3), (100000,)) ** 2.0).astype(jnp.int32), 49999)
        _o = jnp.argsort(dst, stable=True)
        src = src[_o]
        dst = dst[_o]
        edge_type_64 = jax.random.randint(jax.random.fold_in(_gk, 12), (100000,), 0, 64, jnp.int32)
        return (x, src, dst, edge_type_64)
    x, src, dst, edge_type_64 = _rec_inputs()

    def _L0_gnn_setup():
        import jax, jax.numpy as jnp
        import numpy as np
        N_NODES = 6250
        N_EDGES = 62500
        IN_DIM = 256
        HID = 64
        HEADS = 4
        N_REL = 64
        key = jax.random.key(seed)
        ks = jax.random.split(key, 16)
        s = 0.02
        return {'node_features': jax.random.normal(ks[0], (N_NODES, IN_DIM), jnp.float32), 'edge_index': jax.random.randint(ks[1], (2, N_EDGES), 0, N_NODES, jnp.int32), 'edge_relations': jax.random.randint(ks[2], (N_EDGES,), 0, N_REL, jnp.int32), 'query_emb': jax.random.normal(ks[3], (IN_DIM,), jnp.float32), 'Wq': jax.random.normal(ks[4], (IN_DIM, HID * HEADS), jnp.float32) * s, 'bq': jnp.zeros((HID * HEADS,), jnp.float32), 'Wk': jax.random.normal(ks[5], (IN_DIM, HID * HEADS), jnp.float32) * s, 'bk': jnp.zeros((HID * HEADS,), jnp.float32), 'Wv': jax.random.normal(ks[6], (IN_DIM, HID * HEADS), jnp.float32) * s, 'bv': jnp.zeros((HID * HEADS,), jnp.float32), 'rel_w': jax.random.normal(ks[7], (N_REL, HID), jnp.float32) * s, 'Wo': jax.random.normal(ks[8], (HID * HEADS, IN_DIM), jnp.float32) * s, 'bo': jnp.zeros((IN_DIM,), jnp.float32), 'gamma': jnp.ones((IN_DIM,), jnp.float32), 'beta': jnp.zeros((IN_DIM,), jnp.float32)}
    _L0_gnn_all = _L0_gnn_setup()
    _L0_gnn_in = {k: v for k, v in _L0_gnn_all.items() if k in ('query_emb', 'Wq', 'bq', 'Wk', 'bk', 'Wv', 'bv', 'rel_w', 'Wo', 'bo', 'gamma', 'beta')}
    del _L0_gnn_all

    def _L0_mix_setup():
        import jax, jax.numpy as jnp
        import numpy as np
        HEADS = 8
        DIM_HEAD = 64
        EPS = 1e-05

        def _inst_norm_lastdim(t):
            mu = jnp.mean(t, axis=-1, keepdims=True)
            var = jnp.mean(jnp.square(t - mu), axis=-1, keepdims=True)
            return (t - mu) * jax.lax.rsqrt(var + EPS)
        key = jax.random.key(seed)
        k1, k2, k3, k4 = jax.random.split(key, 4)
        b, n, dim = (4, 1024, 256)
        inner = HEADS * DIM_HEAD
        x = jax.random.normal(k1, (b, n, dim), dtype=jnp.float32)
        Wqkv = jax.random.normal(k2, (3 * inner, dim), dtype=jnp.float32) * (1.0 / np.sqrt(dim))
        Wout = jax.random.normal(k3, (dim, inner), dtype=jnp.float32) * (1.0 / np.sqrt(inner))
        bout = jax.random.normal(k4, (dim,), dtype=jnp.float32) * 0.01
        return {'x': x, 'Wqkv': Wqkv, 'Wout': Wout, 'bout': bout}
    _L0_mix_all = _L0_mix_setup()
    _L0_mix_in = {k: v for k, v in _L0_mix_all.items() if k in ('Wqkv', 'Wout', 'bout')}
    del _L0_mix_all

    def _L0_ffn_setup():
        import jax, jax.numpy as jnp
        import numpy as np
        C = 256
        HID = 1024
        E = 8
        TEMP = 1.0
        key = jax.random.key(seed)
        ks = jax.random.split(key, 7)
        x = jax.random.normal(ks[0], (8, 2048, C), dtype=jnp.float32)
        W1 = jax.random.normal(ks[1], (C, HID), dtype=jnp.float32) * 0.02
        b1 = jnp.zeros((HID,), dtype=jnp.float32)
        Wg = jax.random.normal(ks[2], (HID, E), dtype=jnp.float32) * 0.02
        bg = jnp.zeros((E,), dtype=jnp.float32)
        Wd = jax.random.normal(ks[3], (E, HID, C), dtype=jnp.float32) * 0.02
        bd = jnp.zeros((E, C), dtype=jnp.float32)
        return {'x': x, 'W1': W1, 'b1': b1, 'Wg': Wg, 'bg': bg, 'Wd': Wd, 'bd': bd}
    _L0_ffn_all = _L0_ffn_setup()
    _L0_ffn_in = {k: v for k, v in _L0_ffn_all.items() if k in ('W1', 'b1', 'Wg', 'bg', 'Wd', 'bd')}
    del _L0_ffn_all
    return {'x': x, 'src': src, 'dst': dst, 'edge_type_64': edge_type_64, 'L0_gnn_query_emb': _L0_gnn_in['query_emb'], 'L0_gnn_Wq': _L0_gnn_in['Wq'], 'L0_gnn_bq': _L0_gnn_in['bq'], 'L0_gnn_Wk': _L0_gnn_in['Wk'], 'L0_gnn_bk': _L0_gnn_in['bk'], 'L0_gnn_Wv': _L0_gnn_in['Wv'], 'L0_gnn_bv': _L0_gnn_in['bv'], 'L0_gnn_rel_w': _L0_gnn_in['rel_w'], 'L0_gnn_Wo': _L0_gnn_in['Wo'], 'L0_gnn_bo': _L0_gnn_in['bo'], 'L0_gnn_gamma': _L0_gnn_in['gamma'], 'L0_gnn_beta': _L0_gnn_in['beta'], 'L0_mix_Wqkv': _L0_mix_in['Wqkv'], 'L0_mix_Wout': _L0_mix_in['Wout'], 'L0_mix_bout': _L0_mix_in['bout'], 'L0_ffn_W1': _L0_ffn_in['W1'], 'L0_ffn_b1': _L0_ffn_in['b1'], 'L0_ffn_Wg': _L0_ffn_in['Wg'], 'L0_ffn_bg': _L0_ffn_in['bg'], 'L0_ffn_Wd': _L0_ffn_in['Wd'], 'L0_ffn_bd': _L0_ffn_in['bd']}

def reference(x, src, dst, edge_type_64, L0_gnn_query_emb, L0_gnn_Wq, L0_gnn_bq, L0_gnn_Wk, L0_gnn_bk, L0_gnn_Wv, L0_gnn_bv, L0_gnn_rel_w, L0_gnn_Wo, L0_gnn_bo, L0_gnn_gamma, L0_gnn_beta, L0_mix_Wqkv, L0_mix_Wout, L0_mix_bout, L0_ffn_W1, L0_ffn_b1, L0_ffn_Wg, L0_ffn_bg, L0_ffn_Wd, L0_ffn_bd):
    import jax
    import jax.numpy as jnp

    def _L0_gnn_ref(node_features, edge_index, edge_relations, query_emb, Wq, bq, Wk, bk, Wv, bv, rel_w, Wo, bo, gamma, beta):
        import jax, jax.numpy as jnp
        import numpy as np
        N_NODES = 6250
        N_EDGES = 62500
        IN_DIM = 256
        HID = 64
        HEADS = 4
        N_REL = 64
        N = node_features.shape[0]
        D = rel_w.shape[1]
        H = Wq.shape[1] // D
        enh = node_features + 0.1 * query_emb[None, :]
        Q = (enh @ Wq + bq).reshape(N, H, D)
        K = (enh @ Wk + bk).reshape(N, H, D)
        V = (enh @ Wv + bv).reshape(N, H, D)
        src, dst = (edge_index[0], edge_index[1])
        rel = rel_w[edge_relations]
        mod_k = K[src] + 0.2 * rel[:, None, :]
        scores = jnp.einsum('ehd,ehd->eh', Q[dst], mod_k) / D ** 0.5
        seg_max = jax.ops.segment_max(scores, dst, num_segments=N)
        ex = jnp.exp(scores - seg_max[dst])
        denom = jax.ops.segment_sum(ex, dst, num_segments=N)
        w = ex / denom[dst]
        agg = jax.ops.segment_sum(w[:, :, None] * V[src], dst, num_segments=N)
        deg = jax.ops.segment_sum(jnp.ones((src.shape[0],), jnp.float32), dst, num_segments=N)
        msgs = jnp.where(deg[:, None, None] > 0, agg, V)
        out = msgs.reshape(N, H * D) @ Wo + bo
        x = out + node_features
        mu = jnp.mean(x, axis=-1, keepdims=True)
        var = jnp.var(x, axis=-1, keepdims=True)
        return (x - mu) / jnp.sqrt(var + 1e-05) * gamma + beta

    def _L0_mix_ref(x, Wqkv, Wout, bout):
        import jax, jax.numpy as jnp
        import numpy as np
        HEADS = 8
        DIM_HEAD = 64
        EPS = 1e-05

        def _inst_norm_lastdim(t):
            mu = jnp.mean(t, axis=-1, keepdims=True)
            var = jnp.mean(jnp.square(t - mu), axis=-1, keepdims=True)
            return (t - mu) * jax.lax.rsqrt(var + EPS)
        b, n, dim = x.shape
        qkv = jnp.einsum('bnc,fc->bnf', x, Wqkv)
        q, k, v = jnp.split(qkv, 3, axis=-1)

        def to_heads(t):
            return t.reshape(b, n, HEADS, DIM_HEAD).transpose(0, 2, 1, 3)
        q, k, v = (to_heads(q), to_heads(k), to_heads(v))
        k = _inst_norm_lastdim(k)
        v = _inst_norm_lastdim(v)
        dots = jnp.einsum('bhnd,bhne->bhde', k, v)
        out = jnp.einsum('bhnd,bhde->bhne', q, dots) / n
        out = out.transpose(0, 2, 1, 3).reshape(b, n, HEADS * DIM_HEAD)
        return jnp.einsum('bnf,cf->bnc', out, Wout) + bout

    def _L0_ffn_ref(x, W1, b1, Wg, bg, Wd, bd):
        import jax, jax.numpy as jnp
        import numpy as np
        C = 256
        HID = 1024
        E = 8
        TEMP = 1.0
        orig_shape = x.shape
        xf = x.reshape(-1, orig_shape[-1])
        H = jax.nn.gelu(xf @ W1 + b1, approximate=False)
        probs = jax.nn.softmax((H @ Wg + bg) / TEMP, axis=-1)
        assign = jnp.argmax(probs, axis=-1)
        out = jnp.zeros_like(xf)
        for e in range(Wd.shape[0]):
            y = H @ Wd[e] + bd[e]
            sel = (assign == e)[:, None]
            out = out + jnp.where(sel, probs[:, e:e + 1] * y, 0.0)
        return out.reshape(orig_shape)
    edge_index = jnp.stack([src, dst])
    xn = _layernorm(x, axis=-1)
    x = x + _L0_gnn_ref(xn, edge_index, edge_type_64, L0_gnn_query_emb, L0_gnn_Wq, L0_gnn_bq, L0_gnn_Wk, L0_gnn_bk, L0_gnn_Wv, L0_gnn_bv, L0_gnn_rel_w, L0_gnn_Wo, L0_gnn_bo, L0_gnn_gamma, L0_gnn_beta) + _L0_mix_ref(xn[None], L0_mix_Wqkv, L0_mix_Wout, L0_mix_bout)[0]
    x = x + _L0_ffn_ref(_layernorm(x, axis=-1)[None], L0_ffn_W1, L0_ffn_b1, L0_ffn_Wg, L0_ffn_bg, L0_ffn_Wd, L0_ffn_bd)[0]
    return x

_drawn_inputs = setup_inputs


def setup_inputs(seed=0):
    import zlib

    import numpy as np

    out = dict(_drawn_inputs(seed))
    spreads = {'L0_gnn_bq': (0.0, 0.8),
     'L0_gnn_bk': (0.0, 0.8),
     'L0_gnn_bv': (0.0, 0.517),
     'L0_gnn_bo': (0.0, 0.1),
     'L0_gnn_gamma': (1.0, 0.2),
     'L0_gnn_beta': (0.0, 0.1),
     'L0_ffn_b1': (0.0, 0.8),
     'L0_ffn_bg': (0.0, 0.8),
     'L0_ffn_bd': (0.0, 0.8)}
    factors = {'L0_gnn_query_emb': 8.0,
     'L0_gnn_Wq': 8.0,
     'L0_gnn_Wk': 8.0,
     'L0_gnn_Wv': 3.573,
     'L0_gnn_rel_w': 8.0,
     'L0_mix_bout': 8.0,
     'L0_ffn_W1': 5.447,
     'L0_ffn_Wg': 5.851,
     'L0_ffn_Wd': 6.668}
    for name, (base, spread) in spreads.items():
        noise = np.random.default_rng([zlib.crc32(name.encode()), seed]).standard_normal(out[name].shape)
        drawn = base * np.exp(spread * noise) if base else spread * noise
        out[name] = jnp.asarray(drawn.astype(out[name].dtype))
    for name, factor in factors.items():
        out[name] = (out[name] * factor).astype(out[name].dtype)
    return out
```

```python
from contextlib import ExitStack

import numpy as np
import concourse.bass as bass
from concourse import mybir

F32 = mybir.dt.float32
BF16 = mybir.dt.bfloat16
I32 = mybir.dt.int32
ALU = mybir.AluOpType
ACT = mybir.ActivationFunctionType
AX_X = mybir.AxisListType.X

P = 128
C = 256
KC = C // P
N = 6250
E = 100000
QUAD = 4
NBLK = 52
NPAD = NBLK * P
XBLK = NBLK + 2
RBLK = 49
H, D = 4, 64
NREL = 64
MH, MD = 8, 64
MI = MH * MD
HID = 1024
HC = HID // P
NEXP = 8
EPS = 1e-5
WCAT = 3 * C + 2 * MI
TS_ROWS = 104
TS_COLS = 8
T = TS_ROWS * TS_COLS
EROWS, ECOLS = 125, 800
BIG = 1.0e38


class Steps:

    def __init__(self, eng, sem, base=0):
        self.eng, self.sem, self.base, self.n = eng, sem, base, 0

    def mark(self, ins):
        ins.then_inc(self.sem, 1)
        self.n += 1

    def settle(self):
        self.eng.wait_ge(self.sem, self.base + self.n)


def rows(ap, k):
    return ap.rearrange("(k p) f -> p k f", k=k)


def stage_weights(nc, A, M, R):
    with ExitStack() as ctx:
        sb = lambda name, shape, dt=F32: ctx.enter_context(nc.sbuf_tensor(name, shape, dt))
        sem = lambda name: ctx.enter_context(nc.semaphore(name))
        query = sb("query", [P, KC])
        query_all = sb("query_all", [P, KC, P])
        mean = sb("wmean", [P, KC, 2 * MH])
        bias_in = sb("bias_in", [P, 3 * C])
        rel_in = sb("rel_in", [P, D])
        rel_s = sb("rel_s", [P, D])
        rel_1 = sb("rel_p1", [P, D], BF16)
        rel_2 = sb("rel_p2", [P, D], BF16)
        rel_3 = sb("rel_p3", [P, D], BF16)
        rel_r1 = sb("rel_r1", [P, D])
        rel_r2 = sb("rel_r2", [P, D])
        bias_ps = ctx.enter_context(nc.psum_tensor("bias_ps", [P, 2, 512], F32))
        loaded, ones_set, ident_set = sem("w_loaded"), sem("w_ones"), sem("w_ident")
        query_set, bias_done, v_step = sem("w_query"), sem("w_bias"), sem("w_vstep")
        wcat, bias = M["wcat"], M["bias"]
        block = ctx.enter_context(nc.Block())
        n_loads = 9

        @block.sync
        def _(sp):
            for j, name in enumerate(("L0_gnn_Wq", "L0_gnn_Wk", "L0_gnn_Wv")):
                sp.dma_start(wcat[:, :, j * C:(j + 1) * C], rows(A[name], KC)).then_inc(loaded, 16)
            sp.dma_start(wcat[:, :, 3 * C:], rows(A["mix_WkvT"], KC)).then_inc(loaded, 16)
            for j, name in enumerate(("L0_gnn_bq", "L0_gnn_bk", "L0_gnn_bv")):
                sp.dma_start(bias_in[:, j * C:(j + 1) * C],
                             A[name].rearrange("(a n) -> a n", a=1).broadcast_to([P, C])).then_inc(loaded, 16)
            for half in range(2):
                sp.dma_start(rel_in[half * 64:half * 64 + 64, :], A["L0_gnn_rel_w"]).then_inc(loaded, 16)

        @block.scalar
        def _(act):
            act.dma_start(query[:], A["L0_gnn_query_emb"].rearrange("(k p) -> p k", k=KC),
                          allow_slow_non_contiguous=True).then_inc(query_set, 16)
            act.wait_ge(query_set, 16)

        @block.gpsimd
        def _(pool):
            nc.gpsimd.memset(M["ones"][:], 1.0).then_inc(ones_set, 1)
            nc.gpsimd.memset(M["eps"][:], EPS).then_inc(ones_set, 1)
            nc.gpsimd.memset(M["ident"][:], 0.0).then_inc(ident_set, 1)
            pool.wait_ge(ident_set, 1)
            nc.gpsimd.affine_select(out=M["ident"][:], in_=M["ident"][:], compare_op=ALU.not_equal, fill=1.0,
                                    base=0, pattern=[[-1, P]], channel_multiplier=1).then_inc(ident_set, 1)
            nc.gpsimd.iota(M["lane"][:], pattern=[[0, 1]], base=0, channel_multiplier=1,
                           allow_small_or_imprecise_dtypes=True).then_inc(ident_set, 1)
            nc.gpsimd.iota(M["col"][:], pattern=[[1, P]], base=0, channel_multiplier=0,
                           allow_small_or_imprecise_dtypes=True).then_inc(ident_set, 1)
            pool.wait_ge(ident_set, 4)

        @block.vector
        def _(dve):
            st = Steps(dve, v_step)
            dve.wait_ge(ident_set, 4)
            st.mark(nc.vector.tensor_scalar(M["lane64"][:], M["lane"][:], 64.0, -64.0, ALU.is_ge, ALU.mult))
            st.settle()
            st.mark(nc.vector.tensor_tensor(M["lane64"][:], M["lane64"][:], M["lane"][:], ALU.add))
            dve.wait_ge(ones_set, 2)
            dve.wait_ge(query_set, 16)
            for k in range(KC):
                last = nc.vector.tensor_scalar(query_all[:, k, :], M["ones"][:], query[:, k:k + 1], 0.1,
                                               ALU.mult, ALU.mult)
                st.mark(last)
            st.settle()
            dve.wait_ge(loaded, 16 * n_loads)
            heads = wcat[:, :, 3 * C:].rearrange("p k (h d) -> p k h d", d=MD)
            st.mark(nc.vector.tensor_reduce(mean[:], heads, AX_X, ALU.add))
            st.settle()
            st.mark(nc.vector.tensor_scalar(mean[:], mean[:], 1.0 / MD, None, ALU.mult))
            st.settle()
            for k in range(KC):
                st.mark(nc.vector.tensor_tensor(heads[:, k], heads[:, k],
                                                mean[:, k, :, None].broadcast_to([P, 2 * MH, MD]), ALU.subtract))
            st.mark(nc.vector.tensor_scalar(rel_s[:], rel_in[:], 0.2, None, ALU.mult))
            st.settle()
            st.mark(nc.vector.tensor_copy(rel_1[:], rel_s[:]))
            st.settle()
            st.mark(nc.vector.tensor_tensor(rel_r1[:], rel_s[:], rel_1[:], ALU.subtract))
            st.settle()
            st.mark(nc.vector.tensor_copy(rel_2[:], rel_r1[:]))
            st.settle()
            st.mark(nc.vector.tensor_tensor(rel_r2[:], rel_r1[:], rel_2[:], ALU.subtract))
            st.settle()
            st.mark(nc.vector.tensor_copy(rel_3[:], rel_r2[:]))
            st.settle()
            over = lambda x, a, b: x[a:b, None, :].broadcast_to([b - a, H, D])
            by_head = lambda x, a, b: x[a:b, :].rearrange("p (h d) -> p h d", h=H)
            st.mark(nc.vector.tensor_copy(by_head(M["rel_12"], 0, 64), over(rel_1, 0, 64)))
            st.mark(nc.vector.tensor_copy(by_head(M["rel_12"], 64, 128), over(rel_2, 64, 128)))
            st.mark(nc.vector.tensor_copy(by_head(M["rel_3"], 0, 64), over(rel_3, 0, 64)))
            dve.wait_ge(bias_done, 2)
            st.mark(nc.vector.tensor_tensor(bias[:, 0:512], bias_in[:, 0:512], bias_ps[:, 0, :], ALU.add))
            st.mark(nc.vector.tensor_tensor(bias[:, 512:768], bias_in[:, 512:768], bias_ps[:, 1, 0:256], ALU.add))
            st.settle()
            st.mark(nc.vector.tensor_scalar(bias[:, 0:C], bias[:, 0:C], D ** -0.5, None, ALU.mult))
            st.settle()

        @block.tensor
        def _(pe):
            pe.wait_ge(loaded, 16 * n_loads)
            pe.wait_ge(v_step, 4)
            for b, (lo, n) in enumerate(((0, 512), (512, 256))):
                for k in range(KC):
                    last = nc.tensor.matmul(bias_ps[:, b, 0:n], query_all[:, k, :], wcat[:, k, lo:lo + n],
                                            start=(k == 0), stop=(k == KC - 1))
                last.then_inc(bias_done, 1)


def stage_project(nc, A, M, R):
    with ExitStack() as ctx:
        sb = lambda name, shape, dt=F32: ctx.enter_context(nc.sbuf_tensor(name, shape, dt))
        ps = lambda name, shape: ctx.enter_context(nc.psum_tensor(name, shape, F32))
        sem = lambda name: ctx.enter_context(nc.semaphore(name))
        x = sb("px", [P, 2, C])
        xn = sb("pxn", [P, 2, C])
        xnt = sb("pxnt", [P, 2, KC, P])
        stats = sb("pstats", [P, 6])
        mv = sb("pmv", [P, 2])
        std = sb("pstd", [P, 1])
        rstd = sb("prstd", [P, 1])
        vkv = sb("pvkv", [P, MH])
        skv = sb("pskv", [P, MH])
        qf = sb("pqf", [P, 2, C])
        qr = sb("pqr", [P, C])
        kv = sb("pkv", [P, 2, 2 * C])
        sq = sb("psq", [P, 2 * MI])
        ss = sb("pss", [P, 2 * MH])
        rr = sb("prr", [P, 2 * MH])
        rkv = sb("prkv", [P, MH])
        mks = sb("pmks", [P, 2, MI])
        mvs = sb("pmvs", [P, 2, MI])
        zero = sb("pzero", [P, MI])
        t_ps = ps("pt_ps", [P, KC, P])
        qk_ps = ps("pqk_ps", [P, 512])
        v_ps = ps("pv_ps", [P, C])
        mk_ps = ps("pmk_ps", [P, MI])
        mv_ps = ps("pmv_ps", [P, MI])
        dots_ps = ps("pdots_ps", [P, MH // 2, P])
        x_in = [sem(f"x_in{u}") for u in range(2)]
        xn_out = [sem(f"xn_out{u}") for u in range(2)]
        xnt_out = [sem(f"xnt_out{u}") for u in range(2)]
        kv_out = [sem(f"kv_out{u}") for u in range(2)]
        names = ("zeroed xn_ready xnt_ready turned qk_done v_done mk_done mv_done qf_used k_read kv_ready "
                 "mks_ready mvs_ready sq_ready sq_used dots_done v_step p_step qf_ready dots_read "
                 "mv_ready std_ready rstd_ready vkv_ready skv_ready")
        S = {n: sem("p_" + n) for n in names.split()}
        wcat, bias, q3 = M["wcat"], M["bias"], M["q3"]
        x_d = A["x"].rearrange("(b p) c -> b p c", p=P)
        xn_d = R["xn"].rearrange("(b p) c -> b p c", p=P)
        kv_d = R["kv"].rearrange("(b p) c -> b p c", p=P)
        block = ctx.enter_context(nc.Block())
        TURNS = NBLK // 2

        @block.sync
        def _(sp):
            for u in range(2):
                sp.dma_start(x[:, u, :], x_d[u]).then_inc(x_in[u], 16)
            with sp.Fori(0, TURNS) as i:
                for u in range(2):
                    g = i * 2 + u
                    sp.wait_ge(S["xn_ready"], g + 1)
                    sp.nop(nofuse=True)
                    sp.dma_start(x[:, u, :], x_d[bass.ds(g + 2, 1)].rearrange("a p c -> (a p) c")).then_inc(x_in[u], 16)
                    sp.dma_start(xn_d[bass.ds(g, 1)].rearrange("a p c -> (a p) c"), xn[:, u, :]).then_inc(xn_out[u], 16)
                    sp.wait_ge(S["xnt_ready"], g + 1)
                    sp.nop(nofuse=True)
                    sp.dma_start(R["xnt"][bass.ds(g, 1)].rearrange("a p c -> (a p) c"),
                                 xnt[:, u].rearrange("p k n -> p (k n)")).then_inc(xnt_out[u], 16)
                    sp.wait_ge(S["kv_ready"], g + 1)
                    sp.nop(nofuse=True)
                    sp.dma_start(kv_d[bass.ds(g, 1)].rearrange("a p c -> (a p) c"), kv[:, u, :]).then_inc(kv_out[u], 16)
            for u in range(2):
                sp.wait_ge(xn_out[u], 16 * TURNS)
                sp.wait_ge(xnt_out[u], 16 * TURNS)
                sp.wait_ge(kv_out[u], 16 * TURNS)
                sp.wait_ge(x_in[u], 16 * (TURNS + 1))

        @block.vector
        def _(dve):
            nc.vector.memset(zero[:], 0.0).then_inc(S["zeroed"], 1)
            nc.vector.memset(mks[:, 1, :], 0.0).then_inc(S["zeroed"], 1)
            nc.vector.memset(mvs[:, 1, :], 0.0).then_inc(S["zeroed"], 1)

            def normalise(st, w, n):
                dve.wait_ge(S["xn_ready"], n)
                st.mark(nc.vector.bn_stats(stats[:], x[:, w, :]))
                st.settle()
                dve.nop(nofuse=True)
                nc.vector.bn_aggr(mv[:], stats[:]).then_inc(S["mv_ready"], 1)
                dve.wait_ge(S["std_ready"], n + 1)
                nc.vector.reciprocal(rstd[:], std[:]).then_inc(S["rstd_ready"], 1)
                dve.wait_ge(S["rstd_ready"], n + 1)
                nc.vector.tensor_scalar(xn[:, w, :], x[:, w, :], mv[:, 0:1], rstd[:], ALU.subtract,
                                        ALU.mult).then_inc(S["xn_ready"], 1)

            first = Steps(dve, S["v_step"])
            for w in range(2):
                dve.wait_ge(x_in[w], 16)
                normalise(first, w, w)
            PER = 3
            squares = lambda t, k: t[:, k * MH:(k + 1) * MH]
            with dve.Fori(0, TURNS) as i:
                for u in range(2):
                    g = i * 2 + u
                    st = Steps(dve, S["v_step"], g * PER + first.n)
                    dve.wait_ge(S["qk_done"], g + 1)
                    dve.wait_ge(S["qf_used"], g + 1)
                    nc.vector.scalar_tensor_tensor(out=qf[:, u, :], in0=qk_ps[:, 0:C], scalar=D ** -0.5,
                                                   in1=bias[:, 0:C], op0=ALU.mult, op1=ALU.add
                                                   ).then_inc(S["qf_ready"], 1)
                    dve.wait_ge(kv_out[u], i * 16)
                    nc.vector.tensor_tensor(kv[:, u, 0:C], qk_ps[:, C:2 * C], bias[:, C:2 * C],
                                            ALU.add).then_inc(S["k_read"], 1)
                    dve.wait_ge(S["v_done"], g + 1)
                    dve.wait_ge(S["k_read"], g + 1)
                    nc.vector.tensor_tensor(kv[:, u, C:], v_ps[:], bias[:, 2 * C:], ALU.add).then_inc(S["kv_ready"], 1)
                    dve.wait_ge(x_in[u], (i + 2) * 16)
                    dve.wait_ge(S["turned"], g + 1)
                    dve.wait_ge(xn_out[u], (i + 1) * 16)
                    normalise(st, u, g + 2)
                    for k in range(2):
                        dve.wait_ge(S["sq_ready"], g * 2 + k + 1)
                        ins = nc.vector.tensor_reduce(squares(ss, k), sq[:, k * MI:(k + 1) * MI]
                                                      .rearrange("p (h d) -> p h d", d=MD), AX_X, ALU.add)
                    st.mark(ins)
                    st.settle()
                    nc.vector.tensor_scalar(rr[:], ss[:], 1.0 / MD, EPS, ALU.mult, ALU.add).then_inc(S["sq_used"], 1)
                    dve.wait_ge(S["sq_used"], g + 1)
                    nc.vector.tensor_tensor(vkv[:], rr[:, 0:MH], rr[:, MH:], ALU.mult).then_inc(S["vkv_ready"], 1)
                    dve.wait_ge(S["skv_ready"], g + 1)
                    st.mark(nc.vector.reciprocal(rkv[:], skv[:]))
                    st.settle()
                    dve.wait_ge(S["dots_done"], g)
                    nc.vector.tensor_tensor(mks[:, u, :].rearrange("p (h d) -> p h d", d=MD),
                                            mk_ps[:].rearrange("p (h d) -> p h d", d=MD),
                                            rkv[:, :, None].broadcast_to([P, MH, MD]), ALU.mult
                                            ).then_inc(S["mks_ready"], 1)
                    assert st.n == PER
            dve.wait_ge(S["dots_done"], NBLK + 1)
            nc.vector.tensor_copy(M["dots"][:], dots_ps[:]).then_inc(S["dots_read"], 1)
            dve.wait_ge(S["dots_read"], 1)

        @block.gpsimd
        def _(pool):
            nc.gpsimd.memset(qr[:], 0.0).then_inc(S["qf_used"], 2)
            pool.wait_ge(S["qf_used"], 2)
            PER = 3
            with pool.Fori(0, TURNS) as i:
                for u in range(2):
                    g = i * 2 + u
                    st = Steps(pool, S["p_step"], g * PER)
                    part = lambda j: q3[:, bass.ds(g, 1), j, :].rearrange("p a c -> p (a c)")
                    pool.wait_ge(S["qf_ready"], g + 1)
                    pool.nop(nofuse=True)
                    st.mark(nc.gpsimd.tensor_copy(part(0), qf[:, u, :]))
                    st.settle()
                    pool.nop(nofuse=True)
                    st.mark(nc.gpsimd.tensor_tensor(qr[:], qf[:, u, :], part(0), ALU.subtract))
                    st.settle()
                    pool.nop(nofuse=True)
                    st.mark(nc.gpsimd.tensor_copy(part(1), qr[:]))
                    st.settle()
                    pool.nop(nofuse=True)
                    nc.gpsimd.tensor_tensor(part(2), qr[:], part(1), ALU.subtract).then_inc(S["qf_used"], 1)
                    pool.wait_ge(S["qf_used"], g + 3)
                    assert st.n == PER

        @block.scalar
        def _(act):
            def deviation(n):
                act.wait_ge(S["mv_ready"], n + 1)
                act.wait_ge(S["rstd_ready"], n)
                nc.scalar.activation(std[:], mv[:, 1:2], ACT.Sqrt, bias=M["eps"][:]).then_inc(S["std_ready"], 1)

            def turned_copy(w):
                nc.scalar.copy(xnt[:, w].rearrange("p k n -> p (k n)"),
                               t_ps[:].rearrange("p k n -> p (k n)")).then_inc(S["xnt_ready"], 1)

            deviation(0)
            deviation(1)
            act.wait_ge(S["turned"], 1)
            turned_copy(0)
            with act.Fori(0, TURNS) as i:
                for u in range(2):
                    g = i * 2 + u
                    act.wait_ge(S["turned"], g + 2)
                    act.wait_ge(S["mv_done"], g)
                    act.wait_ge(xnt_out[1 - u], (i + u) * 16)
                    turned_copy(1 - u)
                    deviation(g + 2)
                    act.wait_ge(S["mk_done"], g + 1)
                    act.wait_ge(S["sq_used"], g)
                    nc.scalar.activation(sq[:, 0:MI], mk_ps[:], ACT.Square).then_inc(S["sq_ready"], 1)
                    act.wait_ge(S["mv_done"], g + 1)
                    nc.scalar.activation(sq[:, MI:], mv_ps[:], ACT.Square).then_inc(S["sq_ready"], 1)
                    act.wait_ge(S["dots_done"], g)
                    nc.scalar.copy(mvs[:, u, :], mv_ps[:]).then_inc(S["mvs_ready"], 1)
                    act.wait_ge(S["vkv_ready"], g + 1)
                    nc.scalar.activation(skv[:], vkv[:], ACT.Sqrt).then_inc(S["skv_ready"], 1)

        @block.tensor
        def _(pe):
            def dots(w, last=False):
                for j in range(MH // 2):
                    pair = slice(j * P, (j + 1) * P)
                    ins = nc.tensor.matmul(dots_ps[:, j, :], mvs[:, w, pair], mks[:, w, pair],
                                           start=False, stop=last, skip_group_check=True)
                ins.then_inc(S["dots_done"], 1)

            pe.wait_ge(S["zeroed"], 3)
            nc.tensor.matmul(dots_ps[:].rearrange("p j n -> p (j n)"), zero[:, 0:P], zero[:], start=True, stop=False,
                             skip_group_check=True)

            def turn(w, n):
                pe.wait_ge(S["xn_ready"], n + 1)
                pe.wait_ge(S["xnt_ready"], n)
                for k in range(KC):
                    ins = nc.tensor.transpose(t_ps[:, k, :], xn[:, w, k * P:(k + 1) * P], M["ident"][:])
                ins.then_inc(S["turned"], 1)

            def product(w, g, out, lo, n, free, done):
                pe.wait_ge(S[free], g)
                for k in range(KC):
                    ins = nc.tensor.matmul(out[:], xnt[:, w, k, :], wcat[:, k, lo:lo + n],
                                           start=(k == 0), stop=(k == KC - 1))
                ins.then_inc(S[done], 1)

            pe.wait_ge(S["xn_ready"], 1)
            for k in range(KC):
                ins = nc.tensor.transpose(t_ps[:, k, :], xn[:, 0, k * P:(k + 1) * P], M["ident"][:])
            ins.then_inc(S["turned"], 1)
            with pe.Fori(0, TURNS) as i:
                for u in range(2):
                    g = i * 2 + u
                    pe.wait_ge(S["xnt_ready"], g + 1)
                    product(u, g, qk_ps, 0, 512, "k_read", "qk_done")
                    product(u, g, v_ps, 512, 256, "kv_ready", "v_done")
                    turn(1 - u, g + 1)
                    pe.wait_ge(S["mks_ready"], g)
                    pe.wait_ge(S["mvs_ready"], g)
                    dots(1 - u)
                    product(u, g, mk_ps, 768, 512, "mks_ready", "mk_done")
                    product(u, g, mv_ps, 1280, 512, "mvs_ready", "mv_done")
            pe.wait_ge(S["mks_ready"], NBLK)
            pe.wait_ge(S["mvs_ready"], NBLK)
            dots(1, last=True)


def stage_tiles(nc, A, M, R):
    with ExitStack() as ctx:
        sb = lambda name, shape, dt=F32: ctx.enter_context(nc.sbuf_tensor(name, shape, dt))
        sem = lambda name: ctx.enter_context(nc.semaphore(name))
        dst_i = sb("t_dst_i", [EROWS, ECOLS], I32)
        dst = sb("t_dst", [EROWS, ECOLS])
        junk = sb("t_junk", [EROWS, ECOLS])
        count = sb("t_count", [EROWS, RBLK])
        first_edge = sb("t_first_edge", [P, RBLK + 1])
        room = sb("t_room", [P, RBLK])
        room_i = sb("t_room_i", [P, RBLK], I32)
        tiles = sb("t_tiles", [P, RBLK])
        first_tile = sb("t_first_tile", [P, RBLK + 1])
        offset = sb("t_offset", [P, RBLK])
        delta = sb("t_delta", [P, RBLK])
        number = sb("t_number", [TS_ROWS, TS_COLS])
        begun = sb("t_begun", [TS_ROWS, TS_COLS, RBLK])
        begun_off = sb("t_begun_off", [TS_ROWS, TS_COLS, RBLK])
        blk = sb("t_blk", [TS_ROWS, TS_COLS])
        base = sb("t_base", [TS_ROWS, TS_COLS])
        start = sb("t_start", [TS_ROWS, TS_COLS])
        blk_i = sb("t_blk_i", [TS_ROWS, TS_COLS], I32)
        start_i = sb("t_start_i", [TS_ROWS, TS_COLS], I32)
        meta = sb("t_meta", [TS_ROWS, TS_COLS, 3 * P], I32)
        src_f = sb("t_src_f", [TS_ROWS, TS_COLS, P])
        dst_f = sb("t_dst_f", [TS_ROWS, TS_COLS, P])
        local = sb("t_local", [TS_ROWS, TS_COLS, P])
        valid = sb("t_valid", [TS_ROWS, TS_COLS, P])
        low = sb("t_low", [TS_ROWS, TS_COLS, P])
        local_b = sb("t_local_b", [TS_ROWS, TS_COLS * P], BF16)
        type_b = sb("t_type_b", [TS_ROWS, TS_COLS * P], BF16)
        tail = sb("t_tail", [P, 3], I32)
        total_ps = ctx.enter_context(nc.psum_tensor("t_total_ps", [P, RBLK], F32))
        turn_ps = [ctx.enter_context(nc.psum_tensor(f"t_turn_ps{b}", [P, 4, P], F32)) for b in range(4)]
        names = "dst_in tail_set copied counted totals number_set placed gathered stored steps turned back table_in"
        S = {n: sem("t_" + n) for n in names.split()}
        block = ctx.enter_context(nc.Block())

        @block.sync
        def _(sp):
            sp.dma_start(dst_i[:], A["dst"].rearrange("(p k) -> p k", p=EROWS)).then_inc(S["dst_in"], 16)
            sp.dma_start(R["edges"][0:E, :].rearrange("(p k) c -> p (k c)", p=EROWS),
                         A["edges"].rearrange("(p k) c -> p (k c)", p=EROWS)).then_inc(S["copied"], 16)
            sp.wait_ge(S["tail_set"], 1)
            sp.dma_start(R["edges"][E:E + P, :], tail[:]).then_inc(S["copied"], 16)
            sp.wait_ge(S["placed"], 1)
            sp.dma_start(R["blk"].rearrange("(p k) -> p k", p=TS_ROWS), blk_i[:]).then_inc(S["stored"], 16)
            sp.wait_ge(S["stored"], 16)
            sp.dma_start(M["blk"][:], R["blk"].rearrange("(a n) -> a n", a=1)).then_inc(S["table_in"], 16)
            sp.wait_ge(S["back"], 1)
            sp.dma_start(R["local"][0:TS_ROWS, :], local_b[:]).then_inc(S["stored"], 16)
            sp.dma_start(R["type"][0:TS_ROWS, :], type_b[:]).then_inc(S["stored"], 16)
            sp.wait_ge(S["stored"], 48)
            sp.dma_start(R["local"][TS_ROWS:, :], local_b[0:2, :]).then_inc(S["stored"], 16)
            sp.dma_start(R["type"][TS_ROWS:, :], type_b[0:2, :]).then_inc(S["stored"], 16)
            sp.wait_ge(S["stored"], 80)
            sp.wait_ge(S["table_in"], 16)

        @block.gpsimd
        def _(pool):
            nc.gpsimd.memset(tail[:], -1).then_inc(S["tail_set"], 1)
            nc.gpsimd.iota(number[:], pattern=[[1, TS_COLS]], base=0, channel_multiplier=TS_COLS,
                           allow_small_or_imprecise_dtypes=True).then_inc(S["number_set"], 1)
            pool.wait_ge(S["copied"], 32)
            pool.wait_ge(S["placed"], 2)
            for j in range(TS_COLS):
                nc.gpsimd.indirect_dma_start(out=meta[:, j, :], out_offset=None, in_=R["edges"],
                                             in_offset=bass.IndirectOffsetOnAxis(ap=start_i[:, j:j + 1], axis=0)
                                             ).then_inc(S["gathered"], 16)

        @block.vector
        def _(dve):
            st = Steps(dve, S["steps"])

            def then(ins):
                st.mark(ins)
                st.settle()

            dve.wait_ge(S["dst_in"], 16)
            then(nc.vector.tensor_copy(dst[:], dst_i[:]))
            for b in range(RBLK):
                then(nc.vector.tensor_scalar(junk[:], dst[:], float(P * (b + 1)), 0.0, ALU.is_lt, ALU.add,
                                             accum_out=count[:, b:b + 1]))
            nc.vector.memset(first_edge[:, 0:1], 0.0).then_inc(S["counted"], 1)
            st.settle()
            nc.vector.memset(first_tile[:, 0:1], 0.0).then_inc(S["counted"], 1)
            dve.wait_ge(S["totals"], 1)
            then(nc.vector.tensor_copy(first_edge[:, 1:], total_ps[:]))
            then(nc.vector.tensor_tensor(room[:], first_edge[:, 1:], first_edge[:, 0:RBLK], ALU.subtract))
            then(nc.vector.tensor_scalar(room_i[:], room[:], float(P - 1), None, ALU.add))
            then(nc.vector.tensor_scalar(room_i[:], room_i[:], 7, None, ALU.arith_shift_right))
            then(nc.vector.tensor_scalar(tiles[:], room_i[:], 1.0, None, ALU.max))
            then(nc.vector.tensor_tensor_scan(first_tile[:, 1:], M["ones"][:, 0:RBLK], tiles[:], 0.0, ALU.mult, ALU.add))
            then(nc.vector.scalar_tensor_tensor(out=offset[:], in0=first_tile[:, 0:RBLK], scalar=-float(P),
                                                in1=first_edge[:, 0:RBLK], op0=ALU.mult, op1=ALU.add))
            st.mark(nc.vector.tensor_copy(delta[:, 0:1], offset[:, 0:1]))
            then(nc.vector.tensor_tensor(delta[:, 1:], offset[:, 1:], offset[:, 0:RBLK - 1], ALU.subtract))
            dve.wait_ge(S["number_set"], 1)
            over_tiles = lambda x: x[0:TS_ROWS, None, 0:RBLK].broadcast_to([TS_ROWS, TS_COLS, RBLK])
            then(nc.vector.tensor_tensor(begun[:], over_tiles(first_tile),
                                         number[:, :, None].broadcast_to([TS_ROWS, TS_COLS, RBLK]), ALU.is_le))
            st.mark(nc.vector.tensor_reduce(blk[:], begun[:], AX_X, ALU.add))
            then(nc.vector.tensor_tensor(begun_off[:], begun[:], over_tiles(delta), ALU.mult))
            then(nc.vector.tensor_reduce(base[:], begun_off[:], AX_X, ALU.add))
            st.mark(nc.vector.tensor_scalar(blk[:], blk[:], -1.0, None, ALU.add))
            then(nc.vector.scalar_tensor_tensor(out=start[:], in0=number[:], scalar=float(P), in1=base[:],
                                                op0=ALU.mult, op1=ALU.add))
            nc.vector.tensor_copy(blk_i[:], blk[:]).then_inc(S["placed"], 1)
            nc.vector.tensor_scalar(start_i[:], start[:], float(E), None, ALU.min).then_inc(S["placed"], 1)
            dve.wait_ge(S["gathered"], 16 * TS_COLS)
            field = lambda k: meta[:].rearrange("p t (e c) -> p t e c", c=3)[:, :, :, k]
            by_tile = lambda x: x[:].rearrange("p (t e) -> p t e", e=P)
            wide = lambda x: x[:, :, None].broadcast_to([TS_ROWS, TS_COLS, P])
            st.mark(nc.vector.tensor_scalar(src_f[:], field(0), 0.0, None, ALU.max))
            st.mark(nc.vector.tensor_copy(by_tile(type_b), field(2)))
            then(nc.vector.tensor_copy(dst_f[:], field(1)))
            st.mark(nc.vector.tensor_scalar(blk[:], blk[:], float(P), None, ALU.mult))
            st.settle()
            then(nc.vector.tensor_tensor(local[:], dst_f[:], wide(blk), ALU.subtract))
            then(nc.vector.tensor_scalar(low[:], local[:], float(P), None, ALU.is_lt))
            then(nc.vector.scalar_tensor_tensor(out=valid[:], in0=local[:], scalar=0.0, in1=low[:],
                                                op0=ALU.is_ge, op1=ALU.mult))
            then(nc.vector.scalar_tensor_tensor(out=dst_f[:], in0=dst_f[:], scalar=1.0, in1=valid[:],
                                                op0=ALU.add, op1=ALU.mult))
            then(nc.vector.tensor_scalar(by_tile(M["segment"]), dst_f[:], -1.0, None, ALU.add))
            nc.vector.tensor_copy(by_tile(local_b), local[:]).then_inc(S["back"], 1)
            for b in range(4):
                dve.wait_ge(S["turned"], b + 1)
                to = (M["src"] if b < 2 else M["local"])[:].rearrange("p r c -> p c r")
                c = 4 * (b % 2)
                nc.vector.tensor_copy(to[:, c:c + 4, :], turn_ps[b][:, :, 0:TS_ROWS]).then_inc(S["back"], 1)
            dve.wait_ge(S["back"], 5)

        @block.tensor
        def _(pe):
            pe.wait_ge(S["steps"], 1 + RBLK)
            nc.tensor.matmul(total_ps[:], M["ones"][0:EROWS, :], count[:], start=True, stop=True).then_inc(S["totals"], 1)
            pe.wait_ge(S["back"], 1)
            for b in range(4):
                x = src_f if b < 2 else local
                for c in range(4):
                    ins = nc.tensor.transpose(turn_ps[b][:, c, 0:TS_ROWS], x[:, 4 * (b % 2) + c, :],
                                              M["ident"][0:TS_ROWS, 0:TS_ROWS])
                ins.then_inc(S["turned"], 1)


SLOTS = 16
HALF = SLOTS // 2
GROUPS = 4
GROUP = SLOTS // GROUPS
TURNS_E = T // SLOTS


def stage_scores(nc, A, M, R):
    with ExitStack() as ctx:
        sb = lambda name, shape, dt=F32: ctx.enter_context(nc.sbuf_tensor(name, shape, dt))
        sem = lambda name: ctx.enter_context(nc.semaphore(name))
        kv = sb("s_kv", [P, SLOTS, 2 * C])
        index = sb("s_index", [P, GROUPS, GROUP], I32)
        local = sb("s_local", [P, 2, HALF * P], BF16)
        kind = sb("s_kind", [P, 2, HALF * P], BF16)
        is_dst = sb("s_is_dst", [P, 2, HALF * P], BF16)
        is_kind = sb("s_is_kind", [P, 2, HALF * P], BF16)
        key = sb("s_key", [P, 2, GROUP, C])
        part = sb("s_part", [P, 2, HALF, H])
        qr_ps = [ctx.enter_context(nc.psum_tensor(f"s_qr_ps{b}", [P, GROUP, 2, C], F32)) for b in range(2)]
        gathered = [sem(f"s_gathered{g}") for g in range(GROUPS)]
        rows_in = [sem(f"s_rows_in{h}") for h in range(2)]
        v_out = [sem(f"s_v_out{g}") for g in range(GROUPS)]
        names = "index_ready key_added onehot_ready qr_done qr_free reduced part_used steps"
        S = {n: sem("s_" + n) for n in names.split()}
        row = lambda ap, n: ap[bass.ds(n, 1), :].broadcast_to([P, HALF * P])
        block = ctx.enter_context(nc.Block())

        @block.sync
        def _(sp):
            for h in range(2):
                sp.dma_start(local[:, h, :], row(R["local"], h)).then_inc(rows_in[h], 16)
                sp.dma_start(kind[:, h, :], row(R["type"], h)).then_inc(rows_in[h], 16)
            with sp.Fori(0, TURNS_E) as i:
                for h in range(2):
                    sp.wait_ge(S["onehot_ready"], i * 2 + h + 1)
                    sp.nop(nofuse=True)
                    sp.dma_start(local[:, h, :], row(R["local"], i * 2 + h + 2)).then_inc(rows_in[h], 16)
                    sp.dma_start(kind[:, h, :], row(R["type"], i * 2 + h + 2)).then_inc(rows_in[h], 16)
                    for g in (2 * h, 2 * h + 1):
                        sp.wait_ge(gathered[g], (i + 1) * (16 * GROUP))
                        sp.nop(nofuse=True)
                        sp.dma_start(R["v"][bass.ds(i * 2 + h, 1)].rearrange("a p n -> (a p) n")
                                     .rearrange("p (j c) -> p j c", c=C)[:, g % 2 * GROUP:(g % 2 + 1) * GROUP, :],
                                     kv[:, g * GROUP:(g + 1) * GROUP, C:]).then_inc(v_out[g], 16)
            for h in range(2):
                sp.wait_ge(rows_in[h], 32 * (TURNS_E + 1))
            for g in range(GROUPS):
                sp.wait_ge(v_out[g], 16 * TURNS_E)

        @block.scalar
        def _(act):
            def indices(g, turn):
                nc.scalar.copy(index[:, g, :], M["src"][:, bass.ds(turn * 2 + g // 2, 1), :]
                               .rearrange("p a c -> p (a c)")[:, g % 2 * GROUP:(g % 2 + 1) * GROUP]
                               ).then_inc(S["index_ready"], 1)

            def scores(h, i):
                act.wait_ge(S["reduced"], i * GROUPS + 2 * (h + 1))
                act.nop(nofuse=True)
                nc.scalar.copy(M["scores"][:, bass.ds(i * 2 + h, 1), :].rearrange("p a c -> p (a c)"),
                               part[:, h].rearrange("p u h -> p (u h)")).then_inc(S["part_used"], 1)

            for g in range(GROUPS):
                indices(g, 0)
            with act.Fori(0, TURNS_E - 1) as i:
                for g in range(GROUPS):
                    act.wait_ge(gathered[g], (i + 1) * (16 * GROUP))
                    act.nop(nofuse=True)
                    indices(g, i + 1)
                for h in range(2):
                    scores(h, i)
            for h in range(2):
                scores(h, TURNS_E - 1)
            act.wait_ge(S["part_used"], 2 * TURNS_E)

        @block.gpsimd
        def _(pool):
            with pool.Fori(0, TURNS_E) as i:
                for g in range(GROUPS):
                    pool.wait_ge(S["index_ready"], i * GROUPS + g + 1)
                    pool.wait_ge(v_out[g], i * 16)
                    pool.wait_ge(S["key_added"], i * GROUPS + g + 1)
                    pool.nop(nofuse=True)
                    for b in range(GROUP):
                        nc.gpsimd.indirect_dma_start(out=kv[:, g * GROUP + b, :], out_offset=None, in_=R["kv"],
                                                     in_offset=bass.IndirectOffsetOnAxis(ap=index[:, g, b:b + 1], axis=0)
                                                     ).then_inc(gathered[g], 16)

        @block.vector
        def _(dve):
            def onehots(h, n):
                dve.wait_ge(rows_in[h], n)
                nc.vector.tensor_scalar(is_dst[:, h, :], local[:, h, :], M["lane"][:], None, ALU.is_equal)\
                  .then_inc(S["steps"], 1)
                nc.vector.tensor_scalar(is_kind[:, h, :], kind[:, h, :], M["lane64"][:], None, ALU.is_equal)\
                  .then_inc(S["onehot_ready"], 1)

            nc.vector.memset(key[:, 0, 0, 0:1], 0.0).then_inc(S["key_added"], GROUPS)
            nc.vector.memset(key[:, 1, 0, 0:1], 0.0).then_inc(S["qr_free"], 2)
            dve.wait_ge(S["key_added"], GROUPS)
            dve.wait_ge(S["qr_free"], 2)
            onehots(0, 32)
            with dve.Fori(0, TURNS_E) as i:
                for h in range(2):
                    onehots(1 - h, (i + h + 1) * 32)
                    for g in (2 * h, 2 * h + 1):
                        n, b = i * GROUPS + g, g % 2
                        dve.wait_ge(S["qr_done"], n + 1)
                        dve.wait_ge(gathered[g], (i + 1) * (16 * GROUP))
                        if g >= 2:
                            dve.wait_ge(S["reduced"], n - 1)
                        else:
                            dve.wait_ge(S["qr_free"], n + 2)
                        nc.vector.tensor_tensor(key[:, b], kv[:, g * GROUP:(g + 1) * GROUP, 0:C], qr_ps[b][:, :, 1, :],
                                                ALU.add).then_inc(S["key_added"], 1)
                        dve.wait_ge(S["key_added"], n + 1 + GROUPS)
                        nc.vector.tensor_tensor(key[:, b], key[:, b], qr_ps[b][:, :, 0, :], ALU.mult
                                                ).then_inc(S["qr_free"], 1)
                        dve.wait_ge(S["part_used"], i * 2)
                        dve.wait_ge(S["qr_free"], n + 3)
                        nc.vector.tensor_reduce(part[:, h, b * GROUP:(b + 1) * GROUP, :].rearrange("p u h -> p (u h)"),
                                                key[:, b].rearrange("p u (h d) -> p (u h) d", d=D), AX_X, ALU.add
                                                ).then_inc(S["reduced"], 1)

        @block.tensor
        def _(pe):
            at_block = [pe.alloc_register(f"s_at{u}") for u in range(SLOTS)]
            with pe.Fori(0, TURNS_E) as i:
                regs = load_row(pe, at_block, M["blk"][0:1, bass.ds(i * SLOTS, SLOTS)], RBLK - 1)
                for g in range(GROUPS):
                    h, b = g // 2, g % 2
                    if b == 0:
                        pe.wait_ge(S["onehot_ready"], i * 2 + h + 1)
                    pe.wait_ge(S["qr_free"], i * GROUPS + g + 1)
                    pe.nop(nofuse=True)
                    for u in range(GROUP):
                        e = slice((b * GROUP + u) * P, (b * GROUP + u + 1) * P)
                        for j in range(3):
                            nc.tensor.matmul(qr_ps[b][:, u, 0, :], is_dst[:, h, e],
                                             M["q3"][:, bass.ds(regs[g * GROUP + u], 1), j, :]
                                             .rearrange("p a c -> p (a c)"), start=(j == 0), stop=(j == 2))
                        nc.tensor.matmul(qr_ps[b][:, u, 1, :], is_kind[:, h, e], M["rel_12"][:], start=True, stop=False)
                        ins = nc.tensor.matmul(qr_ps[b][:, u, 1, :], is_kind[0:64, h, e], M["rel_3"][0:64, :],
                                               start=False, stop=True)
                    ins.then_inc(S["qr_done"], 1)


def stage_softmax(nc, A, M, R):
    with ExitStack() as ctx:
        sb = lambda name, shape, dt=F32: ctx.enter_context(nc.sbuf_tensor(name, shape, dt))
        sem = lambda name: ctx.enter_context(nc.semaphore(name))
        W = TS_COLS * P
        score = sb("m_score", [TS_ROWS, H, W])
        most = sb("m_most", [TS_ROWS, H, W])
        new = sb("m_new", [TS_ROWS, W + 1])
        in_first = sb("m_in_first", [TS_ROWS, W])
        in_last = sb("m_in_last", [TS_ROWS, W])
        ends = sb("m_ends", [TS_ROWS, 4, H])
        ends_t = sb("m_ends_t", [H, 4, TS_ROWS])
        link = sb("m_link", [H, TS_ROWS + 1])
        whole = sb("m_whole", [H, TS_ROWS])
        gate_f = sb("m_gate_f", [H, TS_ROWS])
        gate_b = sb("m_gate_b", [H, TS_ROWS])
        run_f = sb("m_run_f", [H, TS_ROWS])
        run_b = sb("m_run_b", [H, TS_ROWS])
        carry = sb("m_carry", [H, 2, TS_ROWS])
        carry_t = sb("m_carry_t", [TS_ROWS, 2, H])
        bank = [ctx.enter_context(nc.psum_tensor(f"m_bank{b}", [P, 4, P], F32)) for b in range(4)]
        small = ctx.enter_context(nc.psum_tensor("m_small", [P, 4, P], F32))
        names = "steps turned copied ends_turned ends_ready carry_turned exp_ready back_turned back"
        S = {n: sem("m_" + n) for n in names.split()}
        seg = M["segment"]
        n_bank = 2 * H
        block = ctx.enter_context(nc.Block())

        @block.tensor
        def _(pe):
            view = M["scores"][:].rearrange("p r (c h) -> p h c r", h=H)
            for b in range(n_bank):
                if b >= 4:
                    pe.wait_ge(S["copied"], b - 3)
                for j in range(4):
                    ins = nc.tensor.transpose(bank[b % 4][0:TS_ROWS, j, :], view[:, b // 2, 4 * (b % 2) + j, :],
                                              M["ident"][:])
                ins.then_inc(S["turned"], 1)
            pe.wait_ge(S["ends_ready"], 1)
            for j in range(4):
                ins = nc.tensor.transpose(small[0:H, j, 0:TS_ROWS], ends[:, j, :], M["ident"][0:TS_ROWS, 0:TS_ROWS])
            ins.then_inc(S["ends_turned"], 1)
            pe.wait_ge(S["ends_ready"], 2)
            for j in range(2):
                ins = nc.tensor.transpose(small[0:TS_ROWS, j, 0:H], carry[:, j, :], M["ident"][0:H, 0:H])
            ins.then_inc(S["carry_turned"], 1)
            pe.wait_ge(S["copied"], n_bank)
            for b in range(n_bank):
                pe.wait_ge(S["exp_ready"], b // 2 + 1)
                if b >= 4:
                    pe.wait_ge(S["back"], b - 3)
                for j in range(4):
                    c = 4 * (b % 2) + j
                    ins = nc.tensor.transpose(bank[b % 4][:, j, 0:TS_ROWS], score[:, b // 2, c * P:(c + 1) * P],
                                              M["ident"][0:TS_ROWS, 0:TS_ROWS])
                ins.then_inc(S["back_turned"], 1)

        @block.scalar
        def _(act):
            for b in range(n_bank):
                act.wait_ge(S["turned"], b + 1)
                nc.scalar.copy(score[:, b // 2, (b % 2) * 512:(b % 2) * 512 + 512],
                               bank[b % 4][0:TS_ROWS].rearrange("p j n -> p (j n)")).then_inc(S["copied"], 1)
            for h in range(H):
                act.wait_ge(S["steps"], M["softmax_steps"] + h)
                nc.scalar.activation(score[:, h, :], most[:, h, :], ACT.Exp).then_inc(S["exp_ready"], 1)
            view = M["scores"][:].rearrange("p r (c h) -> p h c r", h=H)
            for b in range(n_bank):
                act.wait_ge(S["back_turned"], b + 1)
                c = 4 * (b % 2)
                nc.scalar.copy(view[:, b // 2, c:c + 4, :], bank[b % 4][:, :, 0:TS_ROWS]).then_inc(S["back"], 1)
            act.wait_ge(S["back"], n_bank)

        @block.vector
        def _(dve):
            st = Steps(dve, S["steps"])

            def then(ins):
                st.mark(ins)
                st.settle()

            st.mark(nc.vector.memset(new[:, 0:1], 0.0))
            st.mark(nc.vector.memset(new[:, W:], 0.0))
            then(nc.vector.tensor_tensor(new[:, 1:W], seg[:, 1:], seg[:, 0:W - 1], ALU.is_equal))
            then(nc.vector.tensor_scalar(new[:], new[:], -1.0, BIG, ALU.add, ALU.mult))
            st.mark(nc.vector.tensor_scalar(in_first[:], seg[:], seg[:, 0:1], None, ALU.is_equal))
            then(nc.vector.tensor_scalar(in_last[:], seg[:], seg[:, W - 1:W], None, ALU.is_equal))
            st.mark(nc.vector.tensor_scalar(in_first[:], in_first[:], -1.0, BIG, ALU.add, ALU.mult))
            then(nc.vector.tensor_scalar(in_last[:], in_last[:], -1.0, BIG, ALU.add, ALU.mult))
            for h in range(H):
                dve.wait_ge(S["copied"], 2 * h + 2)
                then(nc.vector.tensor_tensor_scan(most[:, h, :], new[:, 0:W], score[:, h, :], -BIG, ALU.add, ALU.max))
                then(nc.vector.tensor_copy(ends[:, 0, h:h + 1], most[:, h, W - 1:W]))
                then(nc.vector.tensor_tensor_scan(most[:, h, ::-1], new[:, 1:][:, ::-1], most[:, h, ::-1],
                                                  -BIG, ALU.add, ALU.max))
                st.mark(nc.vector.tensor_copy(ends[:, 1, h:h + 1], most[:, h, 0:1]))
            st.mark(nc.vector.tensor_copy(ends[:, 2, :], seg[:, W - 1:W].broadcast_to([TS_ROWS, H])))
            st.mark(nc.vector.tensor_copy(ends[:, 3, :], seg[:, 0:1].broadcast_to([TS_ROWS, H])))
            st.settle()
            nc.vector.memset(link[:, 0:1], 0.0).then_inc(S["ends_ready"], 1)
            st.mark(nc.vector.memset(link[:, TS_ROWS:], 0.0))
            dve.wait_ge(S["ends_turned"], 1)
            then(nc.vector.tensor_copy(ends_t[:], small[0:H, :, 0:TS_ROWS]))
            last_f, first_b, last_seg, first_seg = (ends_t[:, j, :] for j in range(4))
            st.mark(nc.vector.tensor_tensor(link[:, 1:TS_ROWS], first_seg[:, 1:], last_seg[:, 0:TS_ROWS - 1], ALU.is_equal))
            then(nc.vector.tensor_tensor(whole[:], first_seg, last_seg, ALU.is_equal))
            st.mark(nc.vector.tensor_tensor(gate_f[:], link[:, 0:TS_ROWS], whole[:], ALU.mult))
            then(nc.vector.tensor_tensor(gate_b[:], link[:, 1:], whole[:], ALU.mult))
            st.mark(nc.vector.tensor_scalar(gate_f[:], gate_f[:], -1.0, BIG, ALU.add, ALU.mult))
            st.mark(nc.vector.tensor_scalar(gate_b[:], gate_b[:], -1.0, BIG, ALU.add, ALU.mult))
            then(nc.vector.tensor_scalar(link[:], link[:], -1.0, BIG, ALU.add, ALU.mult))
            st.mark(nc.vector.tensor_tensor_scan(run_f[:], gate_f[:], last_f, -BIG, ALU.add, ALU.max))
            then(nc.vector.tensor_tensor_scan(run_b[:, ::-1], gate_b[:, ::-1], first_b[:, ::-1], -BIG, ALU.add, ALU.max))
            st.mark(nc.vector.memset(carry[:, 0, 0:1], -BIG))
            st.mark(nc.vector.memset(carry[:, 1, TS_ROWS - 1:], -BIG))
            st.mark(nc.vector.tensor_tensor(carry[:, 0, 1:], run_f[:, 0:TS_ROWS - 1], link[:, 1:TS_ROWS], ALU.add))
            st.settle()
            nc.vector.tensor_tensor(carry[:, 1, 0:TS_ROWS - 1], run_b[:, 1:], link[:, 1:TS_ROWS],
                                    ALU.add).then_inc(S["ends_ready"], 1)
            dve.wait_ge(S["carry_turned"], 1)
            then(nc.vector.tensor_copy(carry_t[:], small[0:TS_ROWS, 0:2, 0:H]))
            for h in range(H):
                then(nc.vector.scalar_tensor_tensor(out=most[:, h, :], in0=in_first[:], scalar=carry_t[:, 0, h:h + 1],
                                                    in1=most[:, h, :], op0=ALU.add, op1=ALU.max))
                then(nc.vector.scalar_tensor_tensor(out=most[:, h, :], in0=in_last[:], scalar=carry_t[:, 1, h:h + 1],
                                                    in1=most[:, h, :], op0=ALU.add, op1=ALU.max))
            for h in range(H):
                if h == 0:
                    assert st.n + 1 == M["softmax_steps"], st.n + 1
                then(nc.vector.tensor_tensor(most[:, h, :], score[:, h, :], most[:, h, :], ALU.subtract))


AGG = C + H


def stage_aggregate(nc, A, M, R):
    with ExitStack() as ctx:
        sb = lambda name, shape, dt=F32: ctx.enter_context(nc.sbuf_tensor(name, shape, dt))
        sem = lambda name: ctx.enter_context(nc.semaphore(name))
        v = sb("a_v", [P, 2, HALF, C])
        w = sb("a_w", [P, 2, HALF, AGG])
        is_dst = sb("a_is_dst", [P, 2, HALF, P])
        ex = sb("a_ex", [P, 2, HALF, H])
        odd = sb("a_odd_sums", [P, RBLK, AGG])
        sum_ps = [ctx.enter_context(nc.psum_tensor(f"a_sum_ps{b}", [P, AGG], F32)) for b in range(8)]
        v_in = [sem(f"a_v_in{h}") for h in range(2)]
        names = "zeroed started ex_ready pool_done act_done dve_done onehot_ready summed added whole"
        S = {n: sem("a_" + n) for n in names.split()}
        POOL_N, ACT_N = 5, 2
        sums = M["sums"]
        heads = lambda x: x.rearrange("p u (h d) -> p u h d", d=D)
        block = ctx.enter_context(nc.Block())

        @block.sync
        def _(sp):
            with sp.Fori(0, TURNS_E) as i:
                for h in range(2):
                    for name in ("pool_done", "act_done", "dve_done"):
                        sp.wait_ge(S[name], i * 2 + h)
                    sp.nop(nofuse=True)
                    sp.dma_start(v[:, h].rearrange("p u c -> p (u c)"),
                                 R["v"][bass.ds(i * 2 + h, 1)].rearrange("a p n -> (a p) n")).then_inc(v_in[h], 16)

        @block.scalar
        def _(act):
            act.wait_ge(S["started"], 1)
            with act.Fori(0, TURNS_E) as i:
                for h in range(2):
                    hh = i * 2 + h
                    act.wait_ge(S["pool_done"], hh)
                    act.wait_ge(S["dve_done"], hh)
                    act.wait_ge(S["act_done"], hh)
                    act.nop(nofuse=True)
                    nc.scalar.copy(ex[:, h].rearrange("p u h -> p (u h)"),
                                   M["scores"][:, bass.ds(hh, 1), :].rearrange("p a c -> p (a c)")).then_inc(S["ex_ready"], 1)
                    act.wait_ge(S["ex_ready"], hh + 1)
                    act.wait_ge(v_in[h], (i + 1) * 16)
                    act.wait_ge(S["summed"], hh * 2)
                    for u in range(HALF - ACT_N, HALF):
                        for hd in range(H):
                            ins = nc.scalar.activation(w[:, h, u, hd * D:(hd + 1) * D], v[:, h, u, hd * D:(hd + 1) * D],
                                                       ACT.Copy, scale=ex[:, h, u, hd:hd + 1])
                    ins.then_inc(S["act_done"], 1)

        @block.gpsimd
        def _(pool):
            nc.gpsimd.memset(sums[:], 0.0).then_inc(S["zeroed"], 1)
            pool.wait_ge(S["started"], 1)
            with pool.Fori(0, TURNS_E) as i:
                for h in range(2):
                    hh = i * 2 + h
                    pool.wait_ge(S["ex_ready"], hh + 1)
                    pool.wait_ge(v_in[h], (i + 1) * 16)
                    pool.wait_ge(S["summed"], hh * 2)
                    pool.nop(nofuse=True)
                    nc.gpsimd.tensor_tensor(heads(w[:, h, 0:POOL_N, 0:C]), heads(v[:, h, 0:POOL_N, :]),
                                            ex[:, h, 0:POOL_N, :, None].broadcast_to([P, POOL_N, H, D]), ALU.mult)
                    nc.gpsimd.tensor_copy(w[:, h, :, C:], ex[:, h]).then_inc(S["pool_done"], 1)

        @block.vector
        def _(dve):
            nc.vector.memset(is_dst[:, 0, 0, 0:1], 0.0).then_inc(S["added"], 8)
            for name in ("pool_done", "act_done", "dve_done"):
                dve.sem_inc(S[name], 1)
            dve.sem_inc(S["summed"], 2)
            dve.wait_ge(S["added"], 8)
            dve.sem_inc(S["started"], 3)

            def prepare(h, hh, turn):
                dve.wait_ge(S["summed"], hh * 2)
                dve.nop(nofuse=True)
                nc.vector.tensor_tensor(is_dst[:, h], M["col"][:, None, :].broadcast_to([P, HALF, P]),
                                        M["local"][:, bass.ds(hh, 1), :].rearrange("p a u -> p (a u)")[:, :, None]
                                        .broadcast_to([P, HALF, P]), ALU.is_equal).then_inc(S["onehot_ready"], 1)
                dve.wait_ge(S["ex_ready"], hh + 1)
                dve.wait_ge(v_in[h], (turn + 1) * 16)
                mine = slice(POOL_N, HALF - ACT_N)
                nc.vector.tensor_tensor(heads(w[:, h, mine, 0:C]), heads(v[:, h, mine, :]),
                                        ex[:, h, mine, :, None].broadcast_to([P, HALF - ACT_N - POOL_N, H, D]), ALU.mult
                                        ).then_inc(S["dve_done"], 1)

            def add(h, i, regs):
                for u in range(HALF):
                    t = i * SLOTS + h * HALF + u
                    if u % GROUP == 0:
                        dve.wait_ge(S["summed"], i * GROUPS + h * 2 + u // GROUP + 3)
                    dve.wait_ge(S["added"], t + 7)
                    dve.nop(nofuse=True)
                    at = (sums, odd)[u % 2][:, bass.ds(regs[h * HALF + u], 1), :].rearrange("p a c -> p (a c)")
                    nc.vector.tensor_tensor(at, at, sum_ps[u][:], ALU.add).then_inc(S["added"], 1)

            at_block = [dve.alloc_register(f"a_at{u}") for u in range(SLOTS)]
            row = lambda i: load_row(dve, at_block, M["blk"][0:1, bass.ds(i * SLOTS, SLOTS)], RBLK - 1)
            nc.vector.memset(odd[:], 0.0).then_inc(S["zeroed"], 1)
            prepare(0, 0, 0)
            dve.wait_ge(S["zeroed"], 2)
            with dve.Fori(0, TURNS_E - 1) as i:
                regs = row(i)
                prepare(1, i * 2 + 1, i)
                add(0, i, regs)
                prepare(0, i * 2 + 2, i + 1)
                add(1, i, regs)
            i = TURNS_E - 1
            regs = row(i)
            prepare(1, i * 2 + 1, i)
            add(0, i, regs)
            add(1, i, regs)
            dve.wait_ge(S["added"], T + 8)
            nc.vector.tensor_tensor(sums[:, 0:RBLK, :], sums[:, 0:RBLK, :], odd[:], ALU.add).then_inc(S["whole"], 1)
            dve.wait_ge(S["whole"], 1)

        @block.tensor
        def _(pe):
            pe.wait_ge(S["started"], 1)
            with pe.Fori(0, TURNS_E) as i:
                for h in range(2):
                    hh = i * 2 + h
                    pe.wait_ge(S["onehot_ready"], hh + 1)
                    for name in ("pool_done", "act_done", "dve_done"):
                        pe.wait_ge(S[name], hh + 2)
                    for g in range(2):
                        pe.wait_ge(S["added"], (hh * 2 + g) * GROUP + 4)
                        for u in range(g * GROUP, (g + 1) * GROUP):
                            ins = nc.tensor.matmul(sum_ps[u][:], is_dst[:, h, u, :], w[:, h, u, :], start=True, stop=True)
                        ins.then_inc(S["summed"], 1)


def load_row(eng, regs, row, most):
    eng.load(regs, row)
    return [eng.snap(r, min_val=0, max_val=most) for r in regs]


NQ = NBLK // QUAD


def stage_mixer(nc, A, M, R):
    with ExitStack() as ctx:
        sb = lambda name, shape, dt=F32: ctx.enter_context(nc.sbuf_tensor(name, shape, dt))
        sem = lambda name: ctx.enter_context(nc.semaphore(name))
        wout = sb("x_wout", [P, MH // 2, C])
        wq = sb("x_wq", [P, MH // 2, C])
        pairs = sb("x_pairs", [P, MH // 2, P])
        vw = sb("x_vw", [P, MH // 2, C])
        vw_ps = [ctx.enter_context(nc.psum_tensor(f"x_vw_ps{j}", [P, C], F32)) for j in range(MH // 2)]
        z_ps = [ctx.enter_context(nc.psum_tensor(f"x_z_ps{k}", [P, C], F32)) for k in range(KC)]
        S = {n: sem("x_" + n) for n in "loaded zeroed paired multiplied copied z_done z_read".split()}
        block = ctx.enter_context(nc.Block())

        @block.sync
        def _(sp):
            sp.dma_start(wout[:], rows(A["mix_WoutT"], MH // 2)).then_inc(S["loaded"], 16)
            sp.dma_start(wq[:], rows(A["mix_Wq"], MH // 2)).then_inc(S["loaded"], 16)

        @block.vector
        def _(dve):
            nc.vector.memset(pairs[:], 0.0).then_inc(S["zeroed"], 1)
            dve.wait_ge(S["zeroed"], 1)
            for half in (slice(0, MD), slice(MD, 2 * MD)):
                nc.vector.tensor_copy(pairs[half, :, half], M["dots"][half, :, half]).then_inc(S["paired"], 1)
            for j in range(MH // 2):
                dve.wait_ge(S["multiplied"], j + 1)
                nc.vector.tensor_copy(vw[:, j, :], vw_ps[j][:]).then_inc(S["copied"], 1)
            dve.wait_ge(S["z_done"], KC)
            for k in range(KC):
                nc.vector.tensor_scalar(M["z"][:, k, :], z_ps[k][:], 1.0 / N, None, ALU.mult).then_inc(S["z_read"], 1)
            dve.wait_ge(S["z_read"], KC)

        @block.tensor
        def _(pe):
            pe.wait_ge(S["loaded"], 32)
            pe.wait_ge(S["paired"], 2)
            for j in range(MH // 2):
                nc.tensor.matmul(vw_ps[j][:], pairs[:, j, :], wout[:, j, :], start=True, stop=True
                                 ).then_inc(S["multiplied"], 1)
            pe.wait_ge(S["copied"], MH // 2)
            for k in range(KC):
                for j in range(MH // 2):
                    ins = nc.tensor.matmul(z_ps[k][:], wq[:, j, k * P:(k + 1) * P], vw[:, j, :], start=(j == 0),
                                           stop=(j == MH // 2 - 1))
                ins.then_inc(S["z_done"], 1)


def stage_nodes(nc, A, M, R):
    with ExitStack() as ctx:
        sb = lambda name, shape, dt=F32: ctx.enter_context(nc.sbuf_tensor(name, shape, dt))
        sem = lambda name: ctx.enter_context(nc.semaphore(name))
        wo = sb("n_wo", [P, KC, C])
        bo = sb("n_bo", [P, C])
        gamma = sb("n_gamma", [P, C])
        beta = sb("n_beta", [P, C])
        bout = sb("n_bout", [P, C])
        rden = sb("n_rden", [P, NBLK, H])
        none = sb("n_none", [P, NBLK])
        v = sb("n_v", [P, 3, QUAD, C])
        x = sb("n_x", [P, 3, QUAD, C])
        xn = sb("n_xn", [P, 3, QUAD, C])
        xnt = sb("n_xnt", [P, 3, QUAD, KC * P])
        y = sb("n_y", [P, 3, QUAD, C])
        turned = sb("n_turned", [P, QUAD, KC * P])
        out = sb("n_out", [P, 3, QUAD, 2 * C])
        x2t = sb("n_x2t", [P, QUAD, KC * P])
        x2t_out = sem("n_x2t_out")
        stats = sb("n_stats", [P, 2, QUAD, 6])
        mv = sb("n_mv", [P, 2, QUAD, 2])
        std = sb("n_std", [P, 2, QUAD])
        rstd = sb("n_rstd", [P, 2, QUAD])
        t_ps = ctx.enter_context(nc.psum_tensor("n_t_ps", [P, QUAD, KC * P], F32))
        x2_ps = ctx.enter_context(nc.psum_tensor("n_x2_ps", [P, QUAD, KC * P], F32))
        y_ps = ctx.enter_context(nc.psum_tensor("n_y_ps", [P, QUAD, C], F32))
        z_ps = ctx.enter_context(nc.psum_tensor("n_z_ps", [P, QUAD, C], F32))
        fixed_in = sem("n_fixed_in")
        loads = [sem(f"n_loads{w}") for w in range(3)]
        stored = [sem(f"n_stored{w}") for w in range(3)]
        names = ("steps msg_steps x1_steps bias_ready v_ready msg_ready msg_turned msg_copied y_done z_done xn_ready "
                 "x_ready y_sum mv0_ready mv1_ready std0_ready std1_ready y_normed y_scaled x1_ready x2_ready "
                 "x2_turned x2_copied")
        S = {n: sem("n_" + n) for n in names.split()}
        sums = M["sums"]
        quad = lambda ap, w: ap.rearrange("(q b p) c -> q p b c", b=QUAD, p=P)[bass.ds(w, 1)].rearrange(
            "a p b c -> (a p) b c")
        block = ctx.enter_context(nc.Block())

        def turns(ahead, main, behind, eng):
            ahead(0, 0, 0)
            ahead(1, 1, 0)
            main(0, 0, 0)
            with eng.Fori(0, (NQ - 2) // 3) as i:
                for w in range(3):
                    ahead(i * 3 + w + 2, (w + 2) % 3, i + (w + 2) // 3)
                    main(i * 3 + w + 1, (w + 1) % 3, i + (w + 1) // 3)
                    behind(i * 3 + w, w, i)
            for q in range((NQ - 2) // 3 * 3 + 1, NQ):
                if q + 1 < NQ:
                    ahead(q + 1, (q + 1) % 3, (q + 1) // 3)
                main(q, q % 3, q // 3)
                behind(q - 1, (q - 1) % 3, (q - 1) // 3)
            behind(NQ - 1, (NQ - 1) % 3, (NQ - 1) // 3)

        def nothing(q, w, k):
            pass

        @block.sync
        def _(sp):
            sp.dma_start(wo[:], rows(A["L0_gnn_Wo"], KC)).then_inc(fixed_in, 16)
            for tile, name in ((bo, "L0_gnn_bo"), (gamma, "L0_gnn_gamma"), (beta, "L0_gnn_beta"), (bout, "L0_mix_bout")):
                sp.dma_start(tile[:], A[name].rearrange("(a n) -> a n", a=1).broadcast_to([P, C])).then_inc(fixed_in, 16)

            def load(q, w):
                sp.dma_start(v[:, w], quad(R["kv"][:, C:], q)).then_inc(loads[w], 16)
                sp.dma_start(x[:, w], quad(A["x"][0:NPAD, :], q)).then_inc(loads[w], 16)
                sp.dma_start(xn[:, w], quad(R["xn"], q)).then_inc(loads[w], 16)
                sp.dma_start(xnt[:, w], R["xnt"].rearrange("(q b) p n -> q p b n", b=QUAD)[bass.ds(q, 1)]
                             .rearrange("a p b n -> (a p) b n")).then_inc(loads[w], 16)

            def load_next(q, w, k):
                if isinstance(q, int) and q + 1 >= NQ:
                    return
                if not (isinstance(q, int) and q <= 1):
                    sp.wait_ge(S["x1_ready"], q - 1)
                    sp.nop(nofuse=True)
                load(q + 1, (w + 1) % 3)

            def store(q, w, k):
                sp.wait_ge(S["x2_ready"], q + 1)
                sp.nop(nofuse=True)
                sp.dma_start(quad(R["x12"], q), out[:, w]).then_inc(stored[w], 16)

            load(0, 0)
            turns(load_next, nothing, store, sp)
            for w in range(3):
                sp.wait_ge(stored[w], 16 * ((NQ + 2 - w) // 3))

        @block.gpsimd
        def _(pool):
            pool.wait_ge(fixed_in, 80)
            nc.gpsimd.tensor_tensor(beta[:], beta[:], bout[:], ALU.add).then_inc(S["bias_ready"], 1)
            pool.wait_ge(S["bias_ready"], 1)
            pool.wait_ge(S["steps"], 3)
            over = lambda t: t[:, None, :].broadcast_to([P, QUAD, C])

            def prepare(q, w, k):
                pool.wait_ge(loads[w], (k + 1) * 64)
                pool.nop(nofuse=True)
                nc.gpsimd.tensor_tensor(v[:, w], v[:, w], none[:, bass.ds(q * QUAD, QUAD)][:, :, None].broadcast_to(
                    [P, QUAD, C]), ALU.mult).then_inc(S["v_ready"], 1)
                nc.gpsimd.tensor_tensor(xn[:, w], xn[:, w], over(bo), ALU.add).then_inc(S["xn_ready"], 1)
                nc.gpsimd.tensor_tensor(x[:, w], x[:, w], over(beta), ALU.add).then_inc(S["x_ready"], 1)

            def scale(q, w, k):
                pool.wait_ge(S["y_normed"], (q + 1) * QUAD)
                pool.nop(nofuse=True)
                nc.gpsimd.tensor_tensor(y[:, w], y[:, w], over(gamma), ALU.mult).then_inc(S["y_scaled"], 1)
                pool.wait_ge(S["y_scaled"], q * 2 + 1)
                pool.wait_ge(S["x_ready"], q + 1)
                pool.nop(nofuse=True)
                nc.gpsimd.tensor_tensor(y[:, w], y[:, w], x[:, w], ALU.add).then_inc(S["y_scaled"], 1)

            turns(prepare, scale, nothing, pool)

        @block.scalar
        def _(act):
            def deviation(q, j):
                act.wait_ge(S[f"mv{j}_ready"], (q + 1) * QUAD)
                act.nop(nofuse=True)
                nc.scalar.activation(std[:, j, :], mv[:, j, :, 1], ACT.Sqrt, bias=M["eps"][:]
                                     ).then_inc(S[f"std{j}_ready"], 1)

            def copy_messages(q, w, k):
                act.wait_ge(S["msg_turned"], q + 1)
                act.wait_ge(S["y_done"], q)
                act.nop(nofuse=True)
                nc.scalar.copy(turned[:], t_ps[:]).then_inc(S["msg_copied"], 1)

            def graph_deviation(q, w, k):
                deviation(q, 0)

            def finish(q, w, k):
                deviation(q, 1)
                act.wait_ge(S["x2_turned"], q + 3)
                act.wait_ge(x2t_out, q * 16)
                act.nop(nofuse=True)
                nc.scalar.copy(x2t[:], x2_ps[:]).then_inc(S["x2_copied"], 1)
                act.wait_ge(S["x2_copied"], q + 1)
                act.nop(nofuse=True)
                act.dma_start(R["x2t"][bass.ds(q, 1)].rearrange("a p n -> (a p) n"),
                              x2t[:].rearrange("p b n -> p (b n)")).then_inc(x2t_out, 16)

            turns(copy_messages, graph_deviation, finish, act)
            act.wait_ge(x2t_out, 16 * NQ)

        @block.vector
        def _(dve):
            st = Steps(dve, S["steps"])

            def then(ins):
                st.mark(ins)
                st.settle()

            den = sums[:, :, C:]
            then(nc.vector.tensor_scalar(rden[:], den, 0.5, None, ALU.max))
            then(nc.vector.reciprocal(rden[:], rden[:]))
            st.mark(nc.vector.tensor_scalar(none[:], sums[:, :, C], 0.0, None, ALU.is_equal))
            for h in range(H):
                part = sums[:, :, h * D:(h + 1) * D]
                st.mark(nc.vector.tensor_tensor(part, part, rden[:, :, h:h + 1].broadcast_to([P, NBLK, D]), ALU.mult))
            st.settle()
            PER = 5

            def statistics(q, src, j, steps):
                st = Steps(dve, S[steps], q * PER)
                for b in range(QUAD):
                    st.mark(nc.vector.bn_stats(stats[:, j, b, :], src[:, b, :]))
                st.settle()
                dve.nop(nofuse=True)
                for b in range(QUAD):
                    nc.vector.bn_aggr(mv[:, j, b, :], stats[:, j, b, :]).then_inc(S[f"mv{j}_ready"], 1)
                dve.wait_ge(S[f"std{j}_ready"], q + 1)
                st.mark(nc.vector.reciprocal(rstd[:, j, :], std[:, j, :]))
                st.settle()
                assert st.n == PER

            def messages(q, w, k):
                dve.wait_ge(S["v_ready"], q + 1)
                dve.nop(nofuse=True)
                nc.vector.tensor_tensor(v[:, w], v[:, w], sums[:, bass.ds(q * QUAD, QUAD), 0:C], ALU.add
                                        ).then_inc(S["msg_ready"], 1)

            def graph_norm(q, w, k):
                dve.wait_ge(S["y_done"], q + 1)
                dve.wait_ge(S["xn_ready"], q + 1)
                dve.wait_ge(S["y_normed"], q * QUAD)
                dve.nop(nofuse=True)
                nc.vector.tensor_tensor(y[:, w], y_ps[:], xn[:, w], ALU.add).then_inc(S["y_sum"], 1)
                dve.wait_ge(S["y_sum"], q + 1)
                dve.nop(nofuse=True)
                statistics(q, y[:, w], 0, "msg_steps")
                for b in range(QUAD):
                    nc.vector.tensor_scalar(y[:, w, b, :], y[:, w, b, :], mv[:, 0, b, 0:1], rstd[:, 0, b:b + 1],
                                            ALU.subtract, ALU.mult).then_inc(S["y_normed"], 1)

            def second_norm(q, w, k):
                dve.wait_ge(S["y_scaled"], q * 2 + 2)
                dve.wait_ge(S["z_done"], q + 1)
                dve.wait_ge(stored[w], k * 16)
                dve.wait_ge(S["x2_turned"], q)
                dve.wait_ge(S["x2_ready"], q)
                dve.nop(nofuse=True)
                nc.vector.tensor_tensor(out[:, w, :, 0:C], z_ps[:], y[:, w], ALU.add).then_inc(S["x1_ready"], 1)
                dve.wait_ge(S["x1_ready"], q + 1)
                dve.nop(nofuse=True)
                statistics(q, out[:, w, :, 0:C], 1, "x1_steps")
                for b in range(QUAD):
                    ins = nc.vector.tensor_scalar(out[:, w, b, C:], out[:, w, b, 0:C], mv[:, 1, b, 0:1],
                                                  rstd[:, 1, b:b + 1], ALU.subtract, ALU.mult)
                ins.then_inc(S["x2_ready"], 1)

            turns(messages, graph_norm, second_norm, dve)
            dve.wait_ge(S["x2_ready"], NQ)

        @block.tensor
        def _(pe):
            pe.wait_ge(fixed_in, 80)
            pe.sem_inc(S["x2_turned"], 2)

            def turn(to, src):
                for b in range(QUAD):
                    for k in range(KC):
                        ins = nc.tensor.transpose(to[:, b, k * P:(k + 1) * P], src[:, b, k * P:(k + 1) * P], M["ident"][:])
                return ins

            def product(to, left, right):
                for b in range(QUAD):
                    for k in range(KC):
                        ins = nc.tensor.matmul(to[:, b, :], left[:, b, k * P:(k + 1) * P], right[:, k, :],
                                               start=(k == 0), stop=(k == KC - 1))
                return ins

            def graph(q, w, k):
                pe.wait_ge(S["msg_ready"], q + 1)
                pe.wait_ge(S["msg_copied"], q)
                turn(t_ps, v[:, w]).then_inc(S["msg_turned"], 1)
                pe.wait_ge(S["msg_copied"], q + 1)
                pe.wait_ge(S["y_sum"], q)
                product(y_ps, turned, wo).then_inc(S["y_done"], 1)

            def mixer(q, w, k):
                pe.wait_ge(loads[w], (k + 1) * 64)
                pe.wait_ge(S["x1_ready"], q)
                product(z_ps, xnt[:, w], M["z"]).then_inc(S["z_done"], 1)

            def turn_x2(q, w, k):
                pe.wait_ge(S["x2_ready"], q + 1)
                pe.wait_ge(S["x2_copied"], q)
                turn(x2_ps, out[:, w, :, C:]).then_inc(S["x2_turned"], 1)

            turns(graph, mixer, turn_x2, pe)


NTILE = 56


def stage_hidden(nc, A, M, R):
    with ExitStack() as ctx:
        sb = lambda name, shape, dt=F32: ctx.enter_context(nc.sbuf_tensor(name, shape, dt))
        sem = lambda name: ctx.enter_context(nc.semaphore(name))
        wg = sb("h_wg", [P, HC, NEXP])
        bg = sb("h_bg", [P, NEXP])
        x2t = sb("h_x2t", [P, 2, QUAD, KC * P])
        ht = sb("h_ht", [P, HC, QUAD * P])
        h_ps = [ctx.enter_context(nc.psum_tensor(f"h_h_ps{b}", [P, QUAD * P], F32)) for b in range(4)]
        l_ps = [ctx.enter_context(nc.psum_tensor(f"h_l_ps{b}", [P, QUAD, NEXP], F32)) for b in range(2)]
        x_in = [sem(f"h_x_in{w}") for w in range(2)]
        S = {n: sem("h_" + n) for n in "fixed_in h_done gelu_done l_done l_read".split()}
        PAIRS = NQ // 2
        block = ctx.enter_context(nc.Block())

        def turns(eng, body):
            with eng.Fori(0, PAIRS) as i:
                for w in range(2):
                    body(i * 2 + w, w, i)
            body(NQ - 1, 0, PAIRS)

        @block.sync
        def _(sp):
            sp.dma_start(M["w1"][:], rows(A["L0_ffn_W1"], KC)).then_inc(S["fixed_in"], 16)
            sp.dma_start(M["b1"][:], A["L0_ffn_b1"].rearrange("(c p) -> p c", p=P),
                         allow_slow_non_contiguous=True).then_inc(S["fixed_in"], 16)
            sp.dma_start(wg[:], rows(A["L0_ffn_Wg"], HC)).then_inc(S["fixed_in"], 16)
            sp.dma_start(bg[:], A["L0_ffn_bg"].rearrange("(a n) -> a n", a=1).broadcast_to([P, NEXP])
                         ).then_inc(S["fixed_in"], 16)

            def load(q, w, i):
                sp.wait_ge(S["l_read"], q)
                sp.nop(nofuse=True)
                sp.dma_start(x2t[:, w].rearrange("p b n -> p (b n)"),
                             R["x2t"][bass.ds(q, 1)].rearrange("a p n -> (a p) n")).then_inc(x_in[w], 16)

            load(0, 0, 0)
            with sp.Fori(0, PAIRS) as i:
                for w in range(2):
                    sp.wait_ge(S["l_read"], i * 2 + w)
                    sp.nop(nofuse=True)
                    sp.dma_start(x2t[:, 1 - w].rearrange("p b n -> p (b n)"),
                                 R["x2t"][bass.ds(i * 2 + w + 1, 1)].rearrange("a p n -> (a p) n")).then_inc(x_in[1 - w], 16)
            for e in range(NEXP):
                sp.dma_start(M["wd"][:, e], rows(A["L0_ffn_Wd"][e], HC)).then_inc(S["fixed_in"], 16)
            sp.dma_start(M["bd"][:].rearrange("p e n -> p (e n)"), A["L0_ffn_bd"].rearrange("(a e) n -> a (e n)", a=1)
                         .broadcast_to([P, NEXP * C])).then_inc(S["fixed_in"], 16)
            sp.wait_ge(S["fixed_in"], 16 * (5 + NEXP))

        @block.scalar
        def _(act):
            act.wait_ge(S["fixed_in"], 64)

            def body(q, w, i):
                for c in range(HC):
                    act.wait_ge(S["h_done"], q * HC + c + 1)
                    if c == 0:
                        act.wait_ge(S["l_done"], q)
                    nc.scalar.activation(ht[:, c, :], h_ps[c % 4][:], ACT.Gelu, bias=M["b1"][:, c:c + 1]
                                         ).then_inc(S["gelu_done"], 1)

            turns(act, body)

        @block.vector
        def _(dve):
            dve.wait_ge(S["fixed_in"], 64)

            def body(q, w, i):
                dve.wait_ge(S["l_done"], q + 1)
                dve.nop(nofuse=True)
                nc.vector.tensor_tensor(M["logits"][:, bass.ds(q * QUAD, QUAD), :], l_ps[w][:],
                                        bg[:, None, :].broadcast_to([P, QUAD, NEXP]), ALU.add).then_inc(S["l_read"], 1)

            turns(dve, body)
            dve.wait_ge(S["l_read"], NQ)

        @block.tensor
        def _(pe):
            pe.wait_ge(S["fixed_in"], 64)

            def logits(q, w, c):
                pe.wait_ge(S["gelu_done"], q * HC + c + 1)
                for b in range(QUAD):
                    ins = nc.tensor.matmul(l_ps[w][:, b, :], ht[:, c, b * P:(b + 1) * P], wg[:, c, :],
                                           start=(c == 0 and b == 0), stop=(c == HC - 1), skip_group_check=True)
                if c == HC - 1:
                    ins.then_inc(S["l_done"], 1)

            def body(q, w, i):
                pe.wait_ge(x_in[w], (i + 1) * 16)
                pe.wait_ge(S["l_read"], q)
                for c in range(HC):
                    if c >= 4:
                        pe.wait_ge(S["gelu_done"], q * HC + c - 3)
                    for k in range(KC):
                        ins = nc.tensor.matmul(h_ps[c % 4][:], M["w1"][:, k, c * P:(c + 1) * P],
                                               x2t[:, w, :, k * P:(k + 1) * P], start=(k == 0), stop=(k == KC - 1))
                    ins.then_inc(S["h_done"], 1)
                    if c >= 2:
                        logits(q, w, c - 2)
                logits(q, w, HC - 2)
                logits(q, w, HC - 1)

            turns(pe, body)


def stage_route(nc, A, M, R):
    with ExitStack() as ctx:
        sb = lambda name, shape, dt=F32: ctx.enter_context(nc.sbuf_tensor(name, shape, dt))
        sem = lambda name: ctx.enter_context(nc.semaphore(name))
        largest = sb("r_largest", [P, NBLK])
        prob = sb("r_prob", [P, NBLK, NEXP])
        total = sb("r_total", [P, NBLK])
        number = sb("r_number", [P, NEXP])
        choice = sb("r_choice", [P, NBLK, NEXP])
        first = sb("r_first", [P, NBLK])
        node = sb("r_node", [P, NBLK])
        real = sb("r_real", [P, NBLK])
        is_exp = sb("r_is_exp", [P, NEXP, NBLK])
        before = sb("r_before", [P, NEXP, NBLK])
        running = sb("r_running", [P, NEXP, NBLK])
        tiles_i = sb("r_tiles_i", [P, NEXP], I32)
        tiles = sb("r_tiles", [P, NEXP])
        first_tile = sb("r_first_tile", [P, NEXP + 1])
        place = sb("r_place", [P, NBLK])
        place_i = sb("r_place_i", [P, NBLK], I32)
        lane_i = sb("r_lane_i", [P, NBLK], I32)
        lane_f = sb("r_lane_f", [P, NBLK])
        column = sb("r_column", [P, NBLK])
        entry = sb("r_entry", [P, NBLK, 2], I32)
        nothing = sb("r_nothing", [P, NTILE, 2], I32)
        tile_no = sb("r_tile_no", [P, NTILE])
        begun = sb("r_begun", [P, NTILE, NEXP])
        expert = sb("r_expert", [P, NTILE])
        expert_i = sb("r_expert_i", [P, NTILE], I32)
        below = sb("r_below", [P, P])
        before_ps = ctx.enter_context(nc.psum_tensor("r_before_ps", [P, NEXP, NBLK], F32))
        total_ps = ctx.enter_context(nc.psum_tensor("r_total_ps", [P, NEXP, NBLK], F32))
        names = "steps fixed shifted exp_done counted cleared placed scattered expert_ready stored below_set"
        S = {n: sem("r_" + n) for n in names.split()}
        block = ctx.enter_context(nc.Block())

        @block.sync
        def _(sp):
            sp.wait_ge(S["fixed"], 4)
            sp.dma_start(R["perm"].rearrange("(p t) c -> p (t c)", p=P), nothing[:].rearrange("p t c -> p (t c)")
                         ).then_inc(S["cleared"], 16)
            sp.wait_ge(S["expert_ready"], 1)
            sp.dma_start(R["expert"].rearrange("(a n) -> a n", a=1), expert_i[0:1, :]).then_inc(S["stored"], 16)
            sp.wait_ge(S["stored"], 16)
            sp.dma_start(M["expert"][:], R["expert"].rearrange("(a n) -> a n", a=1)).then_inc(S["stored"], 16)
            sp.wait_ge(S["stored"], 32)

        @block.gpsimd
        def _(pool):
            io = lambda out, pattern, mult, base=0: nc.gpsimd.iota(
                out, pattern=pattern, base=base, channel_multiplier=mult, allow_small_or_imprecise_dtypes=True
            ).then_inc(S["fixed"], 1)
            io(number[:], [[1, NEXP]], 0)
            io(node[:], [[P, NBLK]], 1)
            io(tile_no[:], [[1, NTILE]], 0)
            nc.gpsimd.memset(nothing[:], 1 << 20).then_inc(S["fixed"], 1)
            nc.gpsimd.affine_select(out=below[:], in_=M["ones"][:], compare_op=ALU.is_gt, fill=0.0, base=0,
                                    pattern=[[1, P]], channel_multiplier=-1).then_inc(S["below_set"], 1)
            pool.wait_ge(S["cleared"], 16)
            pool.wait_ge(S["placed"], 1)
            for b in range(RBLK):
                nc.gpsimd.indirect_dma_start(
                    out=R["perm"], out_offset=bass.IndirectOffsetOnAxis(ap=place_i[:, b:b + 1], axis=0),
                    in_=entry[:, b, :], in_offset=None, bounds_check=P * NTILE - 1, oob_is_err=False
                ).then_inc(S["scattered"], 16)
            pool.wait_ge(S["scattered"], 16 * RBLK)

        @block.scalar
        def _(act):
            act.wait_ge(S["shifted"], 1)
            nc.scalar.activation(prob[:], prob[:], ACT.Exp).then_inc(S["exp_done"], 1)

        @block.vector
        def _(dve):
            st = Steps(dve, S["steps"])

            def then(ins):
                st.mark(ins)
                st.settle()

            by_node = lambda x: x[:, :, None].broadcast_to([P, NBLK, NEXP])
            then(nc.vector.tensor_reduce(largest[:], M["logits"][:], AX_X, ALU.max))
            nc.vector.tensor_tensor(prob[:], M["logits"][:], by_node(largest), ALU.subtract).then_inc(S["shifted"], 1)
            dve.wait_ge(S["exp_done"], 1)
            dve.wait_ge(S["fixed"], 4)
            st.mark(nc.vector.tensor_reduce(total[:], prob[:], AX_X, ALU.add))
            then(nc.vector.tensor_reduce(largest[:], prob[:], AX_X, ALU.max))
            then(nc.vector.tensor_tensor(choice[:], prob[:], by_node(largest), ALU.is_equal))
            then(nc.vector.tensor_scalar(choice[:], choice[:], -float(NEXP), float(NEXP), ALU.mult, ALU.add))
            then(nc.vector.tensor_tensor(choice[:], choice[:], number[:, None, :].broadcast_to([P, NBLK, NEXP]), ALU.add))
            st.mark(nc.vector.tensor_reduce(first[:], choice[:], AX_X, ALU.min))
            st.mark(nc.vector.tensor_scalar(real[:], node[:], float(N), None, ALU.is_lt))
            then(nc.vector.reciprocal(total[:], total[:]))
            st.mark(nc.vector.tensor_tensor(entry[:, :, 1].bitcast(F32), largest[:], total[:], ALU.mult))
            st.mark(nc.vector.tensor_copy(entry[:, :, 0], node[:]))
            view = is_exp[:].rearrange("p e b -> p b e")
            then(nc.vector.tensor_tensor(view, by_node(first), number[:, None, :].broadcast_to([P, NBLK, NEXP]),
                                         ALU.is_equal))
            nc.vector.tensor_tensor(view, view, by_node(real), ALU.mult).then_inc(S["fixed"], 1)
            dve.wait_ge(S["counted"], 2)
            then(nc.vector.tensor_copy(before[:], total_ps[:]))
            for e in range(NEXP):
                st.mark(nc.vector.tensor_tensor_scan(running[:, e, :], M["ones"][:, 0:NBLK], before[:, e, :], 0.0,
                                                     ALU.mult, ALU.add))
            st.settle()
            then(nc.vector.tensor_scalar(tiles_i[:], running[:, :, NBLK - 1], float(P - 1), None, ALU.add))
            then(nc.vector.tensor_scalar(tiles_i[:], tiles_i[:], 7, None, ALU.arith_shift_right))
            st.mark(nc.vector.tensor_copy(tiles[:], tiles_i[:]))
            then(nc.vector.memset(first_tile[:, 0:1], 0.0))
            then(nc.vector.tensor_tensor_scan(first_tile[:, 1:], M["ones"][:, 0:NEXP], tiles[:], 0.0, ALU.mult, ALU.add))
            then(nc.vector.tensor_tensor(before[:], running[:], before[:], ALU.subtract))
            then(nc.vector.tensor_tensor(before[:], before[:], before_ps[:], ALU.add))
            then(nc.vector.tensor_scalar(first_tile[:], first_tile[:], float(P), None, ALU.mult))
            then(nc.vector.tensor_tensor(before[:], before[:], first_tile[:, 0:NEXP, None].broadcast_to([P, NEXP, NBLK]),
                                         ALU.add))
            then(nc.vector.tensor_tensor(before[:], before[:], is_exp[:], ALU.mult))
            then(nc.vector.tensor_reduce(place[:], before[:].rearrange("p e b -> p b e"), AX_X, ALU.add))
            then(nc.vector.tensor_copy(place_i[:], place[:]))
            then(nc.vector.tensor_scalar(lane_i[:], place_i[:], P - 1, None, ALU.bitwise_and))
            st.mark(nc.vector.tensor_copy(lane_f[:], lane_i[:]))
            then(nc.vector.tensor_scalar(place_i[:], place_i[:], 7, None, ALU.arith_shift_right))
            then(nc.vector.tensor_copy(column[:], place_i[:]))
            then(nc.vector.scalar_tensor_tensor(out=place[:], in0=lane_f[:], scalar=float(NTILE), in1=column[:],
                                                op0=ALU.mult, op1=ALU.add))
            then(nc.vector.scalar_tensor_tensor(out=real[:], in0=real[:], scalar=-1.0, in1=node[:], op0=ALU.add,
                                                op1=ALU.mult))
            then(nc.vector.scalar_tensor_tensor(out=place[:], in0=real[:], scalar=-2.0, in1=place[:], op0=ALU.mult,
                                                op1=ALU.add))
            nc.vector.tensor_copy(place_i[:], place[:]).then_inc(S["placed"], 1)
            then(nc.vector.tensor_scalar(tile_no[:], tile_no[:], float(P), None, ALU.mult))
            then(nc.vector.tensor_tensor(begun[:], first_tile[:, None, 0:NEXP].broadcast_to([P, NTILE, NEXP]),
                                         tile_no[:, :, None].broadcast_to([P, NTILE, NEXP]), ALU.is_le))
            then(nc.vector.tensor_reduce(expert[:], begun[:], AX_X, ALU.add))
            nc.vector.tensor_scalar(expert_i[:], expert[:], -1.0, None, ALU.add).then_inc(S["expert_ready"], 1)
            dve.wait_ge(S["expert_ready"], 1)

        @block.tensor
        def _(pe):
            pe.wait_ge(S["fixed"], 5)
            pe.wait_ge(S["below_set"], 1)
            flat = lambda x: x[:].rearrange("p e b -> p (e b)")
            nc.tensor.matmul(flat(before_ps), below[:], flat(is_exp), start=True, stop=True).then_inc(S["counted"], 1)
            nc.tensor.matmul(flat(total_ps), M["ones"][:], flat(is_exp), start=True, stop=True).then_inc(S["counted"], 1)


def stage_experts(nc, A, M, R, out):
    with ExitStack() as ctx:
        sb = lambda name, shape, dt=F32: ctx.enter_context(nc.sbuf_tensor(name, shape, dt))
        sem = lambda name: ctx.enter_context(nc.semaphore(name))
        entry = sb("e_entry", [P, NTILE, 2], I32)
        near = sb("e_near", [P, NTILE // QUAD + 2, QUAD], I32)
        prob = sb("e_prob", [P, NTILE])
        index = sb("e_index", [P, 2, QUAD], I32)
        to = sb("e_to", [P, 2, QUAD], I32)
        x12 = sb("e_x12", [P, 2, QUAD, 2 * C])
        x2t = sb("e_x2t", [P, 2, QUAD, KC * P])
        ht = sb("e_ht", [P, 2, HC, QUAD * P])
        y = sb("e_y", [P, QUAD, C])
        res = sb("e_res", [P, 2, QUAD, C])
        t_ps = ctx.enter_context(nc.psum_tensor("e_t_ps", [P, QUAD, KC * P], F32))
        h_ps = [ctx.enter_context(nc.psum_tensor(f"e_h_ps{b}", [P, QUAD * P], F32)) for b in range(4)]
        y_ps = ctx.enter_context(nc.psum_tensor("e_y_ps", [P, QUAD, C], F32))
        gathered = [sem(f"e_gathered{w}") for w in range(2)]
        scattered = [sem(f"e_scattered{w}") for w in range(2)]
        names = "entry_in ready to_ready index_ready turned copied h_done gelu_done y_done biased res_done"
        S = {n: sem("e_" + n) for n in names.split()}
        TURNS = NTILE // QUAD
        with nc.Block() as fresh:
            @fresh.gpsimd
            def _(pool):
                for s in (*gathered, *scattered, *S.values()):
                    pool.sem_clear(s)
        block = ctx.enter_context(nc.Block())

        @block.sync
        def _(sp):
            sp.dma_start(entry[:].rearrange("p t c -> p (t c)"), R["perm"].rearrange("(p t) c -> p (t c)", p=P)
                         ).then_inc(S["entry_in"], 16)

        @block.gpsimd
        def _(pool):
            def gather(w, n):
                pool.wait_ge(S["index_ready"], n)
                pool.nop(nofuse=True)
                for b in range(QUAD):
                    nc.gpsimd.indirect_dma_start(out=x12[:, w, b, :], out_offset=None, in_=R["x12"],
                                                 in_offset=bass.IndirectOffsetOnAxis(ap=index[:, w, b:b + 1], axis=0)
                                                 ).then_inc(gathered[w], 16)

            def scatter(w, n, done):
                pool.wait_ge(S["to_ready"], n)
                pool.wait_ge(S["res_done"], done)
                pool.nop(nofuse=True)
                for b in range(QUAD):
                    nc.gpsimd.indirect_dma_start(out=out, out_offset=bass.IndirectOffsetOnAxis(ap=to[:, w, b:b + 1], axis=0),
                                                 in_=res[:, w, b, :], in_offset=None, bounds_check=N - 1, oob_is_err=False
                                                 ).then_inc(scattered[w], 16)

            gather(0, 1)
            gather(1, 2)
            with pool.Fori(0, TURNS // 2 - 1) as i:
                for w in range(2):
                    scatter(w, i * 2 + w + 1, (i * 2 + w + 1) * QUAD)
                    gather(w, i * 2 + w + 3)
            for w in range(2):
                scatter(w, TURNS - 1 + w, (TURNS - 1 + w) * QUAD)
            for w in range(2):
                pool.wait_ge(scattered[w], 16 * QUAD * (TURNS // 2))

        @block.scalar
        def _(act):
            act.wait_ge(S["ready"], 3)
            for w in range(2):
                nc.scalar.copy(index[:, w, :], near[:, w, :]).then_inc(S["index_ready"], 1)

            with act.Fori(0, TURNS // 2) as i:
                for w in range(2):
                    n = i * 2 + w
                    act.wait_ge(S["turned"], n + 1)
                    act.nop(nofuse=True)
                    nc.scalar.copy(x2t[:, w], t_ps[:]).then_inc(S["copied"], 1)
                    for c in range(HC):
                        act.wait_ge(S["h_done"], n * HC + c + 1)
                        nc.scalar.activation(ht[:, w, c, :], h_ps[c % 4][:], ACT.Gelu, bias=M["b1"][:, c:c + 1]
                                             ).then_inc(S["gelu_done"], 1)
                    act.wait_ge(scattered[w], i * (16 * QUAD))
                    act.nop(nofuse=True)
                    nc.scalar.copy(to[:, w, :], entry[:, bass.ds(n * QUAD, QUAD), 0]).then_inc(S["to_ready"], 1)
                    act.wait_ge(gathered[w], (i + 1) * (16 * QUAD))
                    act.nop(nofuse=True)
                    nc.scalar.copy(index[:, w, :], near[:, bass.ds(n + 2, 1), :].rearrange("p a b -> p (a b)")
                                   ).then_inc(S["index_ready"], 1)

        @block.vector
        def _(dve):
            dve.wait_ge(S["entry_in"], 16)
            nc.vector.tensor_copy(prob[:], entry[:, :, 1].bitcast(F32)).then_inc(S["ready"], 1)
            nc.vector.memset(near[:], 0).then_inc(S["ready"], 1)
            dve.wait_ge(S["ready"], 2)
            nc.vector.tensor_scalar(near[:, 0:NTILE // QUAD, :], entry[:].rearrange("p (t b) c -> p t b c", b=QUAD)[:, :, :, 0],
                                    float(N - 1), None, ALU.min).then_inc(S["ready"], 1)
            dve.wait_ge(S["ready"], 3)
            at_expert = [dve.alloc_register(f"e_dve{b}") for b in range(QUAD)]
            with dve.Fori(0, TURNS // 2) as i:
                for w in range(2):
                    n = i * 2 + w
                    regs = load_row(dve, at_expert, M["expert"][0:1, bass.ds(n * QUAD, QUAD)], NEXP - 1)
                    dve.wait_ge(scattered[w], i * (16 * QUAD))
                    for b in range(QUAD):
                        t = n * QUAD + b
                        dve.wait_ge(S["y_done"], n * QUAD + b // 2 * 2 + 2)
                        dve.wait_ge(S["res_done"], n * QUAD)
                        dve.nop(nofuse=True)
                        nc.vector.tensor_tensor(y[:, b, :], y_ps[:, b, :],
                                                M["bd"][:, bass.ds(regs[b], 1), :].rearrange("p a n -> p (a n)"), ALU.add
                                                ).then_inc(S["biased"], 1)
                        dve.wait_ge(S["biased"], t + 1)
                        dve.wait_ge(gathered[w], (i + 1) * (16 * QUAD))
                        dve.nop(nofuse=True)
                        nc.vector.scalar_tensor_tensor(out=res[:, w, b, :], in0=y[:, b, :], scalar=prob[:, bass.ds(t, 1)],
                                                       in1=x12[:, w, b, 0:C], op0=ALU.mult, op1=ALU.add
                                                       ).then_inc(S["res_done"], 1)

        @block.tensor
        def _(pe):
            def turn(w, n, got):
                pe.wait_ge(gathered[w], got)
                pe.wait_ge(S["copied"], n)
                for b in range(QUAD):
                    for k in range(KC):
                        ins = nc.tensor.transpose(t_ps[:, b, k * P:(k + 1) * P], x12[:, w, b, C + k * P:C + (k + 1) * P],
                                                  M["ident"][:])
                ins.then_inc(S["turned"], 1)

            def hidden(w, n):
                pe.wait_ge(S["copied"], n + 1)
                for c in range(HC):
                    pe.wait_ge(S["gelu_done"], n * HC + max(c - 3, 0))
                    for k in range(KC):
                        ins = nc.tensor.matmul(h_ps[c % 4][:], M["w1"][:, k, c * P:(c + 1) * P],
                                               x2t[:, w, :, k * P:(k + 1) * P], start=(k == 0), stop=(k == KC - 1))
                    ins.then_inc(S["h_done"], 1)

            at_expert = [pe.alloc_register(f"e_pe{b}") for b in range(QUAD)]

            def down(w, n):
                regs = load_row(pe, at_expert, M["expert"][0:1, bass.ds(n * QUAD, QUAD)], NEXP - 1)
                pe.wait_ge(S["gelu_done"], (n + 1) * HC)
                pe.wait_ge(S["biased"], n * QUAD)
                pe.nop(nofuse=True)
                for b in range(QUAD):
                    for c in range(HC):
                        ins = nc.tensor.matmul(y_ps[:, b, :], ht[:, w, c, b * P:(b + 1) * P],
                                               M["wd"][:, bass.ds(regs[b], 1), c, :].rearrange("p a n -> p (a n)"),
                                               start=(c == 0), stop=(c == HC - 1))
                    ins.then_inc(S["y_done"], 1)

            turn(0, 0, 16 * QUAD)
            with pe.Fori(0, TURNS // 2 - 1) as i:
                for w in range(2):
                    n = i * 2 + w
                    hidden(w, n)
                    turn(1 - w, n + 1, (i + w + 1) * (16 * QUAD))
                    down(w, n)
            hidden(0, TURNS - 2)
            turn(1, TURNS - 1, (TURNS // 2) * (16 * QUAD))
            down(0, TURNS - 2)
            hidden(1, TURNS - 1)
            down(1, TURNS - 1)


def build(nc, A, out, dbg=None):
    dram = lambda name, shape, dt=F32: nc.dram_tensor(name, shape, dt).ap()
    R = {"xn": dram("xn_d", (NPAD, C)), "xnt": dram("xnt_d", (NBLK, P, KC * P)), "kv": dram("kv_d", (NPAD, 2 * C)),
         "edges": dram("edges_d", (E + P, 3), I32), "blk": dram("blk_d", (T,), I32),
         "local": dram("local_d", (TS_ROWS + 2, TS_COLS * P), BF16), "type": dram("type_d", (TS_ROWS + 2, TS_COLS * P), BF16),
         "v": dram("v_d", (TS_ROWS, P, TS_COLS * C)), "x12": dram("x12_d", (NPAD, 2 * C)),
         "x2t": dram("x2t_d", (NQ, P, QUAD * KC * P)), "perm": dram("perm_d", (P * NTILE, 2), I32),
         "expert": dram("expert_d", (NTILE,), I32)}
    with ExitStack() as ctx:
        sb = lambda name, shape, dt=F32: ctx.enter_context(nc.sbuf_tensor(name, shape, dt))
        M = {"ones": sb("ones", [P, P]), "eps": sb("eps", [P, 1]), "ident": sb("ident", [P, P]), "lane": sb("lane", [P, 1]),
             "lane64": sb("lane64", [P, 1]), "col": sb("col", [P, P]),
             "rel_12": sb("rel_12", [P, C], BF16), "rel_3": sb("rel_3", [P, C], BF16),
             "dots": sb("dots", [P, MH // 2, P]),
             "blk": sb("blk", [1, T], I32)}
        M["softmax_steps"] = 50
        with ExitStack() as edge_part:
            sbe = lambda name, shape, dt=F32: edge_part.enter_context(nc.sbuf_tensor(name, shape, dt))
            M["src"] = sbe("src", [P, TS_ROWS, TS_COLS])
            M["local"] = sbe("local", [P, TS_ROWS, TS_COLS])
            M["segment"] = sbe("segment", [TS_ROWS, TS_COLS * P])
            M["scores"] = sbe("scores", [P, TS_ROWS, TS_COLS * H])
            with ExitStack() as queries:
                M["q3"] = queries.enter_context(nc.sbuf_tensor("q3", [P, NBLK, 3, C], BF16))
                with ExitStack() as project:
                    sbp = lambda name, shape, dt=F32: project.enter_context(nc.sbuf_tensor(name, shape, dt))
                    M["wcat"] = sbp("wcat", [P, KC, WCAT])
                    M["bias"] = sbp("bias", [P, 3 * C])
                    stage_weights(nc, A, M, R)
                    stage_project(nc, A, M, R)
                stage_tiles(nc, A, M, R)
                stage_scores(nc, A, M, R)
            stage_softmax(nc, A, M, R)
            M["sums"] = sbe("sums", [P, NBLK, AGG])
            stage_aggregate(nc, A, M, R)
            M["z"] = sbe("z", [P, KC, C])
            stage_mixer(nc, A, M, R)
            stage_nodes(nc, A, M, R)
            if dbg is not None:
                dbg(nc, M, R)
        with ExitStack() as ffn:
            sbf = lambda name, shape, dt=F32: ffn.enter_context(nc.sbuf_tensor(name, shape, dt))
            M["w1"] = sbf("w1", [P, KC, HID])
            M["b1"] = sbf("b1", [P, HC])
            M["wd"] = sbf("wd", [P, NEXP, HC, C])
            M["bd"] = sbf("bd", [P, NEXP, C])
            M["logits"] = sbf("logits", [P, NBLK, NEXP])
            M["expert"] = sbf("expert", [1, NTILE], I32)
            stage_hidden(nc, A, M, R)
            stage_route(nc, A, M, R)
            stage_experts(nc, A, M, R, out)


_OUT = (N, C)


def kernel(**inputs):
    import concourse.bacc as _bacc
    from concourse.bass_utils import run_bass_kernel_spmd as _run

    arrays = {name: np.ascontiguousarray(a) for name, a in inputs.items()}
    x = np.zeros((XBLK * P, C), arrays["x"].dtype)
    x[:N] = arrays["x"]
    wqkv = arrays.pop("L0_mix_Wqkv")
    src, kind = arrays.pop("src"), arrays.pop("edge_type_64")
    arrays["x"] = x
    arrays["edges"] = np.ascontiguousarray(np.stack([src, arrays["dst"], kind], axis=1))
    arrays["mix_Wq"] = np.ascontiguousarray(wqkv[:MI])
    arrays["mix_WkvT"] = np.ascontiguousarray(wqkv[MI:].T)
    arrays["mix_WoutT"] = np.ascontiguousarray(arrays.pop("L0_mix_Wout").T)
    nc = _bacc.Bacc("TRN2", target_bir_lowering=False, num_devices=1)
    ins = {name: nc.dram_tensor(f"in_{name}", a.shape, mybir.dt.from_np(a.dtype), kind="ExternalInput").ap()
           for name, a in arrays.items()}
    out = nc.dram_tensor("out", _OUT, F32, kind="ExternalOutput").ap()
    build(nc, ins, out)
    r = _run(nc, [{f"in_{name}": a for name, a in arrays.items()}], core_ids=[0])
    return r.results[0]["out"]
```

```python
from contextlib import ExitStack

import numpy as np
import concourse.bass as bass
from concourse import mybir

F32 = mybir.dt.float32
BF16 = mybir.dt.bfloat16
I32 = mybir.dt.int32
ALU = mybir.AluOpType
ACT = mybir.ActivationFunctionType
AX_X = mybir.AxisListType.X

P = 128
C = 256
KC = C // P
N = 6250
E = 100000
QUAD = 4
NBLK = 52
NPAD = NBLK * P
XBLK = NBLK + 2
RBLK = 49
PBLK = 50
H, D = 4, 64
NREL = 64
MH, MD = 8, 64
MI = MH * MD
HID = 1024
HC = HID // P
NEXP = 8
EPS = 1e-5
WCAT = 3 * C + 2 * MI
TS_ROWS = 104
TS_COLS = 8
T = TS_ROWS * TS_COLS
EROWS, ECOLS = 125, 800
BIG = 1.0e38


class Steps:

    def __init__(self, eng, sem, base=0):
        self.eng, self.sem, self.base, self.n = eng, sem, base, 0

    def mark(self, ins):
        ins.then_inc(self.sem, 1)
        self.n += 1

    def settle(self):
        self.eng.wait_ge(self.sem, self.base + self.n)


def rows(ap, k):
    return ap.rearrange("(k p) f -> p k f", k=k)


def stage_weights(nc, A, M, R):
    with ExitStack() as ctx:
        sb = lambda name, shape, dt=F32: ctx.enter_context(nc.sbuf_tensor(name, shape, dt))
        sem = lambda name: ctx.enter_context(nc.semaphore(name))
        query = sb("query", [P, KC])
        query_all = sb("query_all", [P, KC, P])
        mean = sb("wmean", [P, KC, 2 * MH])
        bias_in = sb("bias_in", [P, 3 * C])
        rel_in = sb("rel_in", [P, D])
        rel_s = sb("rel_s", [P, D])
        rel_1 = sb("rel_p1", [P, D], BF16)
        rel_2 = sb("rel_p2", [P, D], BF16)
        rel_3 = sb("rel_p3", [P, D], BF16)
        rel_r1 = sb("rel_r1", [P, D])
        rel_r2 = sb("rel_r2", [P, D])
        bias_ps = ctx.enter_context(nc.psum_tensor("bias_ps", [P, 2, 512], F32))
        loaded, ones_set, ident_set = sem("w_loaded"), sem("w_ones"), sem("w_ident")
        query_set, bias_done, v_step = sem("w_query"), sem("w_bias"), sem("w_vstep")
        wcat, bias = M["wcat"], M["bias"]
        block = ctx.enter_context(nc.Block())
        n_loads = 9

        @block.sync
        def _(sp):
            for j, name in enumerate(("L0_gnn_Wq", "L0_gnn_Wk", "L0_gnn_Wv")):
                sp.dma_start(wcat[:, :, j * C:(j + 1) * C], rows(A[name], KC)).then_inc(loaded, 16)
            sp.dma_start(wcat[:, :, 3 * C:], rows(A["mix_WkvT"], KC)).then_inc(loaded, 16)
            for j, name in enumerate(("L0_gnn_bq", "L0_gnn_bk", "L0_gnn_bv")):
                sp.dma_start(bias_in[:, j * C:(j + 1) * C],
                             A[name].rearrange("(a n) -> a n", a=1).broadcast_to([P, C])).then_inc(loaded, 16)
            for half in range(2):
                sp.dma_start(rel_in[half * 64:half * 64 + 64, :], A["L0_gnn_rel_w"]).then_inc(loaded, 16)

        @block.scalar
        def _(act):
            act.dma_start(query[:], A["L0_gnn_query_emb"].rearrange("(k p) -> p k", k=KC),
                          allow_slow_non_contiguous=True).then_inc(query_set, 16)
            act.wait_ge(query_set, 16)

        @block.gpsimd
        def _(pool):
            nc.gpsimd.memset(M["ones"][:], 1.0).then_inc(ones_set, 1)
            nc.gpsimd.memset(M["eps"][:], EPS).then_inc(ones_set, 1)
            nc.gpsimd.memset(M["ident"][:], 0.0).then_inc(ident_set, 1)
            pool.wait_ge(ident_set, 1)
            nc.gpsimd.affine_select(out=M["ident"][:], in_=M["ident"][:], compare_op=ALU.not_equal, fill=1.0,
                                    base=0, pattern=[[-1, P]], channel_multiplier=1).then_inc(ident_set, 1)
            nc.gpsimd.iota(M["lane"][:], pattern=[[0, 1]], base=0, channel_multiplier=1,
                           allow_small_or_imprecise_dtypes=True).then_inc(ident_set, 1)
            nc.gpsimd.iota(M["col"][:], pattern=[[1, P]], base=0, channel_multiplier=0,
                           allow_small_or_imprecise_dtypes=True).then_inc(ident_set, 1)
            nc.gpsimd.iota(M["bound"][:], pattern=[[P, NBLK]], base=P, channel_multiplier=0,
                           allow_small_or_imprecise_dtypes=True).then_inc(ident_set, 1)
            pool.wait_ge(ident_set, 5)

        @block.vector
        def _(dve):
            st = Steps(dve, v_step)
            dve.wait_ge(ident_set, 4)
            st.mark(nc.vector.tensor_scalar(M["lane64"][:], M["lane"][:], 64.0, -64.0, ALU.is_ge, ALU.mult))
            st.settle()
            st.mark(nc.vector.tensor_tensor(M["lane64"][:], M["lane64"][:], M["lane"][:], ALU.add))
            dve.wait_ge(ones_set, 2)
            dve.wait_ge(query_set, 16)
            for k in range(KC):
                last = nc.vector.tensor_scalar(query_all[:, k, :], M["ones"][:], query[:, k:k + 1], 0.1,
                                               ALU.mult, ALU.mult)
                st.mark(last)
            st.settle()
            dve.wait_ge(loaded, 16 * n_loads)
            heads = wcat[:, :, 3 * C:].rearrange("p k (h d) -> p k h d", d=MD)
            st.mark(nc.vector.tensor_reduce(mean[:], heads, AX_X, ALU.add))
            st.settle()
            st.mark(nc.vector.tensor_scalar(mean[:], mean[:], 1.0 / MD, None, ALU.mult))
            st.settle()
            for k in range(KC):
                st.mark(nc.vector.tensor_tensor(heads[:, k], heads[:, k],
                                                mean[:, k, :, None].broadcast_to([P, 2 * MH, MD]), ALU.subtract))
            st.mark(nc.vector.tensor_scalar(rel_s[:], rel_in[:], 0.2, None, ALU.mult))
            st.settle()
            st.mark(nc.vector.tensor_copy(rel_1[:], rel_s[:]))
            st.settle()
            st.mark(nc.vector.tensor_tensor(rel_r1[:], rel_s[:], rel_1[:], ALU.subtract))
            st.settle()
            st.mark(nc.vector.tensor_copy(rel_2[:], rel_r1[:]))
            st.settle()
            st.mark(nc.vector.tensor_tensor(rel_r2[:], rel_r1[:], rel_2[:], ALU.subtract))
            st.settle()
            st.mark(nc.vector.tensor_copy(rel_3[:], rel_r2[:]))
            st.settle()
            for j, part in enumerate((rel_1, rel_2, rel_3)):
                st.mark(nc.vector.tensor_copy(M["rel3"][:, j, :].rearrange("p (h d) -> p h d", h=H),
                                              part[:, None, :].broadcast_to([P, H, D])))
            dve.wait_ge(bias_done, 2)
            st.mark(nc.vector.tensor_tensor(bias[:, 0:512], bias_in[:, 0:512], bias_ps[:, 0, :], ALU.add))
            st.mark(nc.vector.tensor_tensor(bias[:, 512:768], bias_in[:, 512:768], bias_ps[:, 1, 0:256], ALU.add))
            st.settle()
            st.mark(nc.vector.tensor_scalar(bias[:, 0:C], bias[:, 0:C], D ** -0.5, None, ALU.mult))
            st.settle()

        @block.tensor
        def _(pe):
            pe.wait_ge(loaded, 16 * n_loads)
            pe.wait_ge(v_step, 4)
            for b, (lo, n) in enumerate(((0, 512), (512, 256))):
                for k in range(KC):
                    last = nc.tensor.matmul(bias_ps[:, b, 0:n], query_all[:, k, :], wcat[:, k, lo:lo + n],
                                            start=(k == 0), stop=(k == KC - 1))
                last.then_inc(bias_done, 1)


def stage_project(nc, A, M, R):
    with ExitStack() as ctx:
        sb = lambda name, shape, dt=F32: ctx.enter_context(nc.sbuf_tensor(name, shape, dt))
        ps = lambda name, shape: ctx.enter_context(nc.psum_tensor(name, shape, F32))
        sem = lambda name: ctx.enter_context(nc.semaphore(name))
        x = sb("px", [P, 2, C])
        xn = sb("pxn", [P, 2, C])
        xnt = sb("pxnt", [P, 2, KC, P])
        stats = sb("pstats", [P, 6])
        mv = sb("pmv", [P, 2])
        std = sb("pstd", [P, 1])
        rstd = sb("prstd", [P, 1])
        vkv = sb("pvkv", [P, MH])
        skv = sb("pskv", [P, MH])
        qf = sb("pqf", [P, 2, C])
        qr = sb("pqr", [P, C])
        kv = sb("pkv", [P, 2, 2 * C])
        sq = sb("psq", [P, 2 * MI])
        ss = sb("pss", [P, 2 * MH])
        rr = sb("prr", [P, 2 * MH])
        rkv = sb("prkv", [P, MH])
        mks = sb("pmks", [P, 2, MI])
        mvs = sb("pmvs", [P, 2, MI])
        zero = sb("pzero", [P, MI])
        dst_i = sb("pdst_i", [EROWS, ECOLS], I32)
        dst = sb("pdst", [EROWS, ECOLS])
        below = sb("pbelow", [EROWS, ECOLS])
        t_ps = ps("pt_ps", [P, KC, P])
        qk_ps = ps("pqk_ps", [P, 512])
        v_ps = ps("pv_ps", [P, C])
        mk_ps = ps("pmk_ps", [P, MI])
        mv_ps = ps("pmv_ps", [P, MI])
        dots_ps = ps("pdots_ps", [P, MH // 2, P])
        x_in = [sem(f"x_in{u}") for u in range(2)]
        xn_out = [sem(f"xn_out{u}") for u in range(2)]
        xnt_out = [sem(f"xnt_out{u}") for u in range(2)]
        kv_out = [sem(f"kv_out{u}") for u in range(2)]
        names = ("zeroed xn_ready xnt_ready turned qk_done v_done mk_done mv_done qf_used k_read kv_ready "
                 "mks_ready mvs_ready sq_ready sq_used dots_done v_step p_step qf_ready dots_read "
                 "mv_ready std_ready rstd_ready vkv_ready skv_ready dst_in rest_in")
        S = {n: sem("p_" + n) for n in names.split()}
        wcat, bias, q3 = M["wcat"], M["bias"], M["q3"]
        x_d = A["x"].rearrange("(b p) c -> b p c", p=P)
        xn_d = R["xn"].rearrange("(b p) c -> b p c", p=P)
        kv_d = R["kv"].rearrange("(b p) c -> b p c", p=P)
        block = ctx.enter_context(nc.Block())
        TURNS = PBLK // 2

        @block.sync
        def _(sp):
            for u in range(2):
                sp.dma_start(x[:, u, :], x_d[u]).then_inc(x_in[u], 16)
            sp.dma_start(dst_i[:], A["dst"].rearrange("(p k) -> p k", p=EROWS)).then_inc(S["dst_in"], 16)
            blank = A["x"][PBLK * P:NPAD, :]
            sp.dma_start(R["xn"][PBLK * P:, :], blank).then_inc(S["rest_in"], 16)
            sp.dma_start(R["kv"][PBLK * P:, 0:C], blank).then_inc(S["rest_in"], 16)
            sp.dma_start(R["kv"][PBLK * P:, C:], blank).then_inc(S["rest_in"], 16)
            sp.dma_start(R["xnt"][PBLK:].rearrange("b p n -> (b p) n"), blank).then_inc(S["rest_in"], 16)
            with sp.Fori(0, TURNS) as i:
                for u in range(2):
                    g = i * 2 + u
                    sp.wait_ge(S["xn_ready"], g + 1)
                    sp.nop(nofuse=True)
                    sp.dma_start(x[:, u, :], x_d[bass.ds(g + 2, 1)].rearrange("a p c -> (a p) c")).then_inc(x_in[u], 16)
                    sp.dma_start(xn_d[bass.ds(g, 1)].rearrange("a p c -> (a p) c"), xn[:, u, :]).then_inc(xn_out[u], 16)
                    sp.wait_ge(S["xnt_ready"], g + 1)
                    sp.nop(nofuse=True)
                    sp.dma_start(R["xnt"][bass.ds(g, 1)].rearrange("a p c -> (a p) c"),
                                 xnt[:, u].rearrange("p k n -> p (k n)")).then_inc(xnt_out[u], 16)
                    sp.wait_ge(S["kv_ready"], g + 1)
                    sp.nop(nofuse=True)
                    sp.dma_start(kv_d[bass.ds(g, 1)].rearrange("a p c -> (a p) c"), kv[:, u, :]).then_inc(kv_out[u], 16)
            sp.wait_ge(S["rest_in"], 16 * 4)
            for u in range(2):
                sp.wait_ge(xn_out[u], 16 * TURNS)
                sp.wait_ge(xnt_out[u], 16 * TURNS)
                sp.wait_ge(kv_out[u], 16 * TURNS)
                sp.wait_ge(x_in[u], 16 * (TURNS + 1))

        @block.vector
        def _(dve):
            nc.vector.memset(zero[:], 0.0).then_inc(S["zeroed"], 1)
            nc.vector.memset(mks[:, 1, :], 0.0).then_inc(S["zeroed"], 1)
            nc.vector.memset(mvs[:, 1, :], 0.0).then_inc(S["zeroed"], 1)

            def normalise(st, w, n):
                dve.wait_ge(S["xn_ready"], n)
                st.mark(nc.vector.bn_stats(stats[:], x[:, w, :]))
                st.settle()
                dve.nop(nofuse=True)
                nc.vector.bn_aggr(mv[:], stats[:]).then_inc(S["mv_ready"], 1)
                dve.wait_ge(S["std_ready"], n + 1)
                nc.vector.reciprocal(rstd[:], std[:]).then_inc(S["rstd_ready"], 1)
                dve.wait_ge(S["rstd_ready"], n + 1)
                nc.vector.tensor_scalar(xn[:, w, :], x[:, w, :], mv[:, 0:1], rstd[:], ALU.subtract,
                                        ALU.mult).then_inc(S["xn_ready"], 1)

            first = Steps(dve, S["v_step"])
            for w in range(2):
                dve.wait_ge(x_in[w], 16)
                normalise(first, w, w)
            dve.wait_ge(S["dst_in"], 16)
            first.mark(nc.vector.tensor_copy(dst[:], dst_i[:]))
            first.settle()
            PER = 4
            squares = lambda t, k: t[:, k * MH:(k + 1) * MH]
            with dve.Fori(0, TURNS) as i:
                for u in range(2):
                    g = i * 2 + u
                    st = Steps(dve, S["v_step"], g * PER + first.n)
                    dve.wait_ge(S["qk_done"], g + 1)
                    dve.wait_ge(S["qf_used"], g + 1)
                    nc.vector.scalar_tensor_tensor(out=qf[:, u, :], in0=qk_ps[:, 0:C], scalar=D ** -0.5,
                                                   in1=bias[:, 0:C], op0=ALU.mult, op1=ALU.add
                                                   ).then_inc(S["qf_ready"], 1)
                    dve.wait_ge(kv_out[u], i * 16)
                    nc.vector.tensor_tensor(kv[:, u, 0:C], qk_ps[:, C:2 * C], bias[:, C:2 * C],
                                            ALU.add).then_inc(S["k_read"], 1)
                    dve.wait_ge(S["v_done"], g + 1)
                    dve.wait_ge(S["k_read"], g + 1)
                    nc.vector.tensor_tensor(kv[:, u, C:], v_ps[:], bias[:, 2 * C:], ALU.add).then_inc(S["kv_ready"], 1)
                    dve.wait_ge(x_in[u], (i + 2) * 16)
                    dve.wait_ge(S["turned"], g + 1)
                    dve.wait_ge(xn_out[u], (i + 1) * 16)
                    normalise(st, u, g + 2)
                    st.mark(nc.vector.tensor_scalar(below[:], dst[:], M["bound"][0:EROWS, bass.ds(g, 1)], 0.0, ALU.is_lt,
                                                    ALU.add, accum_out=M["count"][:, bass.ds(g, 1)]))
                    for k in range(2):
                        dve.wait_ge(S["sq_ready"], g * 2 + k + 1)
                        ins = nc.vector.tensor_reduce(squares(ss, k), sq[:, k * MI:(k + 1) * MI]
                                                      .rearrange("p (h d) -> p h d", d=MD), AX_X, ALU.add)
                    st.mark(ins)
                    st.settle()
                    nc.vector.tensor_scalar(rr[:], ss[:], 1.0 / MD, EPS, ALU.mult, ALU.add).then_inc(S["sq_used"], 1)
                    dve.wait_ge(S["sq_used"], g + 1)
                    nc.vector.tensor_tensor(vkv[:], rr[:, 0:MH], rr[:, MH:], ALU.mult).then_inc(S["vkv_ready"], 1)
                    dve.wait_ge(S["skv_ready"], g + 1)
                    st.mark(nc.vector.reciprocal(rkv[:], skv[:]))
                    st.settle()
                    dve.wait_ge(S["dots_done"], g)
                    nc.vector.tensor_tensor(mks[:, u, :].rearrange("p (h d) -> p h d", d=MD),
                                            mk_ps[:].rearrange("p (h d) -> p h d", d=MD),
                                            rkv[:, :, None].broadcast_to([P, MH, MD]), ALU.mult
                                            ).then_inc(S["mks_ready"], 1)
                    assert st.n == PER
            dve.wait_ge(S["dots_done"], PBLK + 1)
            nc.vector.tensor_copy(M["dots"][:], dots_ps[:]).then_inc(S["dots_read"], 1)
            dve.wait_ge(S["dots_read"], 1)

        @block.gpsimd
        def _(pool):
            nc.gpsimd.memset(qr[:], 0.0).then_inc(S["qf_used"], 2)
            pool.wait_ge(S["qf_used"], 2)
            PER = 3
            with pool.Fori(0, TURNS) as i:
                for u in range(2):
                    g = i * 2 + u
                    st = Steps(pool, S["p_step"], g * PER)
                    part = lambda j: q3[:, bass.ds(g, 1), j, :].rearrange("p a c -> p (a c)")
                    pool.wait_ge(S["qf_ready"], g + 1)
                    pool.nop(nofuse=True)
                    st.mark(nc.gpsimd.tensor_copy(part(0), qf[:, u, :]))
                    st.settle()
                    pool.nop(nofuse=True)
                    st.mark(nc.gpsimd.tensor_tensor(qr[:], qf[:, u, :], part(0), ALU.subtract))
                    st.settle()
                    pool.nop(nofuse=True)
                    st.mark(nc.gpsimd.tensor_copy(part(1), qr[:]))
                    st.settle()
                    pool.nop(nofuse=True)
                    nc.gpsimd.tensor_tensor(part(2), qr[:], part(1), ALU.subtract).then_inc(S["qf_used"], 1)
                    pool.wait_ge(S["qf_used"], g + 3)
                    assert st.n == PER

        @block.scalar
        def _(act):
            def deviation(n):
                act.wait_ge(S["mv_ready"], n + 1)
                act.wait_ge(S["rstd_ready"], n)
                nc.scalar.activation(std[:], mv[:, 1:2], ACT.Sqrt, bias=M["eps"][:]).then_inc(S["std_ready"], 1)

            def turned_copy(w):
                nc.scalar.copy(xnt[:, w].rearrange("p k n -> p (k n)"),
                               t_ps[:].rearrange("p k n -> p (k n)")).then_inc(S["xnt_ready"], 1)

            deviation(0)
            deviation(1)
            act.wait_ge(S["turned"], 1)
            turned_copy(0)
            with act.Fori(0, TURNS) as i:
                for u in range(2):
                    g = i * 2 + u
                    act.wait_ge(S["turned"], g + 2)
                    act.wait_ge(S["mv_done"], g)
                    act.wait_ge(xnt_out[1 - u], (i + u) * 16)
                    turned_copy(1 - u)
                    deviation(g + 2)
                    act.wait_ge(S["mk_done"], g + 1)
                    act.wait_ge(S["sq_used"], g)
                    nc.scalar.activation(sq[:, 0:MI], mk_ps[:], ACT.Square).then_inc(S["sq_ready"], 1)
                    act.wait_ge(S["mv_done"], g + 1)
                    nc.scalar.activation(sq[:, MI:], mv_ps[:], ACT.Square).then_inc(S["sq_ready"], 1)
                    act.wait_ge(S["dots_done"], g)
                    nc.scalar.copy(mvs[:, u, :], mv_ps[:]).then_inc(S["mvs_ready"], 1)
                    act.wait_ge(S["vkv_ready"], g + 1)
                    nc.scalar.activation(skv[:], vkv[:], ACT.Sqrt).then_inc(S["skv_ready"], 1)

        @block.tensor
        def _(pe):
            def dots(w, last=False):
                for j in range(MH // 2):
                    pair = slice(j * P, (j + 1) * P)
                    ins = nc.tensor.matmul(dots_ps[:, j, :], mvs[:, w, pair], mks[:, w, pair],
                                           start=False, stop=last, skip_group_check=True)
                ins.then_inc(S["dots_done"], 1)

            pe.wait_ge(S["zeroed"], 3)
            nc.tensor.matmul(dots_ps[:].rearrange("p j n -> p (j n)"), zero[:, 0:P], zero[:], start=True, stop=False,
                             skip_group_check=True)

            def turn(w, n):
                pe.wait_ge(S["xn_ready"], n + 1)
                pe.wait_ge(S["xnt_ready"], n)
                for k in range(KC):
                    ins = nc.tensor.transpose(t_ps[:, k, :], xn[:, w, k * P:(k + 1) * P], M["ident"][:])
                ins.then_inc(S["turned"], 1)

            def product(w, g, out, lo, n, free, done):
                pe.wait_ge(S[free], g)
                for k in range(KC):
                    ins = nc.tensor.matmul(out[:], xnt[:, w, k, :], wcat[:, k, lo:lo + n],
                                           start=(k == 0), stop=(k == KC - 1))
                ins.then_inc(S[done], 1)

            pe.wait_ge(S["xn_ready"], 1)
            for k in range(KC):
                ins = nc.tensor.transpose(t_ps[:, k, :], xn[:, 0, k * P:(k + 1) * P], M["ident"][:])
            ins.then_inc(S["turned"], 1)
            with pe.Fori(0, TURNS) as i:
                for u in range(2):
                    g = i * 2 + u
                    pe.wait_ge(S["xnt_ready"], g + 1)
                    product(u, g, qk_ps, 0, 512, "k_read", "qk_done")
                    product(u, g, v_ps, 512, 256, "kv_ready", "v_done")
                    turn(1 - u, g + 1)
                    pe.wait_ge(S["mks_ready"], g)
                    pe.wait_ge(S["mvs_ready"], g)
                    dots(1 - u)
                    product(u, g, mk_ps, 768, 512, "mks_ready", "mk_done")
                    product(u, g, mv_ps, 1280, 512, "mvs_ready", "mv_done")
            pe.wait_ge(S["mks_ready"], PBLK)
            pe.wait_ge(S["mvs_ready"], PBLK)
            dots(1, last=True)


def stage_tiles(nc, A, M, R):
    with ExitStack() as ctx:
        sb = lambda name, shape, dt=F32: ctx.enter_context(nc.sbuf_tensor(name, shape, dt))
        sem = lambda name: ctx.enter_context(nc.semaphore(name))
        first_edge = sb("t_first_edge", [P, RBLK + 1])
        room = sb("t_room", [P, RBLK])
        room_i = sb("t_room_i", [P, RBLK], I32)
        tiles = sb("t_tiles", [P, RBLK])
        first_tile = sb("t_first_tile", [P, RBLK + 1])
        offset = sb("t_offset", [P, RBLK])
        delta = sb("t_delta", [P, RBLK])
        number = sb("t_number", [TS_ROWS, TS_COLS])
        begun = sb("t_begun", [TS_ROWS, TS_COLS, RBLK])
        begun_off = sb("t_begun_off", [TS_ROWS, TS_COLS, RBLK])
        blk = sb("t_blk", [TS_ROWS, TS_COLS])
        base = sb("t_base", [TS_ROWS, TS_COLS])
        start = sb("t_start", [TS_ROWS, TS_COLS])
        blk_i = sb("t_blk_i", [TS_ROWS, TS_COLS], I32)
        start_i = sb("t_start_i", [TS_ROWS, TS_COLS], I32)
        meta = sb("t_meta", [TS_ROWS, TS_COLS, 3 * P], I32)
        src_f = sb("t_src_f", [TS_ROWS, TS_COLS, P])
        dst_f = sb("t_dst_f", [TS_ROWS, TS_COLS, P])
        local = sb("t_local", [TS_ROWS, TS_COLS, P])
        valid = sb("t_valid", [TS_ROWS, TS_COLS, P])
        low = sb("t_low", [TS_ROWS, TS_COLS, P])
        local_b = sb("t_local_b", [TS_ROWS, TS_COLS * P], BF16)
        type_b = sb("t_type_b", [TS_ROWS, TS_COLS * P], BF16)
        total_ps = ctx.enter_context(nc.psum_tensor("t_total_ps", [P, RBLK], F32))
        turn_ps = [ctx.enter_context(nc.psum_tensor(f"t_turn_ps{b}", [P, 4, P], F32)) for b in range(4)]
        names = "counted totals number_set placed gathered stored steps turned back table_in"
        S = {n: sem("t_" + n) for n in names.split()}
        block = ctx.enter_context(nc.Block())

        @block.sync
        def _(sp):
            sp.wait_ge(S["placed"], 1)
            sp.dma_start(R["blk"].rearrange("(p k) -> p k", p=TS_ROWS), blk_i[:]).then_inc(S["stored"], 16)
            sp.wait_ge(S["stored"], 16)
            sp.dma_start(M["blk"][:], R["blk"].rearrange("(a n) -> a n", a=1)).then_inc(S["table_in"], 16)
            sp.wait_ge(S["back"], 1)
            sp.dma_start(R["local"][0:TS_ROWS, :], local_b[:]).then_inc(S["stored"], 16)
            sp.dma_start(R["type"][0:TS_ROWS, :], type_b[:]).then_inc(S["stored"], 16)
            sp.wait_ge(S["stored"], 48)
            sp.dma_start(R["local"][TS_ROWS:, :], local_b[0:2, :]).then_inc(S["stored"], 16)
            sp.dma_start(R["type"][TS_ROWS:, :], type_b[0:2, :]).then_inc(S["stored"], 16)
            sp.wait_ge(S["stored"], 80)
            sp.wait_ge(S["table_in"], 16)

        @block.gpsimd
        def _(pool):
            nc.gpsimd.iota(number[:], pattern=[[1, TS_COLS]], base=0, channel_multiplier=TS_COLS,
                           allow_small_or_imprecise_dtypes=True).then_inc(S["number_set"], 1)
            pool.wait_ge(S["placed"], 2)
            for j in range(TS_COLS):
                nc.gpsimd.indirect_dma_start(out=meta[:, j, :], out_offset=None, in_=A["edges"],
                                             in_offset=bass.IndirectOffsetOnAxis(ap=start_i[:, j:j + 1], axis=0)
                                             ).then_inc(S["gathered"], 16)

        @block.vector
        def _(dve):
            st = Steps(dve, S["steps"])

            def then(ins):
                st.mark(ins)
                st.settle()

            nc.vector.memset(first_edge[:, 0:1], 0.0).then_inc(S["counted"], 1)
            nc.vector.memset(first_tile[:, 0:1], 0.0).then_inc(S["counted"], 1)
            dve.wait_ge(S["totals"], 1)
            then(nc.vector.tensor_copy(first_edge[:, 1:], total_ps[:]))
            then(nc.vector.tensor_tensor(room[:], first_edge[:, 1:], first_edge[:, 0:RBLK], ALU.subtract))
            then(nc.vector.tensor_scalar(room_i[:], room[:], float(P - 1), None, ALU.add))
            then(nc.vector.tensor_scalar(room_i[:], room_i[:], 7, None, ALU.arith_shift_right))
            then(nc.vector.tensor_scalar(tiles[:], room_i[:], 1.0, None, ALU.max))
            then(nc.vector.tensor_tensor_scan(first_tile[:, 1:], M["ones"][:, 0:RBLK], tiles[:], 0.0, ALU.mult, ALU.add))
            then(nc.vector.scalar_tensor_tensor(out=offset[:], in0=first_tile[:, 0:RBLK], scalar=-float(P),
                                                in1=first_edge[:, 0:RBLK], op0=ALU.mult, op1=ALU.add))
            st.mark(nc.vector.tensor_copy(delta[:, 0:1], offset[:, 0:1]))
            then(nc.vector.tensor_tensor(delta[:, 1:], offset[:, 1:], offset[:, 0:RBLK - 1], ALU.subtract))
            dve.wait_ge(S["number_set"], 1)
            over_tiles = lambda x: x[0:TS_ROWS, None, 0:RBLK].broadcast_to([TS_ROWS, TS_COLS, RBLK])
            then(nc.vector.tensor_tensor(begun[:], over_tiles(first_tile),
                                         number[:, :, None].broadcast_to([TS_ROWS, TS_COLS, RBLK]), ALU.is_le))
            st.mark(nc.vector.tensor_reduce(blk[:], begun[:], AX_X, ALU.add))
            then(nc.vector.tensor_tensor(begun_off[:], begun[:], over_tiles(delta), ALU.mult))
            then(nc.vector.tensor_reduce(base[:], begun_off[:], AX_X, ALU.add))
            st.mark(nc.vector.tensor_scalar(blk[:], blk[:], -1.0, None, ALU.add))
            then(nc.vector.scalar_tensor_tensor(out=start[:], in0=number[:], scalar=float(P), in1=base[:],
                                                op0=ALU.mult, op1=ALU.add))
            nc.vector.tensor_copy(blk_i[:], blk[:]).then_inc(S["placed"], 1)
            nc.vector.tensor_scalar(start_i[:], start[:], float(E), None, ALU.min).then_inc(S["placed"], 1)
            dve.wait_ge(S["gathered"], 16 * TS_COLS)
            field = lambda k: meta[:].rearrange("p t (e c) -> p t e c", c=3)[:, :, :, k]
            by_tile = lambda x: x[:].rearrange("p (t e) -> p t e", e=P)
            wide = lambda x: x[:, :, None].broadcast_to([TS_ROWS, TS_COLS, P])
            st.mark(nc.vector.tensor_scalar(src_f[:], field(0), 0.0, None, ALU.max))
            st.mark(nc.vector.tensor_copy(by_tile(type_b), field(2)))
            then(nc.vector.tensor_copy(dst_f[:], field(1)))
            st.mark(nc.vector.tensor_scalar(blk[:], blk[:], float(P), None, ALU.mult))
            st.settle()
            then(nc.vector.tensor_tensor(local[:], dst_f[:], wide(blk), ALU.subtract))
            then(nc.vector.tensor_scalar(low[:], local[:], float(P), None, ALU.is_lt))
            then(nc.vector.scalar_tensor_tensor(out=valid[:], in0=local[:], scalar=0.0, in1=low[:],
                                                op0=ALU.is_ge, op1=ALU.mult))
            then(nc.vector.scalar_tensor_tensor(out=dst_f[:], in0=dst_f[:], scalar=1.0, in1=valid[:],
                                                op0=ALU.add, op1=ALU.mult))
            then(nc.vector.tensor_scalar(by_tile(M["segment"]), dst_f[:], -1.0, None, ALU.add))
            nc.vector.tensor_copy(by_tile(local_b), local[:]).then_inc(S["back"], 1)
            for b in range(4):
                dve.wait_ge(S["turned"], b + 1)
                to = (M["src"] if b < 2 else M["local"])[:, 0:TS_ROWS, :].rearrange("p r c -> p c r")
                c = 4 * (b % 2)
                nc.vector.tensor_copy(to[:, c:c + 4, :], turn_ps[b][:, :, 0:TS_ROWS]).then_inc(S["back"], 1)
            nc.vector.memset(M["src"][:, TS_ROWS:, :], 0.0).then_inc(S["back"], 1)
            dve.wait_ge(S["back"], 6)

        @block.tensor
        def _(pe):
            nc.tensor.matmul(total_ps[:], M["ones"][0:EROWS, :], M["count"][:, 0:RBLK], start=True, stop=True).then_inc(S["totals"], 1)
            pe.wait_ge(S["back"], 1)
            for b in range(4):
                x = src_f if b < 2 else local
                for c in range(4):
                    ins = nc.tensor.transpose(turn_ps[b][:, c, 0:TS_ROWS], x[:, 4 * (b % 2) + c, :],
                                              M["ident"][0:TS_ROWS, 0:TS_ROWS])
                ins.then_inc(S["turned"], 1)


SLOTS = 16
HALF = SLOTS // 2
GROUPS = 4
GROUP = SLOTS // GROUPS
TURNS_E = T // SLOTS


def stage_scores(nc, A, M, R):
    with ExitStack() as ctx:
        sb = lambda name, shape, dt=F32: ctx.enter_context(nc.sbuf_tensor(name, shape, dt))
        sem = lambda name: ctx.enter_context(nc.semaphore(name))
        kv = sb("s_kv", [P, SLOTS, 2 * C])
        index = sb("s_index", [P, GROUPS, GROUP], I32)
        local = sb("s_local", [P, 2, HALF * P], BF16)
        kind = sb("s_kind", [P, 2, GROUP * P], BF16)
        is_dst = sb("s_is_dst", [P, 2, HALF * P], BF16)
        is_kind = sb("s_is_kind", [P, 2, GROUP * P], BF16)
        key = sb("s_key", [P, 2, GROUP, C])
        part = sb("s_part", [P, 2, HALF, H])
        qr_ps = [ctx.enter_context(nc.psum_tensor(f"s_qr_ps{b}", [P, GROUP, 2, C], F32)) for b in range(2)]
        gathered = [sem(f"s_gathered{g}") for g in range(GROUPS)]
        rows_in = [sem(f"s_rows_in{h}") for h in range(2)]
        v_out = [sem(f"s_v_out{g}") for g in range(GROUPS - 1)]
        names = "index_ready key_added onehot_ready qr_done qr_free reduced part_used steps"
        S = {n: sem("s_" + n) for n in names.split()}
        row = lambda ap, n: ap[bass.ds(n, 1), :].broadcast_to([P, HALF * P])
        block = ctx.enter_context(nc.Block())

        @block.sync
        def _(sp):
            def rows_of(h, n):
                sp.dma_start(local[:, h, :], row(R["local"], n)).then_inc(rows_in[h], 16)
                for k in range(2):
                    sp.dma_start(kind[k * NREL:(k + 1) * NREL, h, :],
                                 R["type"][bass.ds(n, 1), k * GROUP * P:(k + 1) * GROUP * P]
                                 .broadcast_to([NREL, GROUP * P])).then_inc(rows_in[h], 16)

            for h in range(2):
                rows_of(h, h)
            with sp.Fori(0, TURNS_E) as i:
                for h in range(2):
                    sp.wait_ge(S["onehot_ready"], i * 2 + h + 1)
                    sp.nop(nofuse=True)
                    rows_of(h, i * 2 + h + 2)
                    for g in (2 * h, 2 * h + 1):
                        if g == GROUPS - 1:
                            continue
                        sp.wait_ge(gathered[g], (i + 1) * (16 * GROUP))
                        sp.nop(nofuse=True)
                        sp.dma_start(R["v"][bass.ds(i * 2 + h, 1)].rearrange("a p n -> (a p) n")
                                     .rearrange("p (j c) -> p j c", c=C)[:, g % 2 * GROUP:(g % 2 + 1) * GROUP, :],
                                     kv[:, g * GROUP:(g + 1) * GROUP, C:]).then_inc(v_out[g], 16)
            for h in range(2):
                sp.wait_ge(rows_in[h], 48 * (TURNS_E + 1))
            for g in range(GROUPS - 1):
                sp.wait_ge(v_out[g], 16 * TURNS_E)

        @block.scalar
        def _(act):
            def indices(g, turn):
                nc.scalar.activation(index[:, g, :], M["src"][:, bass.ds(turn * 2 + g // 2, 1), :]
                                     .rearrange("p a c -> p (a c)")[:, g % 2 * GROUP:(g % 2 + 1) * GROUP],
                                     ACT.Copy, scale=2.0 if g == GROUPS - 1 else 1.0).then_inc(S["index_ready"], 1)

            def scores(h, i):
                act.wait_ge(S["reduced"], i * GROUPS + 2 * (h + 1))
                act.nop(nofuse=True)
                nc.scalar.copy(M["scores"][:, bass.ds(i * 2 + h, 1), :].rearrange("p a c -> p (a c)"),
                               part[:, h].rearrange("p u h -> p (u h)")).then_inc(S["part_used"], 1)

            for g in range(GROUPS):
                indices(g, 0)
            with act.Fori(0, TURNS_E - 1) as i:
                for g in range(GROUPS):
                    act.wait_ge(gathered[g], (i + 1) * (16 * GROUP))
                    act.nop(nofuse=True)
                    indices(g, i + 1)
                for h in range(2):
                    scores(h, i)
            for h in range(2):
                scores(h, TURNS_E - 1)
            act.wait_ge(S["part_used"], 2 * TURNS_E)

        @block.gpsimd
        def _(pool):
            with pool.Fori(0, TURNS_E) as i:
                for g in range(GROUPS):
                    pool.wait_ge(S["index_ready"], i * GROUPS + g + 1)
                    if g < GROUPS - 1:
                        pool.wait_ge(v_out[g], i * 16)
                    pool.wait_ge(S["key_added"], i * GROUPS + g + 1)
                    pool.nop(nofuse=True)
                    for b in range(GROUP):
                        last = g == GROUPS - 1
                        nc.gpsimd.indirect_dma_start(out=kv[:, g * GROUP + b, 0:C if last else 2 * C], out_offset=None,
                                                     in_=R["kv"].rearrange("n (a c) -> (n a) c", a=2) if last else R["kv"],
                                                     in_offset=bass.IndirectOffsetOnAxis(ap=index[:, g, b:b + 1], axis=0)
                                                     ).then_inc(gathered[g], 16)

        @block.vector
        def _(dve):
            def onehots(h, n):
                dve.wait_ge(rows_in[h], n)
                nc.vector.tensor_scalar(is_dst[:, h, :], local[:, h, :], M["lane"][:], None, ALU.is_equal)\
                  .then_inc(S["steps"], 1)
                nc.vector.tensor_scalar(is_kind[:, h, :], kind[:, h, :], M["lane64"][:], None, ALU.is_equal)\
                  .then_inc(S["onehot_ready"], 1)

            nc.vector.memset(key[:, 0, 0, 0:1], 0.0).then_inc(S["key_added"], GROUPS)
            nc.vector.memset(key[:, 1, 0, 0:1], 0.0).then_inc(S["qr_free"], 2)
            dve.wait_ge(S["key_added"], GROUPS)
            dve.wait_ge(S["qr_free"], 2)
            onehots(0, 48)
            with dve.Fori(0, TURNS_E) as i:
                for h in range(2):
                    onehots(1 - h, (i + h + 1) * 48)
                    for g in (2 * h, 2 * h + 1):
                        n, b = i * GROUPS + g, g % 2
                        dve.wait_ge(S["qr_done"], n + 1)
                        dve.wait_ge(gathered[g], (i + 1) * (16 * GROUP))
                        if g >= 2:
                            dve.wait_ge(S["reduced"], n - 1)
                        else:
                            dve.wait_ge(S["qr_free"], n + 2)
                        nc.vector.tensor_tensor(key[:, b], kv[:, g * GROUP:(g + 1) * GROUP, 0:C], qr_ps[b][:, :, 1, :],
                                                ALU.add).then_inc(S["key_added"], 1)
                        dve.wait_ge(S["key_added"], n + 1 + GROUPS)
                        nc.vector.tensor_tensor(key[:, b], key[:, b], qr_ps[b][:, :, 0, :], ALU.mult
                                                ).then_inc(S["qr_free"], 1)
                        dve.wait_ge(S["part_used"], i * 2)
                        dve.wait_ge(S["qr_free"], n + 3)
                        nc.vector.tensor_reduce(part[:, h, b * GROUP:(b + 1) * GROUP, :].rearrange("p u h -> p (u h)"),
                                                key[:, b].rearrange("p u (h d) -> p (u h) d", d=D), AX_X, ALU.add
                                                ).then_inc(S["reduced"], 1)

        @block.tensor
        def _(pe):
            at_block = [pe.alloc_register(f"s_at{u}") for u in range(SLOTS)]
            with pe.Fori(0, TURNS_E) as i:
                regs = load_row(pe, at_block, M["blk"][0:1, bass.ds(i * SLOTS, SLOTS)], RBLK - 1)
                for g in range(GROUPS):
                    h, b = g // 2, g % 2
                    if b == 0:
                        pe.wait_ge(S["onehot_ready"], i * 2 + h + 1)
                    pe.wait_ge(S["qr_free"], i * GROUPS + g + 1)
                    pe.nop(nofuse=True)
                    for u in range(GROUP):
                        e = slice((b * GROUP + u) * P, (b * GROUP + u + 1) * P)
                        for j in range(3):
                            nc.tensor.matmul(qr_ps[b][:, u, 0, :], is_dst[:, h, e],
                                             M["q3"][:, bass.ds(regs[g * GROUP + u], 1), j, :]
                                             .rearrange("p a c -> p (a c)"), start=(j == 0), stop=(j == 2))
                        half = slice(b * NREL, (b + 1) * NREL)
                        for j in range(3):
                            ins = nc.tensor.matmul(qr_ps[b][:, u, 1, :], is_kind[half, h, u * P:(u + 1) * P],
                                                   M["rel3"][half, j, :], start=(j == 0), stop=(j == 2))
                    ins.then_inc(S["qr_done"], 1)


def stage_softmax(nc, A, M, R):
    with ExitStack() as ctx:
        sb = lambda name, shape, dt=F32: ctx.enter_context(nc.sbuf_tensor(name, shape, dt))
        sem = lambda name: ctx.enter_context(nc.semaphore(name))
        W = TS_COLS * P
        score = sb("m_score", [TS_ROWS, H, W])
        most = sb("m_most", [TS_ROWS, H, W])
        new = sb("m_new", [TS_ROWS, W + 1])
        in_first = sb("m_in_first", [TS_ROWS, W])
        in_last = sb("m_in_last", [TS_ROWS, W])
        ends = sb("m_ends", [TS_ROWS, 4, H])
        ends_t = sb("m_ends_t", [H, 4, TS_ROWS])
        link = sb("m_link", [H, TS_ROWS + 1])
        whole = sb("m_whole", [H, TS_ROWS])
        gate_f = sb("m_gate_f", [H, TS_ROWS])
        gate_b = sb("m_gate_b", [H, TS_ROWS])
        run_f = sb("m_run_f", [H, TS_ROWS])
        run_b = sb("m_run_b", [H, TS_ROWS])
        carry = sb("m_carry", [H, 2, TS_ROWS])
        carry_t = sb("m_carry_t", [TS_ROWS, 2, H])
        bank = [ctx.enter_context(nc.psum_tensor(f"m_bank{b}", [P, 4, P], F32)) for b in range(4)]
        small = ctx.enter_context(nc.psum_tensor("m_small", [P, 4, P], F32))
        wout = sb("x_wout", [P, MH // 2, C])
        wq = sb("x_wq", [P, MH // 2, C])
        pairs = sb("x_pairs", [P, MH // 2, P])
        vw = sb("x_vw", [P, MH // 2, C])
        vw_ps = ctx.enter_context(nc.psum_tensor("x_vw_ps", [P, MH // 2, C], F32))
        z_ps = ctx.enter_context(nc.psum_tensor("x_z_ps", [P, KC, C], F32))
        names = "mix_in zeroed paired vw_done vw_copied z_done z_read steps turned copied ends_turned ends_ready carry_turned exp_ready back_turned back"
        S = {n: sem("m_" + n) for n in names.split()}
        seg = M["segment"]
        n_bank = 2 * H
        block = ctx.enter_context(nc.Block())

        @block.sync
        def _(sp):
            sp.dma_start(wout[:], rows(A["mix_WoutT"], MH // 2)).then_inc(S["mix_in"], 16)
            sp.dma_start(wq[:], rows(A["mix_Wq"], MH // 2)).then_inc(S["mix_in"], 16)

        @block.gpsimd
        def _(pool):
            nc.gpsimd.memset(pairs[:], 0.0).then_inc(S["zeroed"], 1)
            pool.wait_ge(S["zeroed"], 1)
            for half in (slice(0, MD), slice(MD, 2 * MD)):
                nc.gpsimd.tensor_copy(pairs[half, :, half], M["dots"][half, :, half]).then_inc(S["paired"], 1)
            pool.wait_ge(S["paired"], 2)

        @block.tensor
        def _(pe):
            view = M["scores"][:].rearrange("p r (c h) -> p h c r", h=H)
            for b in range(n_bank):
                if b >= 4:
                    pe.wait_ge(S["copied"], b - 3)
                for j in range(4):
                    ins = nc.tensor.transpose(bank[b % 4][0:TS_ROWS, j, :], view[:, b // 2, 4 * (b % 2) + j, :],
                                              M["ident"][:])
                ins.then_inc(S["turned"], 1)
            pe.wait_ge(S["mix_in"], 32)
            pe.wait_ge(S["paired"], 2)
            for j in range(MH // 2):
                ins = nc.tensor.matmul(vw_ps[:, j, :], pairs[:, j, :], wout[:, j, :], start=True, stop=True)
            ins.then_inc(S["vw_done"], 1)
            pe.wait_ge(S["vw_copied"], 1)
            for k in range(KC):
                for j in range(MH // 2):
                    ins = nc.tensor.matmul(z_ps[:, k, :], wq[:, j, k * P:(k + 1) * P], vw[:, j, :], start=(j == 0),
                                           stop=(j == MH // 2 - 1))
            ins.then_inc(S["z_done"], 1)
            pe.wait_ge(S["ends_ready"], 1)
            for j in range(4):
                ins = nc.tensor.transpose(small[0:H, j, 0:TS_ROWS], ends[:, j, :], M["ident"][0:TS_ROWS, 0:TS_ROWS])
            ins.then_inc(S["ends_turned"], 1)
            pe.wait_ge(S["ends_ready"], 2)
            for j in range(2):
                ins = nc.tensor.transpose(small[0:TS_ROWS, j, 0:H], carry[:, j, :], M["ident"][0:H, 0:H])
            ins.then_inc(S["carry_turned"], 1)
            pe.wait_ge(S["copied"], n_bank)
            for b in range(n_bank):
                pe.wait_ge(S["exp_ready"], b // 2 + 1)
                if b >= 4:
                    pe.wait_ge(S["back"], b - 3)
                for j in range(4):
                    c = 4 * (b % 2) + j
                    ins = nc.tensor.transpose(bank[b % 4][:, j, 0:TS_ROWS], score[:, b // 2, c * P:(c + 1) * P],
                                              M["ident"][0:TS_ROWS, 0:TS_ROWS])
                ins.then_inc(S["back_turned"], 1)

        @block.scalar
        def _(act):
            for b in range(n_bank):
                act.wait_ge(S["turned"], b + 1)
                nc.scalar.copy(score[:, b // 2, (b % 2) * 512:(b % 2) * 512 + 512],
                               bank[b % 4][0:TS_ROWS].rearrange("p j n -> p (j n)")).then_inc(S["copied"], 1)
            act.wait_ge(S["vw_done"], 1)
            nc.scalar.copy(vw[:], vw_ps[:]).then_inc(S["vw_copied"], 1)
            act.wait_ge(S["z_done"], 1)
            nc.scalar.activation(M["z"][:], z_ps[:], ACT.Copy, scale=1.0 / N).then_inc(S["z_read"], 1)
            act.wait_ge(S["z_read"], 1)
            for h in range(H):
                act.wait_ge(S["steps"], M["softmax_steps"] + 3 * (h + 1))
                nc.scalar.activation(score[:, h, :], most[:, h, :], ACT.Exp).then_inc(S["exp_ready"], 1)
            view = M["scores"][:].rearrange("p r (c h) -> p h c r", h=H)
            for b in range(n_bank):
                act.wait_ge(S["back_turned"], b + 1)
                c = 4 * (b % 2)
                nc.scalar.copy(view[:, b // 2, c:c + 4, :], bank[b % 4][:, :, 0:TS_ROWS]).then_inc(S["back"], 1)
            act.wait_ge(S["back"], n_bank)

        @block.vector
        def _(dve):
            st = Steps(dve, S["steps"])

            def then(ins):
                st.mark(ins)
                st.settle()

            st.mark(nc.vector.memset(new[:, 0:1], 0.0))
            st.mark(nc.vector.memset(new[:, W:], 0.0))
            then(nc.vector.tensor_tensor(new[:, 1:W], seg[:, 1:], seg[:, 0:W - 1], ALU.is_equal))
            then(nc.vector.tensor_scalar(new[:], new[:], -1.0, BIG, ALU.add, ALU.mult))
            st.mark(nc.vector.tensor_scalar(in_first[:], seg[:], seg[:, 0:1], None, ALU.is_equal))
            then(nc.vector.tensor_scalar(in_last[:], seg[:], seg[:, W - 1:W], None, ALU.is_equal))
            st.mark(nc.vector.tensor_scalar(in_first[:], in_first[:], -1.0, BIG, ALU.add, ALU.mult))
            then(nc.vector.tensor_scalar(in_last[:], in_last[:], -1.0, BIG, ALU.add, ALU.mult))
            for h in range(H):
                dve.wait_ge(S["copied"], 2 * h + 2)
                then(nc.vector.tensor_tensor_scan(most[:, h, :], new[:, 0:W], score[:, h, :], -BIG, ALU.add, ALU.max))
                then(nc.vector.tensor_copy(ends[:, 0, h:h + 1], most[:, h, W - 1:W]))
                then(nc.vector.tensor_tensor_scan(most[:, h, ::-1], new[:, 1:][:, ::-1], most[:, h, ::-1],
                                                  -BIG, ALU.add, ALU.max))
                st.mark(nc.vector.tensor_copy(ends[:, 1, h:h + 1], most[:, h, 0:1]))
            st.mark(nc.vector.tensor_copy(ends[:, 2, :], seg[:, W - 1:W].broadcast_to([TS_ROWS, H])))
            st.mark(nc.vector.tensor_copy(ends[:, 3, :], seg[:, 0:1].broadcast_to([TS_ROWS, H])))
            st.settle()
            nc.vector.memset(link[:, 0:1], 0.0).then_inc(S["ends_ready"], 1)
            st.mark(nc.vector.memset(link[:, TS_ROWS:], 0.0))
            dve.wait_ge(S["ends_turned"], 1)
            then(nc.vector.tensor_copy(ends_t[:], small[0:H, :, 0:TS_ROWS]))
            last_f, first_b, last_seg, first_seg = (ends_t[:, j, :] for j in range(4))
            st.mark(nc.vector.tensor_tensor(link[:, 1:TS_ROWS], first_seg[:, 1:], last_seg[:, 0:TS_ROWS - 1], ALU.is_equal))
            then(nc.vector.tensor_tensor(whole[:], first_seg, last_seg, ALU.is_equal))
            st.mark(nc.vector.tensor_tensor(gate_f[:], link[:, 0:TS_ROWS], whole[:], ALU.mult))
            then(nc.vector.tensor_tensor(gate_b[:], link[:, 1:], whole[:], ALU.mult))
            st.mark(nc.vector.tensor_scalar(gate_f[:], gate_f[:], -1.0, BIG, ALU.add, ALU.mult))
            st.mark(nc.vector.tensor_scalar(gate_b[:], gate_b[:], -1.0, BIG, ALU.add, ALU.mult))
            then(nc.vector.tensor_scalar(link[:], link[:], -1.0, BIG, ALU.add, ALU.mult))
            st.mark(nc.vector.tensor_tensor_scan(run_f[:], gate_f[:], last_f, -BIG, ALU.add, ALU.max))
            then(nc.vector.tensor_tensor_scan(run_b[:, ::-1], gate_b[:, ::-1], first_b[:, ::-1], -BIG, ALU.add, ALU.max))
            st.mark(nc.vector.memset(carry[:, 0, 0:1], -BIG))
            st.mark(nc.vector.memset(carry[:, 1, TS_ROWS - 1:], -BIG))
            st.mark(nc.vector.tensor_tensor(carry[:, 0, 1:], run_f[:, 0:TS_ROWS - 1], link[:, 1:TS_ROWS], ALU.add))
            st.settle()
            nc.vector.tensor_tensor(carry[:, 1, 0:TS_ROWS - 1], run_b[:, 1:], link[:, 1:TS_ROWS],
                                    ALU.add).then_inc(S["ends_ready"], 1)
            dve.wait_ge(S["carry_turned"], 1)
            then(nc.vector.tensor_copy(carry_t[:], small[0:TS_ROWS, 0:2, 0:H]))
            assert st.n == M["softmax_steps"], st.n
            for h in range(H):
                then(nc.vector.scalar_tensor_tensor(out=most[:, h, :], in0=in_first[:], scalar=carry_t[:, 0, h:h + 1],
                                                    in1=most[:, h, :], op0=ALU.add, op1=ALU.max))
                then(nc.vector.scalar_tensor_tensor(out=most[:, h, :], in0=in_last[:], scalar=carry_t[:, 1, h:h + 1],
                                                    in1=most[:, h, :], op0=ALU.add, op1=ALU.max))
                then(nc.vector.tensor_tensor(most[:, h, :], score[:, h, :], most[:, h, :], ALU.subtract))


AGG = C + H


def stage_aggregate(nc, A, M, R):
    with ExitStack() as ctx:
        sb = lambda name, shape, dt=F32: ctx.enter_context(nc.sbuf_tensor(name, shape, dt))
        sem = lambda name: ctx.enter_context(nc.semaphore(name))
        v = sb("a_v", [P, 2, HALF, C])
        w = sb("a_w", [P, 2, HALF, AGG])
        is_dst = sb("a_is_dst", [P, 2, HALF, P])
        ex = sb("a_ex", [P, 2, HALF, H])
        index = sb("a_index", [P, GROUP], I32)
        odd = sb("a_odd_sums", [P, RBLK, AGG])
        sum_ps = [ctx.enter_context(nc.psum_tensor(f"a_sum_ps{b}", [P, AGG], F32)) for b in range(8)]
        v_in = [sem(f"a_v_in{h}") for h in range(2)]
        tail_in = sem("a_tail_in")
        names = "zeroed started index_ready ex_ready pool_done act_done dve_done summed added whole pool_whole"
        CUT = 17
        S = {n: sem("a_" + n) for n in names.split()}
        POOL_TILES = (range(0, GROUP), range(GROUP, HALF))
        ACT_TILES = (range(GROUP, HALF), range(0, GROUP))
        sums = M["sums"]
        heads = lambda x: x.rearrange("p u (h d) -> p u h d", d=D)

        block = ctx.enter_context(nc.Block())

        @block.sync
        def _(sp):
            with sp.Fori(0, TURNS_E) as i:
                for h in range(2):
                    for name in ("pool_done", "act_done"):
                        sp.wait_ge(S[name], i * 2 + h)
                    sp.nop(nofuse=True)
                    n = HALF - h * GROUP
                    sp.dma_start(v[:, h, 0:n].rearrange("p u c -> p (u c)"),
                                 R["v"][bass.ds(i * 2 + h, 1)].rearrange("a p n -> (a p) n")[:, 0:n * C]
                                 ).then_inc(v_in[h], 16)

        @block.scalar
        def _(act):
            def indices(turn):
                nc.scalar.activation(index[:], M["src"][:, bass.ds(turn * 2 + 1, 1), :].rearrange("p a c -> p (a c)")
                                     [:, GROUP:], ACT.Copy, scale=2.0, bias=1.0).then_inc(S["index_ready"], 1)

            indices(0)
            act.wait_ge(S["started"], 1)
            with act.Fori(0, TURNS_E) as i:
                for h in range(2):
                    hh = i * 2 + h
                    act.wait_ge(S["pool_done"], hh)
                    act.wait_ge(S["act_done"], hh)
                    act.nop(nofuse=True)
                    nc.scalar.copy(ex[:, h].rearrange("p u h -> p (u h)"),
                                   M["scores"][:, bass.ds(hh, 1), :].rearrange("p a c -> p (a c)")).then_inc(S["ex_ready"], 1)
                    act.wait_ge(S["ex_ready"], hh + 1)
                    act.wait_ge(v_in[h], (i + 1) * 16)
                    if h == 1:
                        act.wait_ge(tail_in, (i + 1) * (16 * GROUP))
                        act.nop(nofuse=True)
                        indices(i + 1)
                    act.wait_ge(S["summed"], hh * 2)
                    for u in ACT_TILES[h]:
                        for hd in range(H):
                            ins = nc.scalar.activation(w[:, h, u, hd * D:(hd + 1) * D], v[:, h, u, hd * D:(hd + 1) * D],
                                                       ACT.Copy, scale=ex[:, h, u, hd:hd + 1])
                    ins.then_inc(S["act_done"], 1)

        @block.gpsimd
        def _(pool):
            nc.gpsimd.memset(sums[:], 0.0).then_inc(S["zeroed"], 1)
            pool.wait_ge(S["started"], 1)

            def gather(turn):
                pool.wait_ge(S["index_ready"], turn + 1)
                pool.nop(nofuse=True)
                for b in range(GROUP):
                    nc.gpsimd.indirect_dma_start(out=v[:, 1, GROUP + b, :], out_offset=None,
                                                 in_=R["kv"].rearrange("n (a c) -> (n a) c", a=2),
                                                 in_offset=bass.IndirectOffsetOnAxis(ap=index[:, b:b + 1], axis=0)
                                                 ).then_inc(tail_in, 16)

            gather(0)
            with pool.Fori(0, TURNS_E) as i:
                for h in range(2):
                    hh = i * 2 + h
                    pool.wait_ge(S["ex_ready"], hh + 1)
                    pool.wait_ge(v_in[h], (i + 1) * 16)
                    if h == 1:
                        pool.wait_ge(tail_in, (i + 1) * (16 * GROUP))
                    pool.wait_ge(S["summed"], hh * 2)
                    pool.nop(nofuse=True)
                    mine = slice(POOL_TILES[h].start, POOL_TILES[h].stop)
                    nc.gpsimd.tensor_tensor(heads(w[:, h, mine, 0:C]), heads(v[:, h, mine, :]),
                                            ex[:, h, mine, :, None].broadcast_to([P, GROUP, H, D]), ALU.mult)
                    nc.gpsimd.tensor_copy(w[:, h, :, C:], ex[:, h]).then_inc(S["pool_done"], 1)
                pool.wait_ge(S["pool_done"], i * 2 + 3)
                gather(i + 1)
            pool.wait_ge(tail_in, (TURNS_E + 1) * (16 * GROUP))
            pool.wait_ge(S["added"], T + 8)
            nc.gpsimd.tensor_tensor(sums[:, 0:CUT, :], sums[:, 0:CUT, :], odd[:, 0:CUT, :], ALU.add
                                    ).then_inc(S["pool_whole"], 1)
            pool.wait_ge(S["pool_whole"], 1)

        @block.vector
        def _(dve):
            nc.vector.memset(is_dst[:, 0, 0, 0:1], 0.0).then_inc(S["added"], 8)
            for name in ("pool_done", "act_done", "dve_done"):
                dve.sem_inc(S[name], 1)
            dve.sem_inc(S["summed"], 2)
            dve.wait_ge(S["added"], 8)
            dve.sem_inc(S["started"], 3)

            def prepare(h, hh):
                dve.wait_ge(S["summed"], hh * 2)
                dve.nop(nofuse=True)
                nc.vector.tensor_tensor(is_dst[:, h], M["col"][:, None, :].broadcast_to([P, HALF, P]),
                                        M["local"][:, bass.ds(hh, 1), :].rearrange("p a u -> p (a u)")[:, :, None]
                                        .broadcast_to([P, HALF, P]), ALU.is_equal).then_inc(S["dve_done"], 1)

            def add(h, i, regs):
                for u in range(HALF):
                    t = i * SLOTS + h * HALF + u
                    if u % GROUP == 0:
                        dve.wait_ge(S["summed"], i * GROUPS + h * 2 + u // GROUP + 3)
                    dve.wait_ge(S["added"], t + 7)
                    dve.nop(nofuse=True)
                    at = (sums, odd)[u % 2][:, bass.ds(regs[h * HALF + u], 1), :].rearrange("p a c -> p (a c)")
                    nc.vector.tensor_tensor(at, at, sum_ps[u][:], ALU.add).then_inc(S["added"], 1)

            at_block = [dve.alloc_register(f"a_at{u}") for u in range(SLOTS)]
            row = lambda i: load_row(dve, at_block, M["blk"][0:1, bass.ds(i * SLOTS, SLOTS)], RBLK - 1)
            nc.vector.memset(odd[:], 0.0).then_inc(S["zeroed"], 1)
            prepare(0, 0)
            dve.wait_ge(S["zeroed"], 2)
            with dve.Fori(0, TURNS_E - 1) as i:
                prepare(1, i * 2 + 1)
                regs = row(i)
                add(0, i, regs)
                prepare(0, i * 2 + 2)
                add(1, i, regs)
            i = TURNS_E - 1
            regs = row(i)
            prepare(1, i * 2 + 1)
            add(0, i, regs)
            add(1, i, regs)
            dve.wait_ge(S["added"], T + 8)
            nc.vector.tensor_tensor(sums[:, CUT:RBLK, :], sums[:, CUT:RBLK, :], odd[:, CUT:, :], ALU.add
                                    ).then_inc(S["whole"], 1)
            dve.wait_ge(S["whole"], 1)

        @block.tensor
        def _(pe):
            pe.wait_ge(S["started"], 1)
            with pe.Fori(0, TURNS_E) as i:
                for h in range(2):
                    hh = i * 2 + h
                    for name in ("pool_done", "act_done", "dve_done"):
                        pe.wait_ge(S[name], hh + 2)
                    for g in range(2):
                        pe.wait_ge(S["added"], (hh * 2 + g) * GROUP + 4)
                        for u in range(g * GROUP, (g + 1) * GROUP):
                            ins = nc.tensor.matmul(sum_ps[u][:], is_dst[:, h, u, :], w[:, h, u, :], start=True, stop=True)
                        ins.then_inc(S["summed"], 1)


def load_row(eng, regs, row, most):
    eng.load(regs, row)
    return [eng.snap(r, min_val=0, max_val=most) for r in regs]


NQ = NBLK // QUAD


def stage_nodes(nc, A, M, R):
    with ExitStack() as ctx:
        sb = lambda name, shape, dt=F32: ctx.enter_context(nc.sbuf_tensor(name, shape, dt))
        sem = lambda name: ctx.enter_context(nc.semaphore(name))
        wo = sb("n_wo", [P, KC, C])
        bo = sb("n_bo", [P, C])
        gamma = sb("n_gamma", [P, C])
        beta = sb("n_beta", [P, C])
        bout = sb("n_bout", [P, C])
        rden = sb("n_rden", [P, NBLK, H])
        none = sb("n_none", [P, NBLK])
        v = sb("n_v", [P, 3, QUAD, C])
        x = sb("n_x", [P, 3, QUAD, C])
        xn = sb("n_xn", [P, 3, QUAD, C])
        xnt = sb("n_xnt", [P, 3, QUAD, KC * P])
        y = sb("n_y", [P, 3, QUAD, C])
        turned = sb("n_turned", [P, QUAD, KC * P])
        out = sb("n_out", [P, 3, QUAD, 2 * C])
        x2t = sb("n_x2t", [P, QUAD, KC * P])
        x2t_out = sem("n_x2t_out")
        stats = sb("n_stats", [P, 2, QUAD, 6])
        mv = sb("n_mv", [P, 2, QUAD, 2])
        std = sb("n_std", [P, 2, QUAD])
        rstd = sb("n_rstd", [P, 2, QUAD])
        t_ps = ctx.enter_context(nc.psum_tensor("n_t_ps", [P, QUAD, KC * P], F32))
        x2_ps = ctx.enter_context(nc.psum_tensor("n_x2_ps", [P, QUAD, KC * P], F32))
        y_ps = ctx.enter_context(nc.psum_tensor("n_y_ps", [P, QUAD, C], F32))
        z_ps = ctx.enter_context(nc.psum_tensor("n_z_ps", [P, QUAD, C], F32))
        fixed_in = sem("n_fixed_in")
        loads = [sem(f"n_loads{w}") for w in range(3)]
        stored = [sem(f"n_stored{w}") for w in range(3)]
        names = ("steps scaled msg_steps x1_steps bias_ready v_ready msg_ready msg_turned msg_copied y_done z_done xn_ready "
                 "x_ready y_sum mv0_ready mv1_ready std0_ready std1_ready y_normed y_scaled x1_ready x2_ready "
                 "x2_turned x2_copied")
        S = {n: sem("n_" + n) for n in names.split()}
        sums = M["sums"]
        quad = lambda ap, w: ap.rearrange("(q b p) c -> q p b c", b=QUAD, p=P)[bass.ds(w, 1)].rearrange(
            "a p b c -> (a p) b c")
        block = ctx.enter_context(nc.Block())

        def turns(ahead, main, behind, eng):
            ahead(0, 0, 0)
            ahead(1, 1, 0)
            main(0, 0, 0)
            with eng.Fori(0, (NQ - 2) // 3) as i:
                for w in range(3):
                    ahead(i * 3 + w + 2, (w + 2) % 3, i + (w + 2) // 3)
                    main(i * 3 + w + 1, (w + 1) % 3, i + (w + 1) // 3)
                    behind(i * 3 + w, w, i)
            for q in range((NQ - 2) // 3 * 3 + 1, NQ):
                if q + 1 < NQ:
                    ahead(q + 1, (q + 1) % 3, (q + 1) // 3)
                main(q, q % 3, q // 3)
                behind(q - 1, (q - 1) % 3, (q - 1) // 3)
            behind(NQ - 1, (NQ - 1) % 3, (NQ - 1) // 3)

        def nothing(q, w, k):
            pass

        @block.sync
        def _(sp):
            sp.dma_start(wo[:], rows(A["L0_gnn_Wo"], KC)).then_inc(fixed_in, 16)
            for tile, name in ((bo, "L0_gnn_bo"), (gamma, "L0_gnn_gamma"), (beta, "L0_gnn_beta"), (bout, "L0_mix_bout")):
                sp.dma_start(tile[:], A[name].rearrange("(a n) -> a n", a=1).broadcast_to([P, C])).then_inc(fixed_in, 16)

            def load(q, w):
                sp.dma_start(v[:, w], quad(R["kv"][:, C:], q)).then_inc(loads[w], 16)
                sp.dma_start(x[:, w], quad(A["x"][0:NPAD, :], q)).then_inc(loads[w], 16)
                sp.dma_start(xn[:, w], quad(R["xn"], q)).then_inc(loads[w], 16)
                sp.dma_start(xnt[:, w], R["xnt"].rearrange("(q b) p n -> q p b n", b=QUAD)[bass.ds(q, 1)]
                             .rearrange("a p b n -> (a p) b n")).then_inc(loads[w], 16)

            def load_next(q, w, k):
                if isinstance(q, int) and q + 1 >= NQ:
                    return
                if not (isinstance(q, int) and q <= 1):
                    sp.wait_ge(S["y_scaled"], q * 2 - 2)
                    sp.nop(nofuse=True)
                    sp.wait_ge(S["z_done"], q - 1)
                    sp.nop(nofuse=True)
                load(q + 1, (w + 1) % 3)

            def store(q, w, k):
                sp.wait_ge(S["x2_ready"], q + 1)
                sp.nop(nofuse=True)
                sp.dma_start(quad(R["x12"], q), out[:, w]).then_inc(stored[w], 16)

            load(0, 0)
            turns(load_next, nothing, store, sp)
            for w in range(3):
                sp.wait_ge(stored[w], 16 * ((NQ + 2 - w) // 3))

        @block.gpsimd
        def _(pool):
            pool.wait_ge(fixed_in, 80)
            nc.gpsimd.tensor_tensor(beta[:], beta[:], bout[:], ALU.add).then_inc(S["bias_ready"], 1)
            pool.wait_ge(S["bias_ready"], 1)
            pool.wait_ge(S["steps"], 3)
            over = lambda t: t[:, None, :].broadcast_to([P, QUAD, C])

            def prepare(q, w, k):
                pool.wait_ge(loads[w], (k + 1) * 64)
                pool.nop(nofuse=True)
                nc.gpsimd.tensor_tensor(v[:, w], v[:, w], none[:, bass.ds(q * QUAD, QUAD)][:, :, None].broadcast_to(
                    [P, QUAD, C]), ALU.mult).then_inc(S["v_ready"], 1)
                nc.gpsimd.tensor_tensor(xn[:, w], xn[:, w], over(bo), ALU.add).then_inc(S["xn_ready"], 1)
                nc.gpsimd.tensor_tensor(x[:, w], x[:, w], over(beta), ALU.add).then_inc(S["x_ready"], 1)

            def scale(q, w, k):
                pool.wait_ge(S["y_normed"], (q + 1) * QUAD)
                pool.nop(nofuse=True)
                nc.gpsimd.tensor_tensor(y[:, w], y[:, w], over(gamma), ALU.mult).then_inc(S["y_scaled"], 1)
                pool.wait_ge(S["y_scaled"], q * 2 + 1)
                pool.wait_ge(S["x_ready"], q + 1)
                pool.nop(nofuse=True)
                nc.gpsimd.tensor_tensor(y[:, w], y[:, w], x[:, w], ALU.add).then_inc(S["y_scaled"], 1)

            turns(prepare, scale, nothing, pool)

        @block.scalar
        def _(act):
            def deviation(q, j):
                act.wait_ge(S[f"mv{j}_ready"], (q + 1) * QUAD)
                act.nop(nofuse=True)
                nc.scalar.activation(std[:, j, :], mv[:, j, :, 1], ACT.Sqrt, bias=M["eps"][:]
                                     ).then_inc(S[f"std{j}_ready"], 1)

            def copy_messages(q, w, k):
                act.wait_ge(S["msg_turned"], q + 1)
                act.wait_ge(S["y_done"], q)
                act.nop(nofuse=True)
                nc.scalar.copy(turned[:], t_ps[:]).then_inc(S["msg_copied"], 1)

            def graph_deviation(q, w, k):
                deviation(q, 0)

            def finish(q, w, k):
                deviation(q, 1)
                act.wait_ge(S["x2_turned"], q + 3)
                act.wait_ge(x2t_out, q * 16)
                act.nop(nofuse=True)
                nc.scalar.copy(x2t[:], x2_ps[:]).then_inc(S["x2_copied"], 1)
                act.wait_ge(S["x2_copied"], q + 1)
                act.nop(nofuse=True)
                act.dma_start(R["x2t"][bass.ds(q, 1)].rearrange("a p n -> (a p) n"),
                              x2t[:].rearrange("p b n -> p (b n)")).then_inc(x2t_out, 16)

            turns(copy_messages, graph_deviation, finish, act)
            act.wait_ge(x2t_out, 16 * NQ)

        @block.vector
        def _(dve):
            st = Steps(dve, S["steps"])

            def then(ins):
                st.mark(ins)
                st.settle()

            den = sums[:, :, C:]
            then(nc.vector.tensor_scalar(rden[:], den, 0.5, None, ALU.max))
            then(nc.vector.reciprocal(rden[:], rden[:]))
            st.mark(nc.vector.tensor_scalar(none[:], sums[:, :, C], 0.0, None, ALU.is_equal))
            st.settle()
            PER = 5

            def statistics(q, src, j, steps):
                st = Steps(dve, S[steps], q * PER)
                for b in range(QUAD):
                    st.mark(nc.vector.bn_stats(stats[:, j, b, :], src[:, b, :]))
                st.settle()
                dve.nop(nofuse=True)
                for b in range(QUAD):
                    nc.vector.bn_aggr(mv[:, j, b, :], stats[:, j, b, :]).then_inc(S[f"mv{j}_ready"], 1)
                dve.wait_ge(S[f"std{j}_ready"], q + 1)
                st.mark(nc.vector.reciprocal(rstd[:, j, :], std[:, j, :]))
                st.settle()
                assert st.n == PER

            def messages(q, w, k):
                part = sums[:, bass.ds(q * QUAD, QUAD), 0:C].rearrange("p b (h d) -> p b h d", d=D)
                nc.vector.tensor_tensor(part, part, rden[:, bass.ds(q * QUAD, QUAD), :][:, :, :, None]
                                        .broadcast_to([P, QUAD, H, D]), ALU.mult).then_inc(S["scaled"], 1)
                dve.wait_ge(S["scaled"], q + 1)
                dve.wait_ge(S["v_ready"], q + 1)
                dve.nop(nofuse=True)
                nc.vector.tensor_tensor(v[:, w], v[:, w], sums[:, bass.ds(q * QUAD, QUAD), 0:C], ALU.add
                                        ).then_inc(S["msg_ready"], 1)

            def graph_norm(q, w, k):
                dve.wait_ge(S["y_done"], q + 1)
                dve.wait_ge(S["xn_ready"], q + 1)
                dve.wait_ge(S["y_normed"], q * QUAD)
                dve.nop(nofuse=True)
                nc.vector.tensor_tensor(y[:, w], y_ps[:], xn[:, w], ALU.add).then_inc(S["y_sum"], 1)
                dve.wait_ge(S["y_sum"], q + 1)
                dve.nop(nofuse=True)
                statistics(q, y[:, w], 0, "msg_steps")
                for b in range(QUAD):
                    nc.vector.tensor_scalar(y[:, w, b, :], y[:, w, b, :], mv[:, 0, b, 0:1], rstd[:, 0, b:b + 1],
                                            ALU.subtract, ALU.mult).then_inc(S["y_normed"], 1)

            def second_norm(q, w, k):
                dve.wait_ge(S["y_scaled"], q * 2 + 2)
                dve.wait_ge(S["z_done"], q + 1)
                dve.wait_ge(stored[w], k * 16)
                dve.wait_ge(S["x2_turned"], q)
                dve.wait_ge(S["x2_ready"], q)
                dve.nop(nofuse=True)
                nc.vector.tensor_tensor(out[:, w, :, 0:C], z_ps[:], y[:, w], ALU.add).then_inc(S["x1_ready"], 1)
                dve.wait_ge(S["x1_ready"], q + 1)
                dve.nop(nofuse=True)
                statistics(q, out[:, w, :, 0:C], 1, "x1_steps")
                for b in range(QUAD):
                    ins = nc.vector.tensor_scalar(out[:, w, b, C:], out[:, w, b, 0:C], mv[:, 1, b, 0:1],
                                                  rstd[:, 1, b:b + 1], ALU.subtract, ALU.mult)
                ins.then_inc(S["x2_ready"], 1)

            turns(messages, graph_norm, second_norm, dve)
            dve.wait_ge(S["x2_ready"], NQ)

        @block.tensor
        def _(pe):
            pe.wait_ge(fixed_in, 80)
            pe.sem_inc(S["x2_turned"], 2)

            def turn(to, src):
                for b in range(QUAD):
                    for k in range(KC):
                        ins = nc.tensor.transpose(to[:, b, k * P:(k + 1) * P], src[:, b, k * P:(k + 1) * P], M["ident"][:])
                return ins

            def product(to, left, right):
                for b in range(QUAD):
                    for k in range(KC):
                        ins = nc.tensor.matmul(to[:, b, :], left[:, b, k * P:(k + 1) * P], right[:, k, :],
                                               start=(k == 0), stop=(k == KC - 1))
                return ins

            def graph(q, w, k):
                pe.wait_ge(S["msg_ready"], q + 1)
                pe.wait_ge(S["msg_copied"], q)
                turn(t_ps, v[:, w]).then_inc(S["msg_turned"], 1)
                pe.wait_ge(S["msg_copied"], q + 1)
                pe.wait_ge(S["y_sum"], q)
                product(y_ps, turned, wo).then_inc(S["y_done"], 1)

            def mixer(q, w, k):
                pe.wait_ge(loads[w], (k + 1) * 64)
                pe.wait_ge(S["x1_ready"], q)
                product(z_ps, xnt[:, w], M["z"]).then_inc(S["z_done"], 1)

            def turn_x2(q, w, k):
                pe.wait_ge(S["x2_ready"], q + 1)
                pe.wait_ge(S["x2_copied"], q)
                turn(x2_ps, out[:, w, :, C:]).then_inc(S["x2_turned"], 1)

            turns(graph, mixer, turn_x2, pe)


NTILE = 56


def stage_hidden(nc, A, M, R):
    with ExitStack() as ctx:
        sb = lambda name, shape, dt=F32: ctx.enter_context(nc.sbuf_tensor(name, shape, dt))
        sem = lambda name: ctx.enter_context(nc.semaphore(name))
        wg = sb("h_wg", [P, HC, NEXP])
        bg = sb("h_bg", [P, NEXP])
        x2t = sb("h_x2t", [P, 2, QUAD, KC * P])
        ht = sb("h_ht", [P, HC, QUAD * P])
        h_ps = [ctx.enter_context(nc.psum_tensor(f"h_h_ps{b}", [P, QUAD * P], F32)) for b in range(4)]
        l_ps = [ctx.enter_context(nc.psum_tensor(f"h_l_ps{b}", [P, QUAD, NEXP], F32)) for b in range(2)]
        x_in = [sem(f"h_x_in{w}") for w in range(2)]
        S = {n: sem("h_" + n) for n in "fixed_in rest_set h_done gelu_done l_done l_read".split()}
        PAIRS = NQ // 2
        block = ctx.enter_context(nc.Block())

        def turns(eng, body):
            with eng.Fori(0, PAIRS) as i:
                for w in range(2):
                    body(i * 2 + w, w, i)
            body(NQ - 1, 0, PAIRS)

        full = lambda q: RBLK - (NQ - 1) * QUAD if isinstance(q, int) and q == NQ - 1 else QUAD

        @block.sync
        def _(sp):
            sp.dma_start(M["w1"][:], rows(A["L0_ffn_W1"], KC)).then_inc(S["fixed_in"], 16)
            sp.dma_start(M["b1"][:], A["L0_ffn_b1"].rearrange("(c p) -> p c", p=P),
                         allow_slow_non_contiguous=True).then_inc(S["fixed_in"], 16)
            sp.dma_start(wg[:], rows(A["L0_ffn_Wg"], HC)).then_inc(S["fixed_in"], 16)
            sp.dma_start(bg[:], A["L0_ffn_bg"].rearrange("(a n) -> a n", a=1).broadcast_to([P, NEXP])
                         ).then_inc(S["fixed_in"], 16)

            def load(q, w, i):
                sp.wait_ge(S["l_read"], q)
                sp.nop(nofuse=True)
                sp.dma_start(x2t[:, w].rearrange("p b n -> p (b n)"),
                             R["x2t"][bass.ds(q, 1)].rearrange("a p n -> (a p) n")).then_inc(x_in[w], 16)

            load(0, 0, 0)
            with sp.Fori(0, PAIRS) as i:
                for w in range(2):
                    sp.wait_ge(S["l_read"], i * 2 + w)
                    sp.nop(nofuse=True)
                    sp.dma_start(x2t[:, 1 - w].rearrange("p b n -> p (b n)"),
                                 R["x2t"][bass.ds(i * 2 + w + 1, 1)].rearrange("a p n -> (a p) n")).then_inc(x_in[1 - w], 16)
            for e in range(NEXP):
                sp.dma_start(M["wd"][:, e], rows(A["L0_ffn_Wd"][e], HC)).then_inc(S["fixed_in"], 16)
            sp.dma_start(M["bd"][:].rearrange("p e n -> p (e n)"), A["L0_ffn_bd"].rearrange("(a e) n -> a (e n)", a=1)
                         .broadcast_to([P, NEXP * C])).then_inc(S["fixed_in"], 16)
            sp.wait_ge(S["fixed_in"], 16 * (5 + NEXP))

        @block.scalar
        def _(act):
            act.wait_ge(S["fixed_in"], 64)

            def body(q, w, i):
                for c in range(HC):
                    act.wait_ge(S["h_done"], q * HC + c + 1)
                    if c == 0:
                        act.wait_ge(S["l_done"], q)
                    n = full(q) * P
                    nc.scalar.activation(ht[:, c, 0:n], h_ps[c % 4][:, 0:n], ACT.Gelu, bias=M["b1"][:, c:c + 1]
                                         ).then_inc(S["gelu_done"], 1)

            turns(act, body)

        @block.vector
        def _(dve):
            dve.wait_ge(S["fixed_in"], 64)
            nc.vector.memset(M["logits"][:, RBLK:, :], 0.0).then_inc(S["rest_set"], 1)

            def body(q, w, i):
                dve.wait_ge(S["l_done"], q + 1)
                dve.nop(nofuse=True)
                n = full(q)
                nc.vector.tensor_tensor(M["logits"][:, bass.ds(q * QUAD, n), :], l_ps[w][:, 0:n, :],
                                        bg[:, None, :].broadcast_to([P, n, NEXP]), ALU.add).then_inc(S["l_read"], 1)

            turns(dve, body)
            dve.wait_ge(S["l_read"], NQ)
            dve.wait_ge(S["rest_set"], 1)

        @block.tensor
        def _(pe):
            pe.wait_ge(S["fixed_in"], 64)

            def logits(q, w, c):
                pe.wait_ge(S["gelu_done"], q * HC + c + 1)
                for b in range(full(q)):
                    ins = nc.tensor.matmul(l_ps[w][:, b, :], ht[:, c, b * P:(b + 1) * P], wg[:, c, :],
                                           start=(c == 0 and b == 0), stop=(c == HC - 1), skip_group_check=True)
                if c == HC - 1:
                    ins.then_inc(S["l_done"], 1)

            def body(q, w, i):
                pe.wait_ge(x_in[w], (i + 1) * 16)
                pe.wait_ge(S["l_read"], q)
                for c in range(HC):
                    if c >= 4:
                        pe.wait_ge(S["gelu_done"], q * HC + c - 3)
                    for k in range(KC):
                        n = full(q)
                        ins = nc.tensor.matmul(h_ps[c % 4][:, 0:n * P], M["w1"][:, k, c * P:(c + 1) * P],
                                               x2t[:, w, 0:n, k * P:(k + 1) * P], start=(k == 0), stop=(k == KC - 1))
                    ins.then_inc(S["h_done"], 1)
                    if c >= 2:
                        logits(q, w, c - 2)
                logits(q, w, HC - 2)
                logits(q, w, HC - 1)

            turns(pe, body)


def stage_route(nc, A, M, R):
    with ExitStack() as ctx:
        sb = lambda name, shape, dt=F32: ctx.enter_context(nc.sbuf_tensor(name, shape, dt))
        sem = lambda name: ctx.enter_context(nc.semaphore(name))
        largest = sb("r_largest", [P, NBLK])
        prob = sb("r_prob", [P, NBLK, NEXP])
        total = sb("r_total", [P, NBLK])
        number = sb("r_number", [P, NEXP])
        choice = sb("r_choice", [P, NBLK, NEXP])
        first = sb("r_first", [P, NBLK])
        node = sb("r_node", [P, NBLK])
        real = sb("r_real", [P, NBLK])
        is_exp = sb("r_is_exp", [P, NEXP, NBLK])
        before = sb("r_before", [P, NEXP, NBLK])
        running = sb("r_running", [P, NEXP, NBLK])
        tiles_i = sb("r_tiles_i", [P, NEXP], I32)
        tiles = sb("r_tiles", [P, NEXP])
        first_tile = sb("r_first_tile", [P, NEXP + 1])
        place = sb("r_place", [P, NBLK])
        place_i = sb("r_place_i", [P, NBLK], I32)
        lane_i = sb("r_lane_i", [P, NBLK], I32)
        lane_f = sb("r_lane_f", [P, NBLK])
        column = sb("r_column", [P, NBLK])
        lane_hot = sb("r_lane_hot", [P, RBLK, P])
        tile_hot = sb("r_tile_hot", [P, RBLK, NTILE])
        value = sb("r_value", [P, 2, NBLK])
        placed_value = sb("r_placed_value", [P, RBLK, 2, NTILE])
        empty = sb("r_empty", [P, NTILE])
        id_f = sb("r_id_f", [P, NTILE])
        tile_no = sb("r_tile_no", [P, NTILE])
        begun = sb("r_begun", [P, NTILE, NEXP])
        expert = sb("r_expert", [P, NTILE])
        below = sb("r_below", [P, P])
        before_ps = ctx.enter_context(nc.psum_tensor("r_before_ps", [P, NEXP, NBLK], F32))
        total_ps = ctx.enter_context(nc.psum_tensor("r_total_ps", [P, NEXP, NBLK], F32))
        perm_ps = ctx.enter_context(nc.psum_tensor("r_perm_ps", [P, 2, NTILE], F32))
        names = "steps fixed shifted exp_done counted lanes_hot tiles_hot weighted placed expert_ready below_set"
        CHUNK = 7
        chunks = range(0, RBLK, CHUNK)
        S = {n: sem("r_" + n) for n in names.split()}
        block = ctx.enter_context(nc.Block())

        @block.gpsimd
        def _(pool):
            io = lambda out, pattern, mult, base=0: nc.gpsimd.iota(
                out, pattern=pattern, base=base, channel_multiplier=mult, allow_small_or_imprecise_dtypes=True
            ).then_inc(S["fixed"], 1)
            io(number[:], [[1, NEXP]], 0)
            io(node[:], [[P, NBLK]], 1)
            io(tile_no[:], [[1, NTILE]], 0)
            nc.gpsimd.affine_select(out=below[:], in_=M["ones"][:], compare_op=ALU.is_gt, fill=0.0, base=0,
                                    pattern=[[1, P]], channel_multiplier=-1).then_inc(S["below_set"], 1)
            for c, lo in enumerate(chunks):
                pool.wait_ge(S["tiles_hot"], c + 1)
                for k in range(2):
                    ins = nc.gpsimd.tensor_tensor(placed_value[:, lo:lo + CHUNK, k, :], tile_hot[:, lo:lo + CHUNK, :],
                                                  value[:, k, lo:lo + CHUNK, None].broadcast_to([P, CHUNK, NTILE]),
                                                  ALU.mult)
                ins.then_inc(S["weighted"], 1)

        @block.scalar
        def _(act):
            act.wait_ge(S["shifted"], 1)
            nc.scalar.activation(prob[:], prob[:], ACT.Exp).then_inc(S["exp_done"], 1)

        @block.vector
        def _(dve):
            st = Steps(dve, S["steps"])

            def then(ins):
                st.mark(ins)
                st.settle()

            by_node = lambda x: x[:, :, None].broadcast_to([P, NBLK, NEXP])
            then(nc.vector.tensor_reduce(largest[:], M["logits"][:], AX_X, ALU.max))
            nc.vector.tensor_tensor(prob[:], M["logits"][:], by_node(largest), ALU.subtract).then_inc(S["shifted"], 1)
            dve.wait_ge(S["exp_done"], 1)
            dve.wait_ge(S["fixed"], 3)
            st.mark(nc.vector.tensor_reduce(total[:], prob[:], AX_X, ALU.add))
            then(nc.vector.tensor_reduce(largest[:], prob[:], AX_X, ALU.max))
            then(nc.vector.tensor_tensor(choice[:], prob[:], by_node(largest), ALU.is_equal))
            then(nc.vector.tensor_scalar(choice[:], choice[:], -float(NEXP), float(NEXP), ALU.mult, ALU.add))
            then(nc.vector.tensor_tensor(choice[:], choice[:], number[:, None, :].broadcast_to([P, NBLK, NEXP]), ALU.add))
            st.mark(nc.vector.tensor_reduce(first[:], choice[:], AX_X, ALU.min))
            st.mark(nc.vector.tensor_scalar(real[:], node[:], float(N), None, ALU.is_lt))
            then(nc.vector.reciprocal(total[:], total[:]))
            st.mark(nc.vector.tensor_tensor(value[:, 1, :], largest[:], total[:], ALU.mult))
            st.mark(nc.vector.tensor_scalar(value[:, 0, :], node[:], 1.0, None, ALU.add))
            view = is_exp[:].rearrange("p e b -> p b e")
            then(nc.vector.tensor_tensor(view, by_node(first), number[:, None, :].broadcast_to([P, NBLK, NEXP]),
                                         ALU.is_equal))
            nc.vector.tensor_tensor(view, view, by_node(real), ALU.mult).then_inc(S["fixed"], 1)
            dve.wait_ge(S["counted"], 2)
            then(nc.vector.tensor_copy(before[:], total_ps[:]))
            for e in range(NEXP):
                st.mark(nc.vector.tensor_tensor_scan(running[:, e, :], M["ones"][:, 0:NBLK], before[:, e, :], 0.0,
                                                     ALU.mult, ALU.add))
            st.settle()
            then(nc.vector.tensor_scalar(tiles_i[:], running[:, :, NBLK - 1], float(P - 1), None, ALU.add))
            then(nc.vector.tensor_scalar(tiles_i[:], tiles_i[:], 7, None, ALU.arith_shift_right))
            st.mark(nc.vector.tensor_copy(tiles[:], tiles_i[:]))
            then(nc.vector.memset(first_tile[:, 0:1], 0.0))
            then(nc.vector.tensor_tensor_scan(first_tile[:, 1:], M["ones"][:, 0:NEXP], tiles[:], 0.0, ALU.mult, ALU.add))
            then(nc.vector.tensor_tensor(before[:], running[:], before[:], ALU.subtract))
            then(nc.vector.tensor_tensor(before[:], before[:], before_ps[:], ALU.add))
            then(nc.vector.tensor_scalar(first_tile[:], first_tile[:], float(P), None, ALU.mult))
            then(nc.vector.tensor_tensor(before[:], before[:], first_tile[:, 0:NEXP, None].broadcast_to([P, NEXP, NBLK]),
                                         ALU.add))
            then(nc.vector.tensor_tensor(before[:], before[:], is_exp[:], ALU.mult))
            then(nc.vector.tensor_reduce(place[:], before[:].rearrange("p e b -> p b e"), AX_X, ALU.add))
            then(nc.vector.scalar_tensor_tensor(out=real[:], in0=real[:], scalar=-1.0, in1=node[:], op0=ALU.add,
                                                op1=ALU.mult))
            then(nc.vector.scalar_tensor_tensor(out=place[:], in0=real[:], scalar=-2.0, in1=place[:], op0=ALU.mult,
                                                op1=ALU.add))
            then(nc.vector.tensor_copy(place_i[:], place[:]))
            then(nc.vector.tensor_scalar(lane_i[:], place_i[:], P - 1, None, ALU.bitwise_and))
            st.mark(nc.vector.tensor_copy(lane_f[:], lane_i[:]))
            then(nc.vector.tensor_scalar(place_i[:], place_i[:], 7, None, ALU.arith_shift_right))
            then(nc.vector.tensor_copy(column[:], place_i[:]))
            for lo in chunks:
                part = slice(lo, lo + CHUNK)
                nc.vector.tensor_tensor(tile_hot[:, part, :], tile_no[:, None, :].broadcast_to([P, CHUNK, NTILE]),
                                        column[:, part, None].broadcast_to([P, CHUNK, NTILE]), ALU.is_equal
                                        ).then_inc(S["tiles_hot"], 1)
                nc.vector.tensor_tensor(lane_hot[:, part, :], M["col"][:, None, :].broadcast_to([P, CHUNK, P]),
                                        lane_f[:, part, None].broadcast_to([P, CHUNK, P]), ALU.is_equal
                                        ).then_inc(S["lanes_hot"], 1)
            dve.wait_ge(S["tiles_hot"], len(chunks))
            then(nc.vector.tensor_scalar(tile_no[:], tile_no[:], float(P), None, ALU.mult))
            then(nc.vector.tensor_tensor(begun[:], first_tile[:, None, 0:NEXP].broadcast_to([P, NTILE, NEXP]),
                                         tile_no[:, :, None].broadcast_to([P, NTILE, NEXP]), ALU.is_le))
            then(nc.vector.tensor_reduce(expert[:], begun[:], AX_X, ALU.add))
            nc.vector.tensor_scalar(M["expert"][:], expert[0:1, :], -1.0, None, ALU.add).then_inc(S["expert_ready"], 1)
            st.mark(nc.vector.memset(M["near"][:], 0))
            dve.wait_ge(S["placed"], 1)
            st.mark(nc.vector.tensor_copy(M["weight"][:], perm_ps[:, 1, :]))
            st.mark(nc.vector.tensor_scalar(empty[:], perm_ps[:, 0, :], 0.0, float(1 << 20), ALU.is_equal, ALU.mult))
            st.settle()
            then(nc.vector.scalar_tensor_tensor(out=id_f[:], in0=perm_ps[:, 0, :], scalar=-1.0, in1=empty[:],
                                                op0=ALU.add, op1=ALU.add))
            st.mark(nc.vector.tensor_copy(M["token"][:], id_f[:]))
            then(nc.vector.tensor_scalar(M["near"][:, 0:NTILE // QUAD, :].rearrange("p t b -> p (t b)"), id_f[:],
                                         float(N - 1), None, ALU.min))
            dve.wait_ge(S["expert_ready"], 1)

        @block.tensor
        def _(pe):
            pe.wait_ge(S["fixed"], 4)
            pe.wait_ge(S["below_set"], 1)
            flat = lambda x: x[:].rearrange("p e b -> p (e b)")
            nc.tensor.matmul(flat(before_ps), below[:], flat(is_exp), start=True, stop=True).then_inc(S["counted"], 1)
            nc.tensor.matmul(flat(total_ps), M["ones"][:], flat(is_exp), start=True, stop=True).then_inc(S["counted"], 1)
            for c, lo in enumerate(chunks):
                pe.wait_ge(S["lanes_hot"], c + 1)
                pe.wait_ge(S["weighted"], c + 1)
                for b in range(lo, lo + CHUNK):
                    ins = nc.tensor.matmul(perm_ps[:].rearrange("p k t -> p (k t)"), lane_hot[:, b, :],
                                           placed_value[:, b].rearrange("p k t -> p (k t)"),
                                           start=(b == 0), stop=(b == RBLK - 1))
            ins.then_inc(S["placed"], 1)


def stage_experts(nc, A, M, R, out):
    with ExitStack() as ctx:
        sb = lambda name, shape, dt=F32: ctx.enter_context(nc.sbuf_tensor(name, shape, dt))
        sem = lambda name: ctx.enter_context(nc.semaphore(name))
        token, near, weight = M["token"], M["near"], M["weight"]
        index = sb("e_index", [P, 2, QUAD], I32)
        to = sb("e_to", [P, 2, QUAD], I32)
        x12 = sb("e_x12", [P, 2, QUAD, 2 * C])
        x2t = sb("e_x2t", [P, 2, QUAD, KC * P])
        ht = sb("e_ht", [P, 2, HC, QUAD * P])
        y = sb("e_y", [P, QUAD, C])
        res = sb("e_res", [P, 2, QUAD, C])
        t_ps = ctx.enter_context(nc.psum_tensor("e_t_ps", [P, QUAD, KC * P], F32))
        h_ps = [ctx.enter_context(nc.psum_tensor(f"e_h_ps{b}", [P, QUAD * P], F32)) for b in range(4)]
        y_ps = ctx.enter_context(nc.psum_tensor("e_y_ps", [P, QUAD, C], F32))
        gathered = [sem(f"e_gathered{w}") for w in range(2)]
        scattered = [sem(f"e_scattered{w}") for w in range(2)]
        names = "to_ready index_ready turned copied h_done gelu_done y_done biased res_done"
        S = {n: sem("e_" + n) for n in names.split()}
        TURNS = NTILE // QUAD
        with nc.Block() as fresh:
            @fresh.gpsimd
            def _(pool):
                for s in (*gathered, *scattered, *S.values()):
                    pool.sem_clear(s)
        block = ctx.enter_context(nc.Block())

        @block.gpsimd
        def _(pool):
            def gather(w, n):
                pool.wait_ge(S["index_ready"], n)
                pool.nop(nofuse=True)
                for b in range(QUAD):
                    nc.gpsimd.indirect_dma_start(out=x12[:, w, b, :], out_offset=None, in_=R["x12"],
                                                 in_offset=bass.IndirectOffsetOnAxis(ap=index[:, w, b:b + 1], axis=0)
                                                 ).then_inc(gathered[w], 16)

            def scatter(w, n, done):
                pool.wait_ge(S["to_ready"], n)
                pool.wait_ge(S["res_done"], done)
                pool.nop(nofuse=True)
                for b in range(QUAD):
                    nc.gpsimd.indirect_dma_start(out=out, out_offset=bass.IndirectOffsetOnAxis(ap=to[:, w, b:b + 1], axis=0),
                                                 in_=res[:, w, b, :], in_offset=None, bounds_check=N - 1, oob_is_err=False
                                                 ).then_inc(scattered[w], 16)

            gather(0, 1)
            gather(1, 2)
            with pool.Fori(0, TURNS // 2 - 1) as i:
                for w in range(2):
                    scatter(w, i * 2 + w + 1, (i * 2 + w + 1) * QUAD)
                    gather(w, i * 2 + w + 3)
            for w in range(2):
                scatter(w, TURNS - 1 + w, (TURNS - 1 + w) * QUAD)
            for w in range(2):
                pool.wait_ge(scattered[w], 16 * QUAD * (TURNS // 2))

        @block.scalar
        def _(act):
            for w in range(2):
                nc.scalar.copy(index[:, w, :], near[:, w, :]).then_inc(S["index_ready"], 1)

            with act.Fori(0, TURNS // 2) as i:
                for w in range(2):
                    n = i * 2 + w
                    act.wait_ge(S["turned"], n + 1)
                    act.nop(nofuse=True)
                    nc.scalar.copy(x2t[:, w], t_ps[:]).then_inc(S["copied"], 1)
                    for c in range(HC):
                        act.wait_ge(S["h_done"], n * HC + c + 1)
                        nc.scalar.activation(ht[:, w, c, :], h_ps[c % 4][:], ACT.Gelu, bias=M["b1"][:, c:c + 1]
                                             ).then_inc(S["gelu_done"], 1)
                    act.wait_ge(scattered[w], i * (16 * QUAD))
                    act.nop(nofuse=True)
                    nc.scalar.copy(to[:, w, :], token[:, bass.ds(n * QUAD, QUAD)]).then_inc(S["to_ready"], 1)
                    act.wait_ge(gathered[w], (i + 1) * (16 * QUAD))
                    act.nop(nofuse=True)
                    nc.scalar.copy(index[:, w, :], near[:, bass.ds(n + 2, 1), :].rearrange("p a b -> p (a b)")
                                   ).then_inc(S["index_ready"], 1)

        @block.vector
        def _(dve):
            at_expert = [dve.alloc_register(f"e_dve{b}") for b in range(QUAD)]
            with dve.Fori(0, TURNS // 2) as i:
                for w in range(2):
                    n = i * 2 + w
                    regs = load_row(dve, at_expert, M["expert"][0:1, bass.ds(n * QUAD, QUAD)], NEXP - 1)
                    dve.wait_ge(scattered[w], i * (16 * QUAD))
                    for b in range(QUAD):
                        t = n * QUAD + b
                        dve.wait_ge(S["y_done"], n * QUAD + b // 2 * 2 + 2)
                        dve.wait_ge(S["res_done"], n * QUAD)
                        dve.nop(nofuse=True)
                        nc.vector.tensor_tensor(y[:, b, :], y_ps[:, b, :],
                                                M["bd"][:, bass.ds(regs[b], 1), :].rearrange("p a n -> p (a n)"), ALU.add
                                                ).then_inc(S["biased"], 1)
                        dve.wait_ge(S["biased"], t + 1)
                        dve.wait_ge(gathered[w], (i + 1) * (16 * QUAD))
                        dve.nop(nofuse=True)
                        nc.vector.scalar_tensor_tensor(out=res[:, w, b, :], in0=y[:, b, :], scalar=weight[:, bass.ds(t, 1)],
                                                       in1=x12[:, w, b, 0:C], op0=ALU.mult, op1=ALU.add
                                                       ).then_inc(S["res_done"], 1)

        @block.tensor
        def _(pe):
            def turn(w, n, got):
                pe.wait_ge(gathered[w], got)
                pe.wait_ge(S["copied"], n)
                for b in range(QUAD):
                    for k in range(KC):
                        ins = nc.tensor.transpose(t_ps[:, b, k * P:(k + 1) * P], x12[:, w, b, C + k * P:C + (k + 1) * P],
                                                  M["ident"][:])
                ins.then_inc(S["turned"], 1)

            def hidden(w, n):
                pe.wait_ge(S["copied"], n + 1)
                for c in range(HC):
                    pe.wait_ge(S["gelu_done"], n * HC + max(c - 3, 0))
                    for k in range(KC):
                        ins = nc.tensor.matmul(h_ps[c % 4][:], M["w1"][:, k, c * P:(c + 1) * P],
                                               x2t[:, w, :, k * P:(k + 1) * P], start=(k == 0), stop=(k == KC - 1))
                    ins.then_inc(S["h_done"], 1)

            at_expert = [pe.alloc_register(f"e_pe{b}") for b in range(QUAD)]

            def down(w, n):
                regs = load_row(pe, at_expert, M["expert"][0:1, bass.ds(n * QUAD, QUAD)], NEXP - 1)
                pe.wait_ge(S["gelu_done"], (n + 1) * HC)
                pe.wait_ge(S["biased"], n * QUAD)
                pe.nop(nofuse=True)
                for b in range(QUAD):
                    for c in range(HC):
                        ins = nc.tensor.matmul(y_ps[:, b, :], ht[:, w, c, b * P:(b + 1) * P],
                                               M["wd"][:, bass.ds(regs[b], 1), c, :].rearrange("p a n -> p (a n)"),
                                               start=(c == 0), stop=(c == HC - 1))
                    ins.then_inc(S["y_done"], 1)

            turn(0, 0, 16 * QUAD)
            with pe.Fori(0, TURNS // 2 - 1) as i:
                for w in range(2):
                    n = i * 2 + w
                    hidden(w, n)
                    turn(1 - w, n + 1, (i + w + 1) * (16 * QUAD))
                    down(w, n)
            hidden(0, TURNS - 2)
            turn(1, TURNS - 1, (TURNS // 2) * (16 * QUAD))
            down(0, TURNS - 2)
            hidden(1, TURNS - 1)
            down(1, TURNS - 1)


def build(nc, A, out, dbg=None):
    dram = lambda name, shape, dt=F32: nc.dram_tensor(name, shape, dt).ap()
    R = {"xn": dram("xn_d", (NPAD, C)), "xnt": dram("xnt_d", (NBLK, P, KC * P)), "kv": dram("kv_d", (NPAD, 2 * C)),
         "blk": dram("blk_d", (T,), I32),
         "local": dram("local_d", (TS_ROWS + 2, TS_COLS * P), BF16), "type": dram("type_d", (TS_ROWS + 2, TS_COLS * P), BF16),
         "v": dram("v_d", (TS_ROWS, P, TS_COLS * C)), "x12": dram("x12_d", (NPAD, 2 * C)),
         "x2t": dram("x2t_d", (NQ, P, QUAD * KC * P))}
    with ExitStack() as ctx:
        sb = lambda name, shape, dt=F32: ctx.enter_context(nc.sbuf_tensor(name, shape, dt))
        M = {"ones": sb("ones", [P, P]), "eps": sb("eps", [P, 1]), "ident": sb("ident", [P, P]), "lane": sb("lane", [P, 1]),
             "lane64": sb("lane64", [P, 1]), "col": sb("col", [P, P]),
             "bound": sb("bound", [P, NBLK]), "count": sb("count", [EROWS, NBLK]),
             "rel3": sb("rel3", [P, 3, C], BF16),
             "dots": sb("dots", [P, MH // 2, P]),
             "blk": sb("blk", [1, T], I32)}
        M["softmax_steps"] = 41
        with ExitStack() as edge_part:
            sbe = lambda name, shape, dt=F32: edge_part.enter_context(nc.sbuf_tensor(name, shape, dt))
            M["src"] = sbe("src", [P, TS_ROWS + 2, TS_COLS])
            M["local"] = sbe("local", [P, TS_ROWS, TS_COLS])
            M["segment"] = sbe("segment", [TS_ROWS, TS_COLS * P])
            M["scores"] = sbe("scores", [P, TS_ROWS, TS_COLS * H])
            with ExitStack() as queries:
                M["q3"] = queries.enter_context(nc.sbuf_tensor("q3", [P, NBLK, 3, C], BF16))
                with ExitStack() as project:
                    sbp = lambda name, shape, dt=F32: project.enter_context(nc.sbuf_tensor(name, shape, dt))
                    M["wcat"] = sbp("wcat", [P, KC, WCAT])
                    M["bias"] = sbp("bias", [P, 3 * C])
                    stage_weights(nc, A, M, R)
                    stage_project(nc, A, M, R)
                stage_tiles(nc, A, M, R)
                stage_scores(nc, A, M, R)
            M["z"] = sbe("z", [P, KC, C])
            stage_softmax(nc, A, M, R)
            M["sums"] = sbe("sums", [P, NBLK, AGG])
            stage_aggregate(nc, A, M, R)
            stage_nodes(nc, A, M, R)
            if dbg is not None:
                dbg(nc, M, R)
        with ExitStack() as ffn:
            sbf = lambda name, shape, dt=F32: ffn.enter_context(nc.sbuf_tensor(name, shape, dt))
            M["w1"] = sbf("w1", [P, KC, HID])
            M["b1"] = sbf("b1", [P, HC])
            M["wd"] = sbf("wd", [P, NEXP, HC, C])
            M["bd"] = sbf("bd", [P, NEXP, C])
            M["logits"] = sbf("logits", [P, NBLK, NEXP])
            M["expert"] = sbf("expert", [1, NTILE], I32)
            M["token"] = sbf("token", [P, NTILE], I32)
            M["near"] = sbf("near", [P, NTILE // QUAD + 2, QUAD], I32)
            M["weight"] = sbf("weight", [P, NTILE])
            stage_hidden(nc, A, M, R)
            stage_route(nc, A, M, R)
            stage_experts(nc, A, M, R, out)


_OUT = (N, C)


def kernel(**inputs):
    import concourse.bacc as _bacc
    from concourse.bass_utils import run_bass_kernel_spmd as _run

    arrays = {name: np.ascontiguousarray(a) for name, a in inputs.items()}
    x = np.zeros((XBLK * P, C), arrays["x"].dtype)
    x[:N] = arrays["x"]
    wqkv = arrays.pop("L0_mix_Wqkv")
    src, kind = arrays.pop("src"), arrays.pop("edge_type_64")
    arrays["x"] = x
    arrays["edges"] = np.full((E + P, 3), -1, src.dtype)
    for j, field in enumerate((src, arrays["dst"], kind)):
        arrays["edges"][:E, j] = field
    arrays["mix_Wq"] = np.ascontiguousarray(wqkv[:MI])
    arrays["mix_WkvT"] = np.ascontiguousarray(wqkv[MI:].T)
    arrays["mix_WoutT"] = np.ascontiguousarray(arrays.pop("L0_mix_Wout").T)
    nc = _bacc.Bacc("TRN2", target_bir_lowering=False, num_devices=1)
    ins = {name: nc.dram_tensor(f"in_{name}", a.shape, mybir.dt.from_np(a.dtype), kind="ExternalInput").ap()
           for name, a in arrays.items()}
    out = nc.dram_tensor("out", _OUT, F32, kind="ExternalOutput").ap()
    build(nc, ins, out)
    r = _run(nc, [{f"in_{name}": a for name, a in arrays.items()}], core_ids=[0])
    return r.results[0]["out"]
```
